# Optimizing a Trainium2 kernel written in Bass

```python
import numpy as np
import jax
import jax.numpy as jnp

def _softmax(x, axis=-1):
    return jax.nn.softmax(x, axis=axis)

def _gelu(x):
    return jax.nn.gelu(x, approximate=True)

def _silu(x):
    return jax.nn.silu(x)

def _sigmoid(x):
    return jax.nn.sigmoid(x)

def _layernorm(x, axis=-1, eps=1e-05):
    m = jnp.mean(x, axis=axis, keepdims=True)
    v = jnp.var(x, axis=axis, keepdims=True)
    return (x - m) / jnp.sqrt(v + eps)

def _scatter_add(tgt, idx, src, axis=0):
    return tgt.at[idx].add(src)

def _segment_sum(src, seg, n):
    return jax.ops.segment_sum(src, seg, n)
kernel_name = 'mk_early_fusion_d2_tok_img256_r4_885d6a'

def setup_inputs(seed: int=0):
    np.random.seed(seed)
    _w = jnp.asarray

    def _rec_inputs():
        import jax
        import jax.numpy as jnp
        _rk = jax.random.key(seed)
        x = -0.00016672 + 0.999947 * jax.random.normal(jax.random.fold_in(_rk, 1), (32, 3, 224, 224), jnp.float32)
        txt = 0.000202745 + 0.998873 * jax.random.normal(jax.random.fold_in(_rk, 2), (32, 77, 64), jnp.float32)
        return (x, txt)
    x, txt = _rec_inputs()

    def _L0_tok_setup():
        import jax, jax.numpy as jnp
        import numpy as np
        PATCH = 16
        key = jax.random.key(seed)
        k1, k2, k3 = jax.random.split(key, 3)
        B, C, H, Wd = (64, 3, 96, 96)
        E = 64
        pdim = PATCH * PATCH * C
        x = jax.random.normal(k1, (B, C, H, Wd), dtype=jnp.float32)
        W = jax.random.normal(k2, (E, pdim), dtype=jnp.float32) * pdim ** (-0.5)
        b = jax.random.normal(k3, (E,), dtype=jnp.float32) * 0.01
        return {'x': x, 'W': W, 'b': b}
    _L0_tok_all = _L0_tok_setup()
    _L0_tok_in = {k: v for k, v in _L0_tok_all.items() if k in ('W', 'b')}
    del _L0_tok_all

    def _L0_attn_setup():
        import jax, jax.numpy as jnp
        import numpy as np
        B_SZ, L_SEQ, H_CH, N_ST = (8, 1024, 64, 64)

        def _dplr_kernel(Lambda_re, Lambda_im, P_re, P_im, Q_re, Q_im, B_re, B_im, C_re, C_im, step, L):
            Lam = (Lambda_re + 1j * Lambda_im).astype(jnp.complex64)
            Pc = (P_re + 1j * P_im).astype(jnp.complex64)
            Qc = (Q_re + 1j * Q_im).astype(jnp.complex64)
            Bc = (B_re + 1j * B_im).astype(jnp.complex64)
            Cc = (C_re + 1j * C_im).astype(jnp.complex64)
            k = jnp.arange(L, dtype=jnp.float32)
            Omega = jnp.exp(-2j * jnp.pi * (k / L)).astype(jnp.complex64)
            c = 2.0 / (1.0 + Omega)
            g = 2.0 / step[0] * (1.0 - Omega) / (1.0 + Omega)
            inv = 1.0 / (g[:, None] - Lam[None, :])
            k00 = jnp.einsum('hn,ln->hl', Cc * Bc[None, :], inv)
            k01 = jnp.einsum('hn,ln->hl', Cc * Pc[None, :], inv)
            k10 = jnp.einsum('n,ln->l', Qc * Bc, inv)
            k11 = jnp.einsum('n,ln->l', Qc * Pc, inv)
            atRoots = c[None, :] * (k00 - k01 * (k10 / (1.0 + k11))[None, :])
            K = jnp.fft.ifft(atRoots, axis=-1).real
            return K.astype(jnp.float32)

        def _reference_tuple_inner(x, Lambda_re, Lambda_im, P_re, P_im, Q_re, Q_im, B_re, B_im, C_re, C_im, step, D, W_fc, b_fc, ln_g, ln_b):
            Bsz, L, H = x.shape
            step = jnp.maximum(step, 1e-06)
            K = _dplr_kernel(Lambda_re, Lambda_im, P_re, P_im, Q_re, Q_im, B_re, B_im, C_re, C_im, step, L)
            n = 2 * L
            Kf = jnp.fft.rfft(K, n=n, axis=-1)
            uf = jnp.fft.rfft(x, n=n, axis=1)
            h1 = jnp.fft.irfft(uf * Kf.T[None], n=n, axis=1)[:, :L, :]
            y1 = jax.nn.gelu(h1 + D * x, approximate=False)
            y2 = jax.nn.gelu(y1 @ W_fc.T + b_fc, approximate=False)
            y2 = y2 + x
            mu = jnp.mean(y2, axis=-1, keepdims=True)
            var = jnp.var(y2, axis=-1, keepdims=True)
            y = (y2 - mu) / jnp.sqrt(var + 1e-05) * ln_g + ln_b
            h_ratio = jnp.max(jnp.abs(y), axis=1) / (jnp.max(jnp.abs(x), axis=1) + 1e-06)
            return (y, h_ratio)
        key = jax.random.key(seed)
        ks = jax.random.split(key, 12)
        rn = lambda k, s, sc=1.0: jax.random.normal(k, s, jnp.float32) * sc
        inp = {'x': rn(ks[0], (B_SZ, L_SEQ, H_CH)), 'Lambda_re': -(jnp.abs(rn(ks[1], (N_ST,))) + 0.1), 'Lambda_im': jnp.pi * jnp.arange(N_ST, dtype=jnp.float32), 'P_re': rn(ks[2], (N_ST,), N_ST ** (-0.5)), 'P_im': rn(ks[3], (N_ST,), N_ST ** (-0.5)), 'Q_re': rn(ks[4], (N_ST,), N_ST ** (-0.5)), 'Q_im': rn(ks[5], (N_ST,), N_ST ** (-0.5)), 'B_re': rn(ks[6], (N_ST,), N_ST ** (-0.5)), 'B_im': rn(ks[7], (N_ST,), N_ST ** (-0.5)), 'C_re': rn(ks[8], (H_CH, N_ST), N_ST ** (-0.5)), 'C_im': rn(ks[9], (H_CH, N_ST), N_ST ** (-0.5)), 'step': jnp.ones((1,), jnp.float32) * 0.001, 'D': jnp.zeros((1,), jnp.float32), 'W_fc': rn(ks[10], (H_CH, H_CH), H_CH ** (-0.5)), 'b_fc': jnp.zeros((H_CH,), jnp.float32), 'ln_g': jnp.ones((H_CH,), jnp.float32), 'ln_b': jnp.zeros((H_CH,), jnp.float32)}
        return inp
    _L0_attn_all = _L0_attn_setup()
    _L0_attn_in = {k: v for k, v in _L0_attn_all.items() if k in ('Lambda_re', 'Lambda_im', 'P_re', 'P_im', 'Q_re', 'Q_im', 'B_re', 'B_im', 'C_re', 'C_im', 'step', 'D', 'W_fc', 'b_fc', 'ln_g', 'ln_b')}
    del _L0_attn_all

    def _L0_ffn_setup():
        import jax, jax.numpy as jnp
        import numpy as np
        N_EXPERTS = 8
        TOP_K = 2
        key = jax.random.key(seed)
        ks = jax.random.split(key, 5)
        B, T, C, E, H = (8, 512, 64, 8, 682)
        scale = 1.0 / np.sqrt(C)
        return {'x': jax.random.normal(ks[0], (B, T, C), dtype=jnp.float32), 'router_w': jax.random.normal(ks[1], (E, C), dtype=jnp.float32) * scale, 'w1': jax.random.normal(ks[2], (E, H, C), dtype=jnp.float32) * scale, 'w2': jax.random.normal(ks[3], (E, C, H), dtype=jnp.float32) * (1.0 / np.sqrt(H)), 'w3': jax.random.normal(ks[4], (E, H, C), dtype=jnp.float32) * scale}
    _L0_ffn_all = _L0_ffn_setup()
    _L0_ffn_in = {k: v for k, v in _L0_ffn_all.items() if k in ('router_w', 'w1', 'w2', 'w3')}
    del _L0_ffn_all

    def _L1_attn_setup():
        import jax, jax.numpy as jnp
        import numpy as np
        B, PLEN, D = (32, 256, 64)
        key = jax.random.key(seed)
        ks = jax.random.split(key, 8)
        u = lambda k, shape: jax.random.uniform(k, shape, jnp.float32, -0.05, 0.05)
        return {'P': jax.random.normal(ks[0], (B, PLEN, D), jnp.float32), 'w_itr_att': u(ks[1], (3 * D,)), 'w1': u(ks[2], (2 * D, D)), 'w2': u(ks[3], (2 * D, D)), 'w3': u(ks[4], (2 * D, D)), 'b1': u(ks[5], (D,)), 'b2': u(ks[6], (D,)), 'b3': u(ks[7], (D,))}
    _L1_attn_all = _L1_attn_setup()
    _L1_attn_in = {k: v for k, v in _L1_attn_all.items() if k in ('w_itr_att', 'w1', 'w2', 'w3', 'b1', 'b2', 'b3')}
    del _L1_attn_all

    def _L1_ffn_setup():
        import jax, jax.numpy as jnp
        import numpy as np
        DIM = 64
        HEADS = 8
        NUM_KEYS = 64
        NUM_KV = NUM_KEYS ** 2
        PK_TOPK = 16
        FINAL_TOPK = 16
        DIM_KEY = DIM // 2
        P = 2

        def _pk(x, Wq_pk, pk_keys):
            b, n, _ = x.shape
            q = (x @ Wq_pk).reshape(b, n, P, HEADS, DIM_KEY).transpose(2, 0, 1, 3, 4)
            sim = jnp.einsum('pbnhd,pkhd->pbnhk', q, pk_keys)
            scores, idx = jax.lax.top_k(sim, PK_TOPK)
            idx0 = idx[0]
            idx1 = idx[1] * NUM_KEYS
            index = (idx0[..., :, None] + idx1[..., None, :]).reshape(b, n, HEADS, PK_TOPK * PK_TOPK)
            score = (scores[0][..., :, None] + scores[1][..., None, :]).reshape(b, n, HEADS, PK_TOPK * PK_TOPK)
            final_scores, pk_idx = jax.lax.top_k(score, FINAL_TOPK)
            final_indices = jnp.take_along_axis(index, pk_idx, axis=-1)
            final_scores = jax.nn.softmax(final_scores, axis=-1)
            return (final_scores, final_indices)
        key = jax.random.key(seed)
        ks = jax.random.split(key, 7)
        b, n = (2, 256)
        std = 0.02
        x = jax.random.normal(ks[0], (b, n, DIM), dtype=jnp.float32)
        Wq_pk = jax.random.normal(ks[1], (DIM, P * HEADS * DIM_KEY), dtype=jnp.float32) * std
        pk_keys = jax.random.normal(ks[2], (P, NUM_KEYS, HEADS, DIM_KEY), dtype=jnp.float32) * std
        Wq = jax.random.normal(ks[3], (DIM, HEADS * DIM), dtype=jnp.float32) * std
        keys_table = jax.random.normal(ks[4], (NUM_KV * HEADS, DIM), dtype=jnp.float32) * std
        values_table = jax.random.normal(ks[5], (NUM_KV * HEADS, DIM), dtype=jnp.float32) * std
        Wo = jax.random.normal(ks[6], (DIM * HEADS, DIM), dtype=jnp.float32) * std
        return {'x': x, 'Wq_pk': Wq_pk, 'pk_keys': pk_keys, 'Wq': Wq, 'keys_table': keys_table, 'values_table': values_table, 'Wo': Wo}
    _L1_ffn_all = _L1_ffn_setup()
    _L1_ffn_in = {k: v for k, v in _L1_ffn_all.items() if k in ('Wq_pk', 'pk_keys', 'Wq', 'keys_table', 'values_table', 'Wo')}
    del _L1_ffn_all
    return {'x': x, 'txt': txt, 'L0_tok_W': _L0_tok_in['W'], 'L0_tok_b': _L0_tok_in['b'], 'L0_attn_Lambda_re': _L0_attn_in['Lambda_re'], 'L0_attn_Lambda_im': _L0_attn_in['Lambda_im'], 'L0_attn_P_re': _L0_attn_in['P_re'], 'L0_attn_P_im': _L0_attn_in['P_im'], 'L0_attn_Q_re': _L0_attn_in['Q_re'], 'L0_attn_Q_im': _L0_attn_in['Q_im'], 'L0_attn_B_re': _L0_attn_in['B_re'], 'L0_attn_B_im': _L0_attn_in['B_im'], 'L0_attn_C_re': _L0_attn_in['C_re'], 'L0_attn_C_im': _L0_attn_in['C_im'], 'L0_attn_step': _L0_attn_in['step'], 'L0_attn_D': _L0_attn_in['D'], 'L0_attn_W_fc': _L0_attn_in['W_fc'], 'L0_attn_b_fc': _L0_attn_in['b_fc'], 'L0_attn_ln_g': _L0_attn_in['ln_g'], 'L0_attn_ln_b': _L0_attn_in['ln_b'], 'L0_ffn_router_w': _L0_ffn_in['router_w'], 'L0_ffn_w1': _L0_ffn_in['w1'], 'L0_ffn_w2': _L0_ffn_in['w2'], 'L0_ffn_w3': _L0_ffn_in['w3'], 'L1_attn_w_itr_att': _L1_attn_in['w_itr_att'], 'L1_attn_w1': _L1_attn_in['w1'], 'L1_attn_w2': _L1_attn_in['w2'], 'L1_attn_w3': _L1_attn_in['w3'], 'L1_attn_b1': _L1_attn_in['b1'], 'L1_attn_b2': _L1_attn_in['b2'], 'L1_attn_b3': _L1_attn_in['b3'], 'L1_ffn_Wq_pk': _L1_ffn_in['Wq_pk'], 'L1_ffn_pk_keys': _L1_ffn_in['pk_keys'], 'L1_ffn_Wq': _L1_ffn_in['Wq'], 'L1_ffn_keys_table': _L1_ffn_in['keys_table'], 'L1_ffn_values_table': _L1_ffn_in['values_table'], 'L1_ffn_Wo': _L1_ffn_in['Wo']}

def reference(x, txt, L0_tok_W, L0_tok_b, L0_attn_Lambda_re, L0_attn_Lambda_im, L0_attn_P_re, L0_attn_P_im, L0_attn_Q_re, L0_attn_Q_im, L0_attn_B_re, L0_attn_B_im, L0_attn_C_re, L0_attn_C_im, L0_attn_step, L0_attn_D, L0_attn_W_fc, L0_attn_b_fc, L0_attn_ln_g, L0_attn_ln_b, L0_ffn_router_w, L0_ffn_w1, L0_ffn_w2, L0_ffn_w3, L1_attn_w_itr_att, L1_attn_w1, L1_attn_w2, L1_attn_w3, L1_attn_b1, L1_attn_b2, L1_attn_b3, L1_ffn_Wq_pk, L1_ffn_pk_keys, L1_ffn_Wq, L1_ffn_keys_table, L1_ffn_values_table, L1_ffn_Wo):
    import jax
    import jax.numpy as jnp

    def _L0_tok_ref(x, W, b):
        import jax, jax.numpy as jnp
        import numpy as np
        PATCH = 16
        B, C, H, Wd = x.shape
        p = PATCH
        nH, nW = (H // p, Wd // p)
        patches = x.reshape(B, C, nH, p, nW, p)
        patches = patches.transpose(0, 2, 4, 1, 3, 5)
        patches = patches.reshape(B, nH * nW, C * p * p)
        return jnp.einsum('bnk,ek->bne', patches, W) + b

    def _L0_attn_ref(x, Lambda_re, Lambda_im, P_re, P_im, Q_re, Q_im, B_re, B_im, C_re, C_im, step, D, W_fc, b_fc, ln_g, ln_b):
        import jax, jax.numpy as jnp
        import numpy as np
        B_SZ, L_SEQ, H_CH, N_ST = (8, 1024, 64, 64)

        def _dplr_kernel(Lambda_re, Lambda_im, P_re, P_im, Q_re, Q_im, B_re, B_im, C_re, C_im, step, L):
            Lam = (Lambda_re + 1j * Lambda_im).astype(jnp.complex64)
            Pc = (P_re + 1j * P_im).astype(jnp.complex64)
            Qc = (Q_re + 1j * Q_im).astype(jnp.complex64)
            Bc = (B_re + 1j * B_im).astype(jnp.complex64)
            Cc = (C_re + 1j * C_im).astype(jnp.complex64)
            k = jnp.arange(L, dtype=jnp.float32)
            Omega = jnp.exp(-2j * jnp.pi * (k / L)).astype(jnp.complex64)
            c = 2.0 / (1.0 + Omega)
            g = 2.0 / step[0] * (1.0 - Omega) / (1.0 + Omega)
            inv = 1.0 / (g[:, None] - Lam[None, :])
            k00 = jnp.einsum('hn,ln->hl', Cc * Bc[None, :], inv)
            k01 = jnp.einsum('hn,ln->hl', Cc * Pc[None, :], inv)
            k10 = jnp.einsum('n,ln->l', Qc * Bc, inv)
            k11 = jnp.einsum('n,ln->l', Qc * Pc, inv)
            atRoots = c[None, :] * (k00 - k01 * (k10 / (1.0 + k11))[None, :])
            K = jnp.fft.ifft(atRoots, axis=-1).real
            return K.astype(jnp.float32)

        def _reference_tuple_inner(x, Lambda_re, Lambda_im, P_re, P_im, Q_re, Q_im, B_re, B_im, C_re, C_im, step, D, W_fc, b_fc, ln_g, ln_b):
            Bsz, L, H = x.shape
            step = jnp.maximum(step, 1e-06)
            K = _dplr_kernel(Lambda_re, Lambda_im, P_re, P_im, Q_re, Q_im, B_re, B_im, C_re, C_im, step, L)
            n = 2 * L
            Kf = jnp.fft.rfft(K, n=n, axis=-1)
            uf = jnp.fft.rfft(x, n=n, axis=1)
            h1 = jnp.fft.irfft(uf * Kf.T[None], n=n, axis=1)[:, :L, :]
            y1 = jax.nn.gelu(h1 + D * x, approximate=False)
            y2 = jax.nn.gelu(y1 @ W_fc.T + b_fc, approximate=False)
            y2 = y2 + x
            mu = jnp.mean(y2, axis=-1, keepdims=True)
            var = jnp.var(y2, axis=-1, keepdims=True)
            y = (y2 - mu) / jnp.sqrt(var + 1e-05) * ln_g + ln_b
            h_ratio = jnp.max(jnp.abs(y), axis=1) / (jnp.max(jnp.abs(x), axis=1) + 1e-06)
            return (y, h_ratio)
        return _reference_tuple_inner(x, Lambda_re, Lambda_im, P_re, P_im, Q_re, Q_im, B_re, B_im, C_re, C_im, step, D, W_fc, b_fc, ln_g, ln_b)[0]

    def _L0_ffn_ref(x, router_w, w1, w2, w3):
        import jax, jax.numpy as jnp
        import numpy as np
        N_EXPERTS = 8
        TOP_K = 2
        B, T, C = x.shape
        flat = x.reshape(-1, C)
        logits = flat @ router_w.T
        probs = jax.nn.softmax(logits, axis=-1)
        topk_probs, topk_idx = jax.lax.top_k(probs, TOP_K)
        topk_probs = topk_probs / (jnp.sum(topk_probs, axis=-1, keepdims=True) + 1e-09)
        onehot = jax.nn.one_hot(topk_idx, N_EXPERTS, dtype=flat.dtype)
        gates = jnp.einsum('nk,nke->ne', topk_probs, onehot)
        h1 = jnp.einsum('nc,ehc->neh', flat, w1)
        h3 = jnp.einsum('nc,ehc->neh', flat, w3)
        h = jax.nn.silu(h1) * h3
        y = jnp.einsum('neh,ech->nec', h, w2)
        out = jnp.einsum('ne,nec->nc', gates, y)
        return out.reshape(B, T, C)

    def _L1_attn_ref(P, w_itr_att, w1, w2, w3, b1, b2, b3):
        import jax, jax.numpy as jnp
        import numpy as np
        B, PLEN, D = (32, 256, 64)
        d = P.shape[-1]
        wa, wb, wc = (w_itr_att[:d], w_itr_att[d:2 * d], w_itr_att[2 * d:])
        sa = P @ wa
        sb = P @ wb
        A = sa[:, :, None] + sb[:, None, :] + jnp.einsum('bid,bjd->bij', P * wc, P)
        itr_attn = jnp.einsum('bij,bjd->bid', jax.nn.softmax(A, axis=2), P)
        cat = jnp.concatenate([P, itr_attn], axis=-1)
        z = jnp.tanh(cat @ w1 + b1)
        r = jax.nn.sigmoid(cat @ w2 + b2)
        f = jax.nn.sigmoid(cat @ w3 + b3)
        return r * P + f * z

    def _L1_ffn_ref(x, Wq_pk, pk_keys, Wq, keys_table, values_table, Wo):
        import jax, jax.numpy as jnp
        import numpy as np
        DIM = 64
        HEADS = 8
        NUM_KEYS = 64
        NUM_KV = NUM_KEYS ** 2
        PK_TOPK = 16
        FINAL_TOPK = 16
        DIM_KEY = DIM // 2
        P = 2

        def _pk(x, Wq_pk, pk_keys):
            b, n, _ = x.shape
            q = (x @ Wq_pk).reshape(b, n, P, HEADS, DIM_KEY).transpose(2, 0, 1, 3, 4)
            sim = jnp.einsum('pbnhd,pkhd->pbnhk', q, pk_keys)
            scores, idx = jax.lax.top_k(sim, PK_TOPK)
            idx0 = idx[0]
            idx1 = idx[1] * NUM_KEYS
            index = (idx0[..., :, None] + idx1[..., None, :]).reshape(b, n, HEADS, PK_TOPK * PK_TOPK)
            score = (scores[0][..., :, None] + scores[1][..., None, :]).reshape(b, n, HEADS, PK_TOPK * PK_TOPK)
            final_scores, pk_idx = jax.lax.top_k(score, FINAL_TOPK)
            final_indices = jnp.take_along_axis(index, pk_idx, axis=-1)
            final_scores = jax.nn.softmax(final_scores, axis=-1)
            return (final_scores, final_indices)
        b, n, d = x.shape
        q = (x @ Wq).reshape(b, n, HEADS, DIM) * DIM ** (-0.5)
        kv_scores, indices = _pk(x, Wq_pk, pk_keys)
        offsets = jnp.arange(HEADS, dtype=indices.dtype) * NUM_KV
        ind = indices + offsets[None, None, :, None]
        k = jnp.einsum('bnhk,bnhkd->bnhd', kv_scores, keys_table[ind])
        v = jnp.einsum('bnhk,bnhkd->bnhd', kv_scores, values_table[ind])
        sim = jnp.einsum('bihd,bjhd->bhij', q, k)
        neg = -jnp.finfo(sim.dtype).max
        causal = jnp.tril(jnp.ones((n, n), dtype=bool))
        sim = jnp.where(causal, sim, neg)
        attn = jax.nn.softmax(sim, axis=-1)
        out = jnp.einsum('bhij,bjhd->bhid', attn, v)
        out = out.transpose(0, 2, 1, 3).reshape(b, n, HEADS * DIM)
        return out @ Wo
    h = _L0_tok_ref(x, L0_tok_W, L0_tok_b)
    h = jnp.concatenate([h, txt], axis=1)
    h = h + _L0_attn_ref(_layernorm(h, axis=-1), L0_attn_Lambda_re, L0_attn_Lambda_im, L0_attn_P_re, L0_attn_P_im, L0_attn_Q_re, L0_attn_Q_im, L0_attn_B_re, L0_attn_B_im, L0_attn_C_re, L0_attn_C_im, L0_attn_step, L0_attn_D, L0_attn_W_fc, L0_attn_b_fc, L0_attn_ln_g, L0_attn_ln_b)
    h = h + _L0_ffn_ref(_layernorm(h, axis=-1), L0_ffn_router_w, L0_ffn_w1, L0_ffn_w2, L0_ffn_w3)
    h = h + _L1_attn_ref(_layernorm(h, axis=-1), L1_attn_w_itr_att, L1_attn_w1, L1_attn_w2, L1_attn_w3, L1_attn_b1, L1_attn_b2, L1_attn_b3)
    h = h + _L1_ffn_ref(_layernorm(h, axis=-1), L1_ffn_Wq_pk, L1_ffn_pk_keys, L1_ffn_Wq, L1_ffn_keys_table, L1_ffn_values_table, L1_ffn_Wo)
    return h

_drawn_inputs = setup_inputs


def setup_inputs(seed=0):
    import zlib

    import numpy as np

    out = dict(_drawn_inputs(seed))
    spreads = {'L0_attn_b_fc': (0.0, 0.1), 'L0_attn_ln_g': (1.0, 0.2), 'L0_attn_ln_b': (0.0, 0.1)}
    factors = {'L0_tok_b': 3.567,
     'L0_attn_Lambda_re': 8.0,
     'L0_attn_Lambda_im': 8.0,
     'L0_attn_P_re': 8.0,
     'L0_attn_P_im': 8.0,
     'L0_attn_Q_re': 8.0,
     'L0_attn_Q_im': 8.0,
     'L0_attn_B_re': 8.0,
     'L0_attn_B_im': 8.0,
     'L0_attn_C_re': 8.0,
     'L0_attn_C_im': 8.0,
     'L0_attn_W_fc': 8.0,
     'L1_attn_w_itr_att': 8.0,
     'L1_attn_w3': 8.0,
     'L1_attn_b1': 8.0,
     'L1_attn_b2': 8.0,
     'L1_attn_b3': 64.0,
     'L1_ffn_Wq_pk': 49.27,
     'L1_ffn_pk_keys': 45.471,
     'L1_ffn_Wq': 64.0,
     'L1_ffn_keys_table': 64.0,
     'L1_ffn_values_table': 44.484,
     'L1_ffn_Wo': 43.792}
    for name, (base, spread) in spreads.items():
        noise = np.random.default_rng([zlib.crc32(name.encode()), seed]).standard_normal(out[name].shape)
        drawn = base * np.exp(spread * noise) if base else spread * noise
        out[name] = jnp.asarray(drawn.astype(out[name].dtype))
    for name, factor in factors.items():
        out[name] = (out[name] * factor).astype(out[name].dtype)
    return out
```

```python
from contextlib import ExitStack

import concourse.bass as bass
from concourse import mybir
from concourse.alu_op_type import AluOpType as ALU

F32 = mybir.dt.float32
F32R = mybir.dt.float32r
ACT = mybir.ActivationFunctionType
AX = mybir.AxisListType

NB = 32
C = 64
NIMG = 196
TOK = 273
NTXT = TOK - NIMG
CP = 91
CH = 3
KT = 6
LN_EPS = 1e-5
STAGE = 8


class Mem:
    program = None

    def __init__(self, nc, stage):
        self.nc, self.stage, self.ctx, self.sems = nc, stage, ExitStack(), []

    def __enter__(self):
        return self

    def __exit__(self, *a):
        done = self.ctx.__exit__(*a)
        self.nc.clear_and_free_semaphores(self.sems)
        self.nc.all_engine_barrier()
        return done

    def sb(self, name, shape, dt=F32):
        return self.ctx.enter_context(self.nc.sbuf_tensor(f"{self.stage}_{name}", shape, dt))

    def ps(self, name, shape, dt=F32):
        return self.ctx.enter_context(self.nc.psum_tensor(f"{self.stage}_{name}", shape, dt))

    def sem(self, name):
        self.sems.append(self.nc.alloc_semaphore(name=f"{self.stage}_{name}"))
        return self.sems[-1]

    def pool_dma_sem(self, name):
        return self.program.enter_context(self.nc.semaphore(f"{self.stage}_{name}"))

    def block(self):
        return self.ctx.enter_context(self.nc.Block())


class Chain:

    def __init__(self, eng, sem, i=0, per=0):
        self.eng, self.sem, self.i, self.per, self.n = eng, sem, i, per, 0

    def step(self, ins):
        self.n += 1
        ins.then_inc(self.sem, 1)

    def sync(self):
        self.eng.wait_ge(self.sem, self.i * self.per + self.n)

    def link(self, ins):
        self.step(ins)
        self.sync()

    def close(self):
        assert self.n == self.per, (self.n, self.per)


class Norm:
    STEPS = 11

    def __init__(self, nc, m, held, name="norm"):
        self.nc, self.held = nc, held
        self.stats = m.sb(f"{name}_stats", [CP, 2, CH, 6])
        self.mv = m.sb(f"{name}_mv", [CP, 2, CH, 2])
        self.var_ready = m.sem(f"{name}_var_ready")
        self.root_ready = m.sem(f"{name}_root_ready")

    def vector(self, ch, x, out, j, s):
        nc, stats, mv = self.nc, self.stats[:, j], self.mv[:, j]
        for c in range(CH):
            ch.step(nc.vector.bn_stats(stats[:, c, :], x[:, c, :]))
        ch.sync()
        ch.eng.sem_inc(self.held, 1)
        for c in range(CH):
            ch.step(nc.vector.bn_aggr(mv[:, c, :], stats[:, c, :]))
        ch.sync()
        ch.link(nc.vector.tensor_scalar(mv[:, :, 1], mv[:, :, 1], LN_EPS, None, ALU.add))
        ch.eng.sem_inc(self.var_ready, 1)
        ch.eng.wait_ge(self.root_ready, s + 1)
        ch.link(nc.vector.reciprocal(mv[:, :, 1], mv[:, :, 1]))
        for c in range(CH):
            ch.step(nc.vector.tensor_scalar(out[:, c, :], x[:, c, :], mv[:, c, 0:1], mv[:, c, 1:2],
                                            ALU.subtract, ALU.mult))
        ch.sync()

    def scalar(self, act, j, s):
        act.wait_ge(self.var_ready, s + 1)
        sd = self.mv[:, j, :, 1]
        self.nc.scalar.activation(sd, sd, ACT.Sqrt).then_inc(self.root_ready, 1)


def stage_tokens(nc, d):
    with Mem(nc, "tok") as m:
        xp = m.sb("patches", [128, 2, KT, NIMG])
        hT = m.sb("hT", [C, 2, TOK])
        w = m.sb("w", [128, KT, C])
        b = m.sb("b", [C, 1])
        ident = m.sb("ident", [128, 128])
        h = m.sb("h", [CP, 2, CH, C])
        xn = m.sb("xn", [CP, 2, CH, C])
        xT = m.sb("xT", [C, 2, TOK])
        ps_h = [m.ps(f"ps_h{j}", [C, 512]) for j in range(2)]
        ps_t = [m.ps(f"ps_t{j}", [CP, CH, C]) for j in range(2)]
        ps_x = [m.ps(f"ps_x{j}", [C, 512]) for j in range(2)]
        held = m.sem("held")
        weights_in = m.sem("weights_in")
        pixels_in = [m.sem(f"pixels_in{j}") for j in range(2)]
        text_in = [m.sem(f"text_in{j}") for j in range(2)]
        embedded = m.sem("embedded")
        hT_ready = m.sem("hT_ready")
        h_turned = m.sem("h_turned")
        h_ready = m.sem("h_ready")
        normed = m.sem("normed")
        x_turned = m.sem("x_turned")
        xT_ready = m.sem("xT_ready")
        stored = [m.pool_dma_sem(f"stored{j}") for j in range(2)]
        out_free = m.sem("out_free")
        dve = m.sem("dve")
        norm = Norm(nc, m, held)
        block = m.block()

        @block.sync
        def _(sp):
            sp.dma_start(w[:], d["tokW"]).then_inc(weights_in, 16)
            sp.dma_start(b[:], d["tokb"]).then_inc(weights_in, 16)
            sp.dma_start(ident[:], d["ident"]).then_inc(weights_in, 16)
            with sp.Fori(0, NB // 2) as i:
                for j in range(2):
                    s = i * 2 + j
                    sp.wait_ge(h_turned, s + 1)
                    sp.dma_start(xp[:, j], d["patches"][s]).then_inc(pixels_in[j], 16)
                    sp.dma_start(hT[:, j, NIMG:TOK], d["txtT"][s]).then_inc(text_in[j], 16)

        @block.tensor
        def _(pe):
            pe.sem_inc(h_turned, 2)
            pe.sem_inc(x_turned, 2)
            pe.wait_ge(weights_in, 48)
            with pe.Fori(0, NB // 2) as i:
                for j in range(2):
                    pe.wait_ge(pixels_in[j], i * 16 + 16)
                    pe.wait_ge(hT_ready, i * 2 + j + 1)
                    for k in range(KT):
                        last = nc.tensor.matmul(ps_h[j][:, 0:NIMG], w[:, k, :], xp[:, j, k, :],
                                                start=k == 0, stop=k == KT - 1)
                    last.then_inc(embedded, 1)
                for j in range(2):
                    pe.wait_ge(hT_ready, i * 2 + j + 3)
                    pe.wait_ge(text_in[j], i * 16 + 16)
                    pe.wait_ge(h_ready, i * 2 + j + 1)
                    pe.sem_inc(held, 1)
                    for c in range(CH):
                        last = nc.tensor.transpose(ps_t[j][:, c, :], hT[:, j, c * CP:(c + 1) * CP],
                                                   ident[0:C, 0:C])
                    last.then_inc(h_turned, 1)
                for j in range(2):
                    pe.wait_ge(normed, i * 2 + j + 1)
                    pe.wait_ge(xT_ready, i * 2 + j + 1)
                    pe.sem_inc(held, 1)
                    for c in range(CH):
                        last = nc.tensor.transpose(ps_x[j][:, c * CP:(c + 1) * CP], xn[:, j, c, :],
                                                   ident[0:CP, 0:CP])
                    last.then_inc(x_turned, 1)

        @block.scalar
        def _(act):
            act.sem_inc(hT_ready, 2)
            act.sem_inc(h_ready, 2)
            act.sem_inc(xT_ready, 2)
            act.wait_ge(weights_in, 48)
            with act.Fori(0, NB // 2) as i:
                for j in range(2):
                    act.wait_ge(embedded, i * 2 + j + 1)
                    act.wait_ge(h_turned, i * 2 + j + 1)
                    nc.scalar.activation(hT[:, j, 0:NIMG], ps_h[j][:, 0:NIMG], ACT.Identity,
                                         bias=b[:, 0:1]).then_inc(hT_ready, 1)
                for j in range(2):
                    act.wait_ge(h_turned, i * 2 + j + 3)
                    act.wait_ge(out_free, i * 2 + j + 1)
                    nc.scalar.activation(h[:, j], ps_t[j][:], ACT.Copy).then_inc(h_ready, 1)
                for j in range(2):
                    norm.scalar(act, j, i * 2 + j)
                for j in range(2):
                    act.wait_ge(x_turned, i * 2 + j + 3)
                    nc.scalar.activation(xT[:, j], ps_x[j][:, 0:TOK], ACT.Copy).then_inc(xT_ready, 1)

        @block.vector
        def _(v):
            with v.Fori(0, NB // 2) as i:
                ch = Chain(v, dve, i, 2 * Norm.STEPS)
                for j in range(2):
                    v.wait_ge(h_ready, i * 2 + j + 3)
                    v.wait_ge(out_free, i * 2 + j + 1)
                    v.wait_ge(x_turned, i * 2 + j + 1)
                    norm.vector(ch, h[:, j], xn[:, j], j, i * 2 + j)
                    v.sem_inc(normed, 1)
                ch.close()

        @block.gpsimd
        def _(g):
            g.sem_inc(out_free, 2)
            with g.Fori(0, NB // 2) as i:
                for j in range(2):
                    s = i * 2 + j
                    g.wait_ge(h_ready, s + 3)
                    g.wait_ge(normed, s + 1)
                    g.sem_inc(held, 1)
                    g.dma_start(d["h0"][s], h[:, j]).then_inc(stored[j], 16)
                    g.dma_start(d["xn"][s], xn[:, j]).then_inc(stored[j], 16)
                    g.wait_ge(xT_ready, s + 3)
                    g.sem_inc(held, 1)
                    g.dma_start(d["xnT"][s], xT[:, j]).then_inc(stored[j], 16)
                for j in range(2):
                    g.wait_ge(stored[j], i * 48 + 48)
                    g.sem_inc(out_free, 1)


def stage_ssm_kernel(nc, d):
    with Mem(nc, "ssm") as m:
        par = m.sb("par", [128, 8])
        cq = m.sb("cq", [128, 2, C + 1])
        tanr = m.sb("tanr", [128, TOK])
        tanc = m.sb("tanc", [CP, CH])
        dft = m.sb("dft", [CP, CH, 2, TOK])
        g2 = m.sb("g2", [128, 6])
        den = m.sb("den", [128, TOK])
        q = m.sb("q", [128, TOK])
        V = m.sb("V", [128, TOK])
        dim = m.sb("dim", [128, TOK])
        R = m.sb("R", [128, 2, 2, C + 1])
        kk = m.sb("kk", [CP, CH, 2, 2, C + 1])
        w = m.sb("w", [CP, CH, 12])
        y = m.sb("y", [CP, CH, 2, C])
        at = m.sb("at", [CP, CH, 2, C])
        kr = m.sb("kr", [C, TOK + CP])
        ps = [m.ps(f"ps{c}", [CP, 512]) for c in range(CH)]
        psk = m.ps("psk", [C, 512])
        loaded, sums, turned, done, stored, dve = (m.sem(n) for n in
                                                   ("loaded", "sums", "turned", "done", "stored", "dve"))
        made = m.sem("made")
        spectrum = m.sem("spectrum")
        block = m.block()

        @block.sync
        def _(sp):
            for t, n in ((par, "par"), (cq, "cq"), (tanr, "tanr"), (tanc, "tanc"), (dft, "dft")):
                sp.dma_start(t[:], d[n]).then_inc(loaded, 16)
            sp.wait_ge(done, 1)
            sp.dma_start(d["krev"], kr[:]).then_inc(stored, 16)
            sp.wait_ge(stored, 16)

        @block.vector
        def _(v):
            ch = Chain(v, dve)
            tt, ts, stt = nc.vector.tensor_tensor, nc.vector.tensor_scalar, nc.vector.scalar_tensor_tensor
            v.wait_ge(loaded, 80)
            ch.step(nc.vector.memset(kr[:], 0.0))
            ch.link(ts(g2[:, 0:1], par[:, 6:7], 1e-6, None, ALU.max))
            ch.link(nc.vector.reciprocal(g2[:, 1:2], g2[:, 0:1]))
            ch.link(ts(g2[:, 1:2], g2[:, 1:2], 2.0, None, ALU.mult))
            ch.link(ts(dim[:], tanr[:], g2[:, 1:2], par[:, 1:2], ALU.mult, ALU.subtract))
            ch.link(tt(g2[:, 2:3], par[:, 0:1], par[:, 0:1], ALU.mult))
            ch.link(tt(den[:], dim[:], dim[:], ALU.mult))
            ch.link(ts(den[:], den[:], g2[:, 2:3], None, ALU.add))
            ch.link(nc.vector.reciprocal(den[:], den[:]))
            ch.step(ts(q[0:C, :], dim[0:C, :], 0.0, par[0:C, 0:1], ALU.mult, ALU.add))
            ch.step(nc.vector.tensor_copy(q[C:128, :], dim[C:128, :]))
            ch.sync()
            ch.link(stt(V[:], q[:], -1.0, den[:], ALU.mult, ALU.mult))
            for z in range(2):
                a, b = par[:, 2 + 2 * z:3 + 2 * z], par[:, 3 + 2 * z:4 + 2 * z]
                ch.link(tt(g2[:, 3:4], a, par[:, 7:8], ALU.mult))
                ch.step(ts(R[:, z, 0, :], cq[:, 0, :], g2[:, 3:4], None, ALU.mult))
                ch.step(ts(R[:, z, 1, :], cq[:, 0, :], b, None, ALU.mult))
                ch.step(ts(q[:, 0:C + 1], cq[:, 1, :], b, None, ALU.mult))
                ch.sync()
                ch.link(tt(R[:, z, 0, :], R[:, z, 0, :], q[:, 0:C + 1], ALU.subtract))
                ch.link(stt(R[:, z, 1, :], cq[:, 1, :], g2[:, 3:4], R[:, z, 1, :], ALU.mult, ALU.add))
            v.sem_inc(made, 1)
            v.wait_ge(sums, 1)
            for c in range(CH):
                ch.link(nc.vector.tensor_copy(kk[:, c].rearrange("p a b c -> p (a b c)"),
                                              ps[c][:, 0:4 * (C + 1)]))
            k10r, k10i = kk[:, :, 0, 0, C], kk[:, :, 0, 1, C]
            k11r, k11i = kk[:, :, 1, 0, C], kk[:, :, 1, 1, C]
            W = [w[:, :, n] for n in range(12)]
            ch.link(ts(W[0], k11r, 1.0, None, ALU.add))
            ch.step(tt(W[1], W[0], W[0], ALU.mult))
            ch.step(tt(W[2], k11i, k11i, ALU.mult))
            ch.sync()
            ch.link(tt(W[1], W[1], W[2], ALU.add))
            ch.step(nc.vector.reciprocal(W[3], W[1]))
            ch.step(tt(W[4], k10r, W[0], ALU.mult))
            ch.step(tt(W[5], k10i, k11i, ALU.mult))
            ch.step(tt(W[6], k10i, W[0], ALU.mult))
            ch.step(tt(W[7], k10r, k11i, ALU.mult))
            ch.sync()
            ch.step(tt(W[4], W[4], W[5], ALU.add))
            ch.step(tt(W[6], W[6], W[7], ALU.subtract))
            ch.sync()
            ch.step(tt(W[8], W[4], W[3], ALU.mult))
            ch.step(tt(W[9], W[6], W[3], ALU.mult))
            ch.sync()
            ch.step(ts(W[10], W[8], -1.0, None, ALU.mult))
            ch.step(ts(W[11], W[9], -1.0, None, ALU.mult))
            ch.sync()
            for c in range(CH):
                col = lambda n: w[:, c, n:n + 1]
                k01r, k01i = kk[:, c, 1, 0, 0:C], kk[:, c, 1, 1, 0:C]
                ch.step(stt(y[:, c, 0], k01r, col(10), kk[:, c, 0, 0, 0:C], ALU.mult, ALU.add))
                ch.step(stt(y[:, c, 1], k01r, col(11), kk[:, c, 0, 1, 0:C], ALU.mult, ALU.add))
                ch.sync()
                ch.step(stt(y[:, c, 0], k01i, col(9), y[:, c, 0], ALU.mult, ALU.add))
                ch.step(stt(y[:, c, 1], k01i, col(10), y[:, c, 1], ALU.mult, ALU.add))
                ch.sync()
                ch.link(ts(w[:, c, 0:1], tanc[:, c:c + 1], -1.0, None, ALU.mult))
                ch.step(stt(at[:, c, 0], y[:, c, 1], w[:, c, 0:1], y[:, c, 0], ALU.mult, ALU.add))
                ch.step(stt(at[:, c, 1], y[:, c, 0], tanc[:, c:c + 1], y[:, c, 1], ALU.mult, ALU.add))
                ch.sync()
            v.sem_inc(spectrum, 1)
            v.wait_ge(turned, 1)
            ch.link(nc.vector.tensor_copy(kr[:, 0:TOK], psk[:, 0:TOK]))
            v.sem_inc(done, 1)

        @block.tensor
        def _(pe):
            pe.wait_ge(made, 1)
            for c in range(CH):
                last = nc.tensor.matmul(ps[c][:, 0:4 * (C + 1)], V[:, c * CP:(c + 1) * CP],
                                        R[:].rearrange("p a b c -> p (a b c)"), start=True, stop=True)
            last.then_inc(sums, 1)
            pe.wait_ge(spectrum, 1)
            for c in range(CH):
                for z in range(2):
                    last = nc.tensor.matmul(psk[:, 0:TOK], at[:, c, z], dft[:, c, z],
                                            start=(c, z) == (0, 0), stop=(c, z) == (CH - 1, 1))
            last.then_inc(turned, 1)


def stage_conv(nc, d):
    with Mem(nc, "conv") as m:
        G = 8
        NG = C // G
        x = m.sb("x", [CP, NB, CH, C])
        toep = m.sb("toep", [CP, C, TOK])
        y = m.sb("y", [NB, 2, G, TOK])
        ps = [m.ps(f"ps{j}", [NB, 512]) for j in range(8)]
        x_in = m.sem("x_in")
        toep_in = [m.sem(f"toep_in{g}") for g in range(NG)]
        summed, taken, stored = m.sem("summed"), m.sem("taken"), [m.pool_dma_sem(f"stored{j}") for j in range(2)]
        block = m.block()
        krev = d["krev"]

        @block.sync
        def _(sp):
            sp.dma_start(x[:], d["xn"].rearrange("b p c e -> p b c e")).then_inc(x_in, 16)
            for g in range(NG):
                src = krev[g * G:(g + 1) * G, 0:TOK]
                src = bass.AP(tensor=src.tensor, offset=src.offset,
                              ap=[[1, CP], [TOK + CP, G], [1, TOK]])
                sp.dma_start(toep[:, g * G:(g + 1) * G, :], src).then_inc(toep_in[g], 16)

        @block.tensor
        def _(pe):
            pe.wait_ge(x_in, 16)
            for h in range(C):
                if h % G == 0:
                    pe.wait_ge(toep_in[h // G], 16)
                if h >= 8:
                    pe.wait_ge(taken, h - 7)
                for c in range(CH):
                    last = nc.tensor.matmul(ps[h % 8][:, 0:TOK - c * CP], x[:, :, c, h],
                                            toep[:, h, c * CP:TOK], start=c == 0, stop=c == CH - 1)
                last.then_inc(summed, 1)

        @block.scalar
        def _(act):
            for h in range(C):
                g, k = h // G, h % G
                act.wait_ge(summed, h + 1)
                if k == 0 and g >= 2:
                    act.wait_ge(stored[g % 2], g // 2 * 16)
                nc.scalar.activation(y[:, g % 2, k, :], ps[h % 8][:, 0:TOK][:, ::-1], ACT.Copy).then_inc(taken, 1)

        @block.gpsimd
        def _(g_):
            for g in range(NG):
                g_.wait_ge(taken, (g + 1) * G)
                g_.dma_start(d["conv"][:, g * G:(g + 1) * G, :], y[:, g % 2]).then_inc(stored[g % 2], 16)
            for j in range(2):
                g_.wait_ge(stored[j], NG // 2 * 16)


class Tail:

    def __init__(self, nc, m, d, held, ident, names):
        self.nc, self.d, self.held, self.ident, self.names = nc, d, held, ident, names
        self.h = m.sb("new_h", [CP, 2, CH, C])
        self.x = m.sb("new_x", [CP, 2, CH, C])
        self.xT = m.sb("new_xT", [C, 2, TOK])
        self.ps = m.ps("ps_new_xT", [C, 512])
        self.h_ready = m.sem("new_h_ready")
        self.normed = m.sem("normed")
        self.x_turned = m.sem("x_turned")
        self.xT_ready = m.sem("xT_ready")
        self.stored = [m.pool_dma_sem(f"stored{j}") for j in range(2)]
        self.out_free = m.sem("out_free")
        self.norm = Norm(nc, m, held)

    def vector_begin(self, v, s):
        v.wait_ge(self.out_free, s + 1)
        v.wait_ge(self.x_turned, s + 1)

    def vector(self, ch, j, s):
        ch.eng.sem_inc(self.h_ready, 1)
        self.norm.vector(ch, self.h[:, j], self.x[:, j], j, s)
        ch.eng.sem_inc(self.normed, 1)

    def tensor_start(self, pe):
        pe.sem_inc(self.x_turned, 2)

    def tensor(self, pe, j, s):
        pe.wait_ge(self.normed, s + 1)
        pe.wait_ge(self.xT_ready, s + 1)
        pe.sem_inc(self.held, 1)
        for c in range(CH):
            last = self.nc.tensor.transpose(self.ps[:, c * CP:(c + 1) * CP], self.x[:, j, c, :],
                                            self.ident[0:CP, 0:CP])
        last.then_inc(self.x_turned, 1)

    def scalar_start(self, act):
        act.sem_inc(self.xT_ready, 1)

    def scalar(self, act, j, s):
        act.wait_ge(self.x_turned, s + 3)
        act.wait_ge(self.out_free, s + 1)
        self.nc.scalar.activation(self.xT[:, j], self.ps[:, 0:TOK], ACT.Copy).then_inc(self.xT_ready, 1)

    def gpsimd(self, g):
        hn, xn, xTn = self.names
        g.sem_inc(self.out_free, 2)
        kinds = 3 if xn else 2
        with g.Fori(0, NB // 2) as i:
            for j in range(2):
                s = i * 2 + j
                g.wait_ge(self.normed, s + 1)
                g.sem_inc(self.held, 1)
                g.dma_start(self.d[hn][s], self.h[:, j]).then_inc(self.stored[j], 16)
                if xn:
                    g.dma_start(self.d[xn][s], self.x[:, j]).then_inc(self.stored[j], 16)
                g.wait_ge(self.xT_ready, s + 2)
                g.sem_inc(self.held, 1)
                g.dma_start(self.d[xTn][s], self.xT[:, j]).then_inc(self.stored[j], 16)
            for j in range(2):
                g.wait_ge(self.stored[j], i * (16 * kinds) + 16 * kinds)
                g.sem_inc(self.out_free, 1)


def stage_mix(nc, d):
    with Mem(nc, "mix") as m:
        ident = m.sb("ident", [128, 128])
        w = m.sb("w", [C, C])
        D = m.sb("D", [C, 1])
        rows = m.sb("rows", [CP, 3, CH, C])
        hin = m.sb("hin", [CP, 2, CH, C])
        xin = m.sb("xin", [CP, 2, CH, C])
        xT = m.sb("xT", [C, 2, TOK])
        cv = m.sb("cv", [C, 2, TOK])
        u = m.sb("u", [C, 2, TOK])
        y1 = m.sb("y1", [C, 2, TOK])
        t = m.sb("t", [CP, 2, CH, C])
        g_ = m.sb("g", [CP, 2, CH, C])
        y2 = m.sb("y2", [CP, 2, CH, C])
        ps = [m.ps(f"ps_fc{j}", [CP, CH, C]) for j in range(2)]
        held = m.sem("held")
        weights_in = m.sem("weights_in")
        loaded = [m.sem(f"loaded{j}") for j in range(2)]
        taken = m.sem("taken")
        u_ready, y1_ready, fc_done, t_ready, g_ready = (m.sem(n) for n in (
            "u_ready", "y1_ready", "fc_done", "t_ready", "g_ready"))
        dve = m.sem("dve")
        tail = Tail(nc, m, d, held, ident, ("h1", None, "x1T"))
        inner = Norm(nc, m, held, "inner")
        block = m.block()

        @block.sync
        def _(sp):
            for a, n in ((ident, "ident"), (w, "fcT"), (D, "skipD"), (rows, "mix_rows")):
                sp.dma_start(a[:], d[n]).then_inc(weights_in, 16)
            with sp.Fori(0, NB // 2) as i:
                for j in range(2):
                    s = i * 2 + j
                    sp.wait_ge(taken, s + 1)
                    sp.dma_start(hin[:, j], d["h0"][s]).then_inc(loaded[j], 16)
                    sp.dma_start(xin[:, j], d["xn"][s]).then_inc(loaded[j], 16)
                    sp.dma_start(xT[:, j], d["xnT"][s]).then_inc(loaded[j], 16)
                    sp.dma_start(cv[:, j], d["conv"][s]).then_inc(loaded[j], 16)

        @block.vector
        def _(v):
            v.sem_inc(taken, 2)
            v.wait_ge(weights_in, 64)
            with v.Fori(0, NB // 2) as i:
                ch = Chain(v, dve, i, 2 * (2 + 1 + 2 * Norm.STEPS + 3))
                for j in range(2):
                    v.wait_ge(loaded[j], i * 64 + 64)
                    v.wait_ge(y1_ready, i * 2 + j + 1)
                    ch.link(nc.vector.scalar_tensor_tensor(u[:, j], xT[:, j], D[:, 0:1], cv[:, j],
                                                           ALU.mult, ALU.add))
                    v.sem_inc(u_ready, 1)
                for j in range(2):
                    v.wait_ge(fc_done, i * 2 + j + 1)
                    v.wait_ge(g_ready, i * 2 + j + 1)
                    ch.link(nc.vector.tensor_tensor(t[:, j], ps[j][:], rows[:, 0], ALU.add))
                    v.sem_inc(t_ready, 1)
                for j in range(2):
                    v.wait_ge(g_ready, i * 2 + j + 3)
                    ch.link(nc.vector.tensor_tensor(y2[:, j], g_[:, j], xin[:, j], ALU.add))
                    inner.vector(ch, y2[:, j], y2[:, j], j, i * 2 + j)
                    tail.vector_begin(v, i * 2 + j)
                    ch.link(nc.vector.tensor_tensor(y2[:, j], y2[:, j], rows[:, 1], ALU.mult))
                    ch.link(nc.vector.tensor_tensor(y2[:, j], y2[:, j], rows[:, 2], ALU.add))
                    ch.link(nc.vector.tensor_tensor(tail.h[:, j], y2[:, j], hin[:, j], ALU.add))
                    v.sem_inc(taken, 1)
                    tail.vector(ch, j, i * 2 + j)
                ch.close()

        @block.scalar
        def _(act):
            act.sem_inc(y1_ready, 2)
            act.sem_inc(g_ready, 2)
            tail.scalar_start(act)
            with act.Fori(0, NB // 2) as i:
                for j in range(2):
                    act.wait_ge(u_ready, i * 2 + j + 1)
                    nc.scalar.activation(y1[:, j], u[:, j], ACT.Gelu).then_inc(y1_ready, 1)
                for j in range(2):
                    act.wait_ge(t_ready, i * 2 + j + 1)
                    nc.scalar.activation(g_[:, j], t[:, j], ACT.Gelu).then_inc(g_ready, 1)
                for j in range(2):
                    inner.scalar(act, j, i * 2 + j)
                    tail.norm.scalar(act, j, i * 2 + j)
                for j in range(2):
                    tail.scalar(act, j, i * 2 + j)

        @block.tensor
        def _(pe):
            tail.tensor_start(pe)
            pe.wait_ge(weights_in, 64)
            with pe.Fori(0, NB // 2) as i:
                for j in range(2):
                    pe.wait_ge(y1_ready, i * 2 + j + 3)
                    pe.sem_inc(held, 1)
                    for c in range(CH):
                        last = nc.tensor.matmul(ps[j][:, c, :], y1[:, j, c * CP:(c + 1) * CP], w[:],
                                                start=True, stop=True)
                    last.then_inc(fc_done, 1)
                for j in range(2):
                    tail.tensor(pe, j, i * 2 + j)

        @block.gpsimd
        def _(g):
            tail.gpsimd(g)


E = 8
HID = 682
HT = 114
NT = 6


def stage_experts(nc, d):
    with Mem(nc, "moe") as m:
        ident = m.sb("ident", [128, 128])
        router = m.sb("router", [C, E])
        pick = m.sb("pick", [E, E // 2, 128])
        w13 = m.sb("w13", [128, E, NT * HT])
        w2 = m.sb("w2", [HT, E, NT, C])
        x = m.sb("x", [128, 2, TOK])
        hin = m.sb("hin", [CP, 2, CH, C])
        top = m.sb("top", [CP, CH, 8])
        neg = m.sb("neg", [CP, CH])
        logit = m.sb("logit", [CP, CH, E])
        ex = m.sb("ex", [CP, CH, E])
        gate = m.sb("gate", [CP, CH, E])
        mask = m.sb("mask", [CP, CH, E])
        s1 = m.sb("s1", [CP, CH])
        gT = m.sb("gT", [E, TOK])
        G = m.sb("G", [128, 2, TOK])
        sg = m.sb("sg", [HT, 2, TOK])
        hh = m.sb("hh", [HT, 2, TOK])
        ty = m.sb("ty", [128, 2, TOK])
        acc = m.sb("acc", [128, 2, TOK])
        ps1 = [m.ps(f"ps1{k}", [HT, 512]) for k in range(2)]
        ps3 = [m.ps(f"ps3{k}", [HT, 512]) for k in range(2)]
        psy = m.ps("psy", [128, 512])
        psg = m.ps("psg", [128, 512])
        psr = m.ps("psr", [128, 512])
        held = m.sem("held")
        weights_in = m.sem("weights_in")
        loaded = [m.sem(f"loaded{j}") for j in range(2)]
        taken = m.sem("taken")
        names = ("routed", "logit_ready", "top_ready", "ex_ready", "gate_ready", "gate_turned", "gT_ready",
                 "spread", "G_ready", "G_used", "up_done", "sg_ready", "hh_ready", "down_done", "y_taken",
                 "acc_ready", "acc_turned", "acc_taken")
        (routed, logit_ready, top_ready, ex_ready, gate_ready, gate_turned, gT_ready, spread, G_ready,
         G_used, up_done, sg_ready, hh_ready, down_done, y_taken, acc_ready, acc_turned,
         acc_taken) = (m.sem(n) for n in names)
        dve = m.sem("dve")
        tail = Tail(nc, m, d, held, ident, ("h2", "x2", "x2T"))
        block = m.block()
        TILES = E * NT
        Q = E // 2

        def place(n):
            q, r = divmod(n, 2 * NT)
            return 2 * q + r % 2, r // 2

        @block.sync
        def _(sp):
            for a, n in ((ident, "ident"), (router, "routerT"), (pick, "pick"), (w13, "w13"), (w2, "w2")):
                sp.dma_start(a[:], d[n]).then_inc(weights_in, 16)
            with sp.Fori(0, NB // 2) as i:
                for j in range(2):
                    s = i * 2 + j
                    sp.wait_ge(taken, s + 1)
                    for half in range(2):
                        sp.dma_start(x[half * C:half * C + C, j], d["x1T"][s]).then_inc(loaded[j], 16)
                    sp.dma_start(hin[:, j], d["h1"][s]).then_inc(loaded[j], 16)

        @block.tensor
        def _(pe):
            tail.tensor_start(pe)
            pe.wait_ge(weights_in, 80)
            with pe.Fori(0, NB // 2) as i:
                for j in range(2):
                    s = i * 2 + j
                    base = s * TILES

                    def up(n):
                        e, t = place(n)
                        pe.wait_ge(hh_ready, base + n + 1)
                        cols = slice(t * HT, (t + 1) * HT)
                        nc.tensor.matmul(ps1[n % 2][:, 0:TOK], w13[0:C, e, cols], x[0:C, j], start=True, stop=True)
                        nc.tensor.matmul(ps3[n % 2][:, 0:TOK], w13[C:128, e, cols], x[C:128, j],
                                         start=True, stop=True).then_inc(up_done, 1)

                    pe.wait_ge(loaded[j], i * 48 + 48)
                    pe.wait_ge(gT_ready, s + 1)
                    pe.sem_inc(held, 1)
                    for c in range(CH):
                        last = nc.tensor.matmul(psr[0:CP, c * E:(c + 1) * E], x[0:C, j, c * CP:(c + 1) * CP],
                                                router[:], start=True, stop=True)
                    last.then_inc(routed, 1)
                    up(0)
                    for n in range(TILES):
                        if n + 1 < TILES:
                            up(n + 1)
                        e, t = place(n)
                        if n == NT:
                            pe.wait_ge(gate_ready, s + 1)
                            pe.sem_inc(held, 1)
                            for c in range(CH):
                                last = nc.tensor.transpose(psr[0:E, c * CP:(c + 1) * CP], gate[:, c, :],
                                                           ident[0:CP, 0:CP])
                            last.then_inc(gate_turned, 1)
                        if n % (2 * NT) == 2 * NT - 2:
                            pe.wait_ge(gT_ready, s + 2)
                            pe.wait_ge(G_ready, s * Q + n // (2 * NT) + 1)
                            pe.wait_ge(acc_taken, s + 1)
                            nc.tensor.matmul(psg[:, 0:TOK], pick[:, n // (2 * NT), :], gT[:],
                                             start=True, stop=True).then_inc(spread, 1)
                        if n % (2 * NT) == 0:
                            pe.wait_ge(y_taken, s * Q + n // (2 * NT) + 1)
                        pe.wait_ge(hh_ready, base + n + 3)
                        p = (e % 2) * C
                        nc.tensor.matmul(psy[p:p + C, 0:TOK], w2[:, e, t, :], hh[:, n % 2],
                                         start=t == 0, stop=t == NT - 1).then_inc(down_done, 1)
                    pe.wait_ge(acc_ready, s + 1)
                    pe.sem_inc(held, 1)
                    for c in range(CH):
                        last = nc.tensor.transpose(psg[0:CP, c * 128:(c + 1) * 128],
                                                   acc[:, j, c * CP:(c + 1) * CP], ident[:, :])
                    last.then_inc(acc_turned, 1)
                for j in range(2):
                    tail.tensor(pe, j, i * 2 + j)

        @block.scalar
        def _(act):
            act.sem_inc(gT_ready, 1)
            act.sem_inc(G_ready, 1)
            tail.scalar_start(act)
            with act.Fori(0, NB // 2) as i:
                for j in range(2):
                    s = i * 2 + j
                    base = s * TILES

                    def tiles(a, b):
                        for n in range(a, b):
                            act.wait_ge(up_done, base + n + 1)
                            act.wait_ge(hh_ready, base + n + 1)
                            nc.scalar.activation(sg[:, n % 2], ps1[n % 2][:, 0:TOK], ACT.Silu)\
                                .then_inc(sg_ready, 1)

                    act.wait_ge(top_ready, s + 1)
                    for c in range(CH):
                        last = nc.scalar.activation(ex[:, c, :], logit[:, c, :], ACT.Exp,
                                                    bias=neg[:, c:c + 1])
                    last.then_inc(ex_ready, 1)
                    tiles(0, NT + 1)
                    act.wait_ge(gate_turned, s + 1)
                    act.wait_ge(G_ready, s * Q + 1)
                    nc.scalar.activation(gT[:], psr[0:E, 0:TOK], ACT.Copy).then_inc(gT_ready, 1)
                    for q in range(Q):
                        tiles(max(NT + 1, q * 2 * NT), (q + 1) * 2 * NT)
                        act.wait_ge(spread, s * Q + q + 1)
                        act.wait_ge(G_used, s * Q + q + 1)
                        nc.scalar.activation(G[:, q % 2], psg[:, 0:TOK], ACT.Copy).then_inc(G_ready, 1)
                    tail.norm.scalar(act, j, s)
                for j in range(2):
                    tail.scalar(act, j, i * 2 + j)

        @block.vector
        def _(v):
            tt, ts = nc.vector.tensor_tensor, nc.vector.tensor_scalar
            v.sem_inc(taken, 2)
            v.sem_inc(hh_ready, 2)
            v.sem_inc(y_taken, 1)
            v.sem_inc(G_used, 2)
            v.sem_inc(acc_taken, 1)
            v.wait_ge(weights_in, 80)
            with v.Fori(0, NB // 2) as i:
                ch = Chain(v, dve, i, 2 * (1 + 3 + 1 + 9 + 7 + 2 + Norm.STEPS))
                for j in range(2):
                    s = i * 2 + j
                    base = s * TILES

                    def tiles(a, b):
                        for n in range(a, b):
                            v.wait_ge(sg_ready, base + n + 1)
                            if n >= 2:
                                v.wait_ge(down_done, base + n - 1)
                            tt(hh[:, n % 2], sg[:, n % 2], ps3[n % 2][:, 0:TOK], ALU.mult).then_inc(hh_ready, 1)

                    wide = lambda a: a.unsqueeze(2).broadcast_to((CP, CH, E))
                    v.wait_ge(routed, s + 1)
                    ch.link(nc.vector.tensor_copy(logit[:].rearrange("p c e -> p (c e)"), psr[0:CP, 0:CH * E]))
                    v.sem_inc(held, 1)
                    for c in range(CH):
                        ch.step(nc.vector.max(top[:, c, :], logit[:, c, :]))
                    ch.sync()
                    ch.link(ts(neg[:], top[:, :, 0], -1.0, None, ALU.mult))
                    v.sem_inc(top_ready, 1)
                    v.wait_ge(ex_ready, s + 1)
                    ch.link(nc.vector.tensor_reduce(s1[:], ex[:], AX.X, ALU.add))
                    ch.link(nc.vector.reciprocal(s1[:], s1[:]))
                    ch.step(tt(gate[:], ex[:], wide(s1[:]), ALU.mult))
                    ch.link(tt(mask[:], logit[:], wide(top[:, :, 1]), ALU.is_ge))
                    ch.link(tt(gate[:], gate[:], mask[:], ALU.mult))
                    ch.link(nc.vector.tensor_reduce(s1[:], gate[:], AX.X, ALU.add))
                    ch.link(ts(s1[:], s1[:], 1e-9, None, ALU.add))
                    ch.link(nc.vector.reciprocal(s1[:], s1[:]))
                    ch.link(tt(gate[:], gate[:], wide(s1[:]), ALU.mult))
                    v.sem_inc(gate_ready, 1)
                    for q in range(Q):
                        tiles(q * 2 * NT, (q + 1) * 2 * NT)
                        v.wait_ge(down_done, base + (q + 1) * 2 * NT)
                        v.wait_ge(G_ready, s * Q + q + 2)
                        if q == 0:
                            ch.link(tt(acc[:, j], psy[:, 0:TOK], G[:, q % 2], ALU.mult))
                        else:
                            ch.link(tt(ty[:, 0], psy[:, 0:TOK], G[:, q % 2], ALU.mult))
                            ch.link(tt(acc[:, j], acc[:, j], ty[:, 0], ALU.add))
                        v.sem_inc(y_taken, 1)
                        v.sem_inc(G_used, 1)
                    v.sem_inc(acc_ready, 1)
                    v.wait_ge(acc_turned, s + 1)
                    tail.vector_begin(v, s)
                    both = psg[0:CP, 0:CH * 128].rearrange("p (c h e) -> p c h e", c=CH, h=2)
                    ch.link(tt(tail.h[:, j], both[:, :, 0, :], hin[:, j], ALU.add))
                    ch.link(tt(tail.h[:, j], both[:, :, 1, :], tail.h[:, j], ALU.add))
                    v.sem_inc(acc_taken, 1)
                    v.sem_inc(taken, 1)
                    tail.vector(ch, j, s)
                ch.close()

        @block.gpsimd
        def _(g):
            tail.gpsimd(g)


def stage_pairs(nc, d):
    with Mem(nc, "pair") as m:
        K1 = C + 1
        ident = m.sb("ident", [128, 128])
        mix = m.sb("mix", [K1, K1])
        wtop = m.sb("wtop", [K1, 3 * C])
        wbot = m.sb("wbot", [C, 3 * C])
        xT = m.sb("xT", [K1, 2, TOK])
        x = m.sb("x", [CP, 2, CH, C])
        hin = m.sb("hin", [CP, 2, CH, C])
        L = m.sb("L", [K1, TOK])
        mx = m.sb("mx", [CP, 2, CH])
        sm = m.sb("sm", [CP, 2, CH])
        ex = m.sb("ex", [CP, 2, CH, TOK])
        AT = m.sb("AT", [CP, CH, TOK])
        it = m.sb("it", [C, TOK])
        zr = m.sb("zr", [CP, CH, 3 * C])
        t1 = m.sb("t1", [CP, CH, C])
        t2 = m.sb("t2", [CP, CH, C])
        psA = [m.ps(f"psA{c}", [CP, 512]) for c in range(CH)]
        psT = [m.ps(f"psT{c}", [CP, 512]) for c in range(CH)]
        psL = m.ps("psL", [K1, 512])
        held = m.sem("held")
        weights_in = m.sem("weights_in")
        loaded = [m.sem(f"loaded{j}") for j in range(2)]
        (taken, ones, left_done, left_ready, A_done, max_ready, ex_ready, probs_ready, probs_turned, AT_ready,
         it_done, it_ready, gates_done, gates_ready, mixed) = (m.sem(n) for n in (
             "taken", "ones", "left_done", "left_ready", "A_done", "max_ready", "ex_ready", "probs_ready",
             "probs_turned", "AT_ready", "it_done", "it_ready", "gates_done", "gates_ready", "mixed"))
        dve = m.sem("dve")
        tail = Tail(nc, m, d, held, ident, ("h3", None, "x3T"))
        block = m.block()

        @block.sync
        def _(sp):
            for a, n in ((ident, "ident"), (mix, "pair_mix"), (wtop, "pair_top"), (wbot, "pair_bot")):
                sp.dma_start(a[:], d[n]).then_inc(weights_in, 16)
            with sp.Fori(0, NB // 2) as i:
                for j in range(2):
                    s = i * 2 + j
                    sp.wait_ge(taken, s + 1)
                    sp.dma_start(xT[0:C, j], d["x2T"][s]).then_inc(loaded[j], 16)
                    sp.dma_start(x[:, j], d["x2"][s]).then_inc(loaded[j], 16)
                    sp.dma_start(hin[:, j], d["h2"][s]).then_inc(loaded[j], 16)

        @block.tensor
        def _(pe):
            tail.tensor_start(pe)
            pe.wait_ge(weights_in, 64)
            pe.wait_ge(ones, 1)
            with pe.Fori(0, NB // 2) as i:
                for j in range(2):
                    s = i * 2 + j
                    chunk = lambda c: slice(c * CP, (c + 1) * CP)
                    pe.wait_ge(loaded[j], i * 48 + 48)
                    pe.wait_ge(it_ready, s + 1)
                    pe.wait_ge(gates_ready, s + 1)
                    pe.sem_inc(held, 1)
                    nc.tensor.matmul(psL[:, 0:TOK], mix[:], xT[:, j], start=True, stop=True).then_inc(left_done, 1)
                    pe.wait_ge(left_ready, s + 1)
                    for c in range(CH):
                        last = nc.tensor.matmul(psA[c][:, 0:TOK], L[:, chunk(c)], xT[:, j], start=True, stop=True)
                    last.then_inc(A_done, 1)
                    pe.wait_ge(probs_ready, s + 1)
                    pe.sem_inc(held, 1)
                    for jc in range(CH):
                        for c in range(CH):
                            last = nc.tensor.transpose(psT[jc][:, chunk(c)], ex[:, j, c, chunk(jc)],
                                                       ident[0:CP, 0:CP])
                        last.then_inc(probs_turned, 1)
                    for jc in range(CH):
                        pe.wait_ge(AT_ready, s * 3 + jc + 1)
                        last = nc.tensor.matmul(psL[0:C, 0:TOK], x[:, j, jc, :], AT[:, jc, :],
                                                start=jc == 0, stop=jc == CH - 1)
                    last.then_inc(it_done, 1)
                    pe.wait_ge(it_ready, s + 2)
                    pe.sem_inc(held, 1)
                    for c in range(CH):
                        nc.tensor.matmul(psA[c][:, 0:3 * C], xT[:, j, chunk(c)], wtop[:], start=True, stop=False)
                        last = nc.tensor.matmul(psA[c][:, 0:3 * C], it[:, chunk(c)], wbot[:], start=False, stop=True)
                    last.then_inc(gates_done, 1)
                for j in range(2):
                    tail.tensor(pe, j, i * 2 + j)

        @block.scalar
        def _(act):
            act.sem_inc(it_ready, 1)
            act.sem_inc(gates_ready, 1)
            tail.scalar_start(act)
            with act.Fori(0, NB // 2) as i:
                for j in range(2):
                    s = i * 2 + j
                    act.wait_ge(left_done, s + 1)
                    nc.scalar.activation(L[:], psL[:, 0:TOK], ACT.Copy).then_inc(left_ready, 1)
                    act.wait_ge(max_ready, s + 1)
                    for c in range(CH):
                        last = nc.scalar.activation(ex[:, j, c, :], psA[c][:, 0:TOK], ACT.Exp,
                                                    bias=mx[:, j, c:c + 1], accum_out=sm[:, j, c:c + 1])
                    last.then_inc(ex_ready, 1)
                    for jc in range(CH):
                        act.wait_ge(probs_turned, s * 3 + jc + 1)
                        nc.scalar.activation(AT[:, jc, :], psT[jc][:, 0:TOK], ACT.Copy).then_inc(AT_ready, 1)
                    act.wait_ge(it_done, s + 1)
                    nc.scalar.activation(it[:], psL[0:C, 0:TOK], ACT.Copy).then_inc(it_ready, 1)
                    act.wait_ge(gates_done, s + 1)
                    act.wait_ge(mixed, s + 1)
                    for c in range(CH):
                        nc.scalar.activation(zr[:, c, 0:C], psA[c][:, 0:C], ACT.Tanh)
                        last = nc.scalar.activation(zr[:, c, C:3 * C], psA[c][:, C:3 * C], ACT.Tanh, scale=0.5)
                    last.then_inc(gates_ready, 1)
                    tail.norm.scalar(act, j, s)
                for j in range(2):
                    tail.scalar(act, j, i * 2 + j)

        @block.vector
        def _(v):
            tt, ts = nc.vector.tensor_tensor, nc.vector.tensor_scalar
            nc.vector.memset(xT[C:K1], 1.0).then_inc(ones, 1)
            v.sem_inc(taken, 2)
            v.sem_inc(mixed, 1)
            v.wait_ge(weights_in, 64)
            with v.Fori(0, NB // 2) as i:
                ch = Chain(v, dve, i, 2 * (3 + 1 + 1 + 3 + 5 + Norm.STEPS))
                for j in range(2):
                    s = i * 2 + j
                    v.wait_ge(A_done, s + 1)
                    for c in range(CH):
                        ch.step(nc.vector.tensor_reduce(mx[:, j, c:c + 1], psA[c][:, 0:TOK], AX.X, ALU.max))
                    ch.sync()
                    ch.link(ts(mx[:, j], mx[:, j], -1.0, None, ALU.mult))
                    v.sem_inc(max_ready, 1)
                    v.wait_ge(ex_ready, s + 1)
                    ch.link(nc.vector.reciprocal(sm[:, j], sm[:, j]))
                    for c in range(CH):
                        ch.step(ts(ex[:, j, c, :], ex[:, j, c, :], sm[:, j, c:c + 1], None, ALU.mult))
                    ch.sync()
                    v.sem_inc(probs_ready, 1)
                    v.wait_ge(gates_ready, s + 2)
                    tail.vector_begin(v, s)
                    ch.link(ts(zr[:, :, C:3 * C], zr[:, :, C:3 * C], 0.5, 0.5, ALU.mult, ALU.add))
                    ch.step(tt(t1[:], zr[:, :, C:2 * C], x[:, j], ALU.mult))
                    ch.link(tt(t2[:], zr[:, :, 2 * C:3 * C], zr[:, :, 0:C], ALU.mult))
                    ch.step(tt(t1[:], t1[:], hin[:, j], ALU.add))
                    ch.sync()
                    ch.link(tt(tail.h[:, j], t1[:], t2[:], ALU.add))
                    v.sem_inc(mixed, 1)
                    v.sem_inc(taken, 1)
                    tail.vector(ch, j, s)
                ch.close()

        @block.gpsimd
        def _(g):
            tail.gpsimd(g)


HEADS = 8
NK = 64
DK = 32
TOPK = 16
NT4 = NK * NK // 128
ROWS = [(i, TOPK // (i + 1)) for i in range(5)]
NCAND = sum(w for _, w in ROWS) + 3 * 2 + 8
FLOOR = 87.0
LIFT = 40.0
SLACK = 2.0 ** -21
HIDDEN = -1e30


def stage_keys(nc, d):
    with Mem(nc, "keys") as m:
        wq = m.sb("wq", [DK, 2, HEADS, C])
        keys = m.sb("keys", [DK, 2, HEADS, NK])
        both = m.sb("both", [C, HEADS, 2, NK])
        ps = [m.ps(f"ps{k}", [C, 4, 2, NK]) for k in range(2)]
        loaded, done, copied, stored = (m.sem(n) for n in ("loaded", "done", "copied", "stored"))
        block = m.block()

        @block.sync
        def _(sp):
            sp.dma_start(wq[:], d["wq_pk"]).then_inc(loaded, 16)
            sp.dma_start(keys[:], d["pk_keys"]).then_inc(loaded, 16)
            sp.wait_ge(copied, 2)
            sp.dma_start(d["score_w"].rearrange("h c k -> c h k"),
                         both[:].rearrange("c h p k -> c h (p k)")).then_inc(stored, 16)
            sp.wait_ge(stored, 16)

        @block.tensor
        def _(pe):
            pe.wait_ge(loaded, 32)
            for h in range(HEADS):
                for p in range(2):
                    last = nc.tensor.matmul(ps[h // 4][:, h % 4, p, :], wq[:, p, h, :], keys[:, p, h, :],
                                            start=True, stop=True)
                if h % 4 == 3:
                    last.then_inc(done, 1)

        @block.scalar
        def _(act):
            for k in range(2):
                act.wait_ge(done, k + 1)
                nc.scalar.activation(both[:, 4 * k:4 * k + 4], ps[k][:], ACT.Copy).then_inc(copied, 1)


def stage_memory(nc, d):
    with Mem(nc, "mem") as m:
        ident = m.sb("ident", [128, 128])
        tri = m.sb("tri", [CP, CP])
        acc = m.sb("acc", [CP, NB, CH, C])
        pick_in = m.sb("pick_in", [128, NT4, 128])
        pick = m.sb("pick", [128, NT4, 128], F32R)
        table = m.sb("table", [128, NT4, 128])
        score_w = m.sb("score_w", [C, 2 * NK])
        wq = m.sb("wq", [C, C])
        wo = m.sb("wo", [C, C])
        lift = m.sb("lift", [128, 1])
        xT = m.sb("xT", [C, 2, TOK])
        S = m.sb("S", [CP, CH, 2 * NK])
        rest = m.sb("rest", [CP, CH, 2, NK])
        lists = m.sb("lists", [CP, CH, 2, TOPK])
        cand = m.sb("cand", [CP, CH, NCAND])
        cand2 = m.sb("cand2", [CP, CH, NCAND])
        best = m.sb("best", [CP, CH, TOPK])
        size = m.sb("size", [CP, CH])
        cut = m.sb("cut", [CP, CH])
        terms = m.sb("terms", [CP, CH, TOPK])
        rZ = m.sb("rZ", [CP, 2, CH])
        Zh = m.sb("Zh", [128, 2, TOK + 1], F32R)
        Zl = m.sb("Zl", [128, 2, TOK + 1], F32R)
        ex = m.sb("ex", [128, 3, TOK])
        wt = m.sb("wt", [128, 3, TOK])
        kvT = m.sb("kvT", [128, TOK])
        kv = m.sb("kv", [CP, CH, 128])
        kT = m.sb("kT", [C, TOK])
        qT = m.sb("qT", [C, 2, TOK])
        mx = m.sb("mx", [CP, CH])
        sm = m.sb("sm", [CP, CH])
        pr = m.sb("pr", [CP, CH, TOK])
        PT = m.sb("PT", [CP, 2, TOK])
        oT = m.sb("oT", [C, TOK])
        ps_z = [m.ps(f"ps_z{k}", [128, 512]) for k in range(3)]
        ps_kv = m.ps("ps_kv", [128, 512])
        ps_a = m.ps("ps_a", [128, 512])
        ps_c = m.ps("ps_c", [128, 512])
        ps_s = [m.ps(f"ps_s{k}", [CP, 512]) for k in range(2)]
        held = m.sem("held")
        consts_in = m.sem("consts_in")
        pick_ready = m.sem("pick_ready")
        head_in = m.sem("head_in")
        table_in = [m.sem(f"table_in{k}") for k in range(4)]
        x_in = [m.sem(f"x_in{j}") for j in range(2)]
        scored, S_ready, best_ready, terms_ready, cut_done, cut_turned, high_ready, Z_ready = (
            m.sem(n) for n in ("scored", "S_ready", "best_ready", "terms_ready", "cut_done", "cut_turned",
                               "high_ready", "Z_ready"))
        z_done, ex_ready, wt_ready, kv_done = (m.sem(n) for n in ("z_done", "ex_ready", "wt_ready", "kv_done"))
        (q_done, q_ready, kvT_ready, kv_turned, kv_ready, k_turned, kT_ready, s_done, max_ready, e_ready,
         p_ready, p_turned, PT_ready, o_done, oT_ready, out_done, added) = (m.sem(n) for n in (
             "q_done", "q_ready", "kvT_ready", "kv_turned", "kv_ready", "k_turned", "kT_ready", "s_done",
             "max_ready", "e_ready", "p_ready", "p_turned", "PT_ready", "o_done", "oT_ready", "out_done",
             "added"))
        head_free = m.sem("head_free")
        stored = m.sem("stored")
        dve_a, dve_c = m.sem("dve_a"), m.sem("dve_c")
        block = m.block()
        chunk = lambda c: slice(c * CP, (c + 1) * CP)
        score_at = [ps_s[0][:, 0:CP], ps_s[0][:, CP:3 * CP], ps_s[1][:, 0:TOK]]
        diag_at = [ps_s[0][:, 0:CP], ps_s[0][:, 2 * CP:3 * CP], ps_s[1][:, 2 * CP:TOK]]

        def turned_at(jc, c):
            return ps_s[0][:, chunk(c)] if jc == 0 else ps_s[1][:, chunk(c - 1 if jc == 1 else 2)]

        def before(u, n):
            return u * NT4 + {0: 2, 1: 3}.get(n, n + 1)

        def units(eng, a, body, c):
            with eng.Fori(0, HEADS) as h:
                u0 = h * NB
                yield h
                a(u0, 0, 0)
                body(u0, 0, 0, True, False)
                with eng.Fori(0, (NB - 2) // 2) as i:
                    for j in range(2):
                        s = i * 2 + (1 + j)
                        body(u0 + s, s, (1 + j) % 2, True, True)
                body(u0 + (NB - 1), NB - 1, 1, False, True)
                c(u0 + (NB - 1), NB - 1, 1)

        @block.sync
        def _(sp):
            for t, n in ((ident, "ident"), (tri, "tri"), (pick_in, "key_pick")):
                sp.dma_start(t[:], d[n]).then_inc(consts_in, 16)
            sp.dma_start(acc[:], d["h3"].rearrange("b p c e -> p b c e")).then_inc(consts_in, 16)
            with sp.Fori(0, HEADS) as h:
                sp.wait_ge(head_free, h + 1)
                sp.dma_start(score_w[:], d["score_w"][h]).then_inc(head_in, 16)
                sp.dma_start(wq[:], d["wqT"][h]).then_inc(head_in, 16)
                sp.dma_start(wo[:], d["wo"][h]).then_inc(head_in, 16)
                for j in range(2):
                    sp.dma_start(xT[:, j], d["x3T"][j]).then_inc(x_in[j], 16)
                for k in range(4):
                    sp.dma_start(table[:, k * 8:k * 8 + 8], d["table"][h][:, k * 8:k * 8 + 8])\
                        .then_inc(table_in[k], 16)
                with sp.Fori(0, NB // 2 - 1) as i:
                    for j in range(2):
                        sp.wait_ge(q_done, h * NB + i * 2 + (j + 1))
                        sp.dma_start(xT[:, j], d["x3T"][i * 2 + (2 + j)]).then_inc(x_in[j], 16)
            sp.wait_ge(added, HEADS * NB + 1)
            sp.dma_start(d["out"].rearrange("b (c p) e -> p b c e", p=CP), acc[:]).then_inc(stored, 16)
            sp.wait_ge(stored, 16)

        @block.tensor
        def _(pe):
            mm, tp = nc.tensor.matmul, nc.tensor.transpose
            for sem, n in ((cut_turned, 1), (kv_turned, 1), (kv_done, 3)):
                pe.sem_inc(sem, n)
            pe.wait_ge(consts_in, 64)
            pe.wait_ge(pick_ready, 2)

            def x_arrived(u, s, par):
                pe.wait_ge(x_in[par], u * 8 + (16 if par == 0 else 8))

            def a_scores(u, s, par):
                x_arrived(u, s, par)
                pe.wait_ge(Z_ready, u + 1)
                pe.sem_inc(held, 1)
                for c in range(CH):
                    last = mm(ps_a[0:CP, c * 128:(c + 1) * 128], xT[:, par, chunk(c)], score_w[:],
                              start=True, stop=True)
                last.then_inc(scored, 1)

            def a_turn(u, s, par):
                pe.wait_ge(cut_done, u + 1)
                pe.sem_inc(held, 1)
                for c in range(CH):
                    last = tp(ps_a[:, chunk(c)], S[:, c, :], ident[0:CP, 0:CP])
                last.then_inc(cut_turned, 1)

            def q(u, s, par):
                x_arrived(u, s, par)
                pe.wait_ge(added, u + 1)
                pe.sem_inc(held, 1)
                mm(ps_c[0:C, 0:TOK], wq[:], xT[:, par], start=True, stop=True).then_inc(q_done, 1)

            def b_sum(u, n, par):
                pe.wait_ge(wt_ready, before(u, n))
                mm(ps_z[n % 3][:, 0:TOK + 1], pick[:, n, :], Zh[:, par], start=True, stop=False)
                mm(ps_z[n % 3][:, 0:TOK + 1], pick[:, n, :], Zl[:, par], start=False, stop=True)\
                    .then_inc(z_done, 1)

            def b_product(u, n):
                pe.wait_ge(wt_ready, u * NT4 + (n + 4))
                mm(ps_kv[:, 0:TOK], table[:, n, :], wt[:, n % 3], start=n == 0, stop=n == NT4 - 1)\
                    .then_inc(kv_done, 1)

            def c_turn_kv(u):
                pe.wait_ge(kvT_ready, u + 2)
                pe.wait_ge(q_ready, u + 1)
                pe.sem_inc(held, 1)
                for c in range(CH):
                    last = tp(ps_c[0:CP, c * 128:(c + 1) * 128], kvT[:, chunk(c)], ident[:])
                last.then_inc(kv_turned, 1)

            def c_turn_k(u):
                pe.wait_ge(kv_ready, u + 1)
                pe.sem_inc(held, 1)
                for c in range(CH):
                    last = tp(ps_c[0:C, chunk(c)], kv[:, c, 0:C], ident[0:CP, 0:CP])
                last.then_inc(k_turned, 1)

            def c_scores(u, par):
                pe.wait_ge(kT_ready, u + 1)
                pe.wait_ge(PT_ready, u * 2 + 2)
                pe.sem_inc(held, 1)
                for c in range(CH):
                    last = mm(score_at[c], qT[:, par, chunk(c)], kT[:, 0:(c + 1) * CP], start=True, stop=True)
                last.then_inc(s_done, 1)

            def c_turn_p(u):
                pe.wait_ge(p_ready, u + 1)
                pe.sem_inc(held, 1)
                for jc in range(CH):
                    for c in range(jc, CH):
                        last = tp(turned_at(jc, c), pr[:, c, chunk(jc)], ident[0:CP, 0:CP])
                    if jc != 1:
                        last.then_inc(p_turned, 1)

            def c_attend(u):
                pe.wait_ge(PT_ready, u * 2 + 4)
                pe.sem_inc(held, 1)
                for jc, src in ((0, PT[:, 0, 0:TOK]), (1, PT[:, 1, 0:2 * CP]), (2, PT[:, 1, 2 * CP:TOK])):
                    last = mm(ps_c[0:C, jc * CP:TOK], kv[:, jc, C:128], src, start=jc == 0, stop=jc == CH - 1)
                last.then_inc(o_done, 1)

            def c_out(u):
                pe.wait_ge(oT_ready, u + 1)
                pe.sem_inc(held, 1)
                for c in range(CH):
                    last = mm(ps_c[0:CP, c * C:(c + 1) * C], oT[:, chunk(c)], wo[:], start=True, stop=True)
                last.then_inc(out_done, 1)

            def a(u, s, par):
                a_scores(u, s, par)
                a_turn(u, s, par)

            def body(u, s, par, with_a, with_c):
                pe.wait_ge(Z_ready, u + 2)
                pe.sem_inc(held, 1)
                b_sum(u, 0, par)
                b_sum(u, 1, par)
                for n in range(NT4):
                    if n + 2 < NT4:
                        b_sum(u, n + 2, par)
                    if n == 0:
                        pe.wait_ge(kvT_ready, u + 1)
                    if n % 8 == 0:
                        table_arrived(n // 8)
                    b_product(u, n)
                    if with_a and n == 0:
                        a_scores(u + 1, None, 1 - par)
                    if with_a and n == 25:
                        a_turn(u + 1, None, 1 - par)
                    if with_c and n == 1:
                        c_turn_kv(u - 1)
                    if with_c and n == 3:
                        c_turn_k(u - 1)
                    if with_c and n == 6:
                        c_scores(u - 1, 1 - par)
                    if with_c and n == 12:
                        c_turn_p(u - 1)
                    if with_c and n == 15:
                        c_attend(u - 1)
                    if with_c and n == 18:
                        c_out(u - 1)
                    if n == 21:
                        q(u, s, par)

            def c(u, s, par):
                c_turn_kv(u)
                c_turn_k(u)
                c_scores(u, par)
                c_turn_p(u)
                c_attend(u)
                c_out(u)

            head = []

            def table_arrived(k):
                pe.wait_ge(table_in[k], head[0] * 16 + 16)

            for h in units(pe, a, body, c):
                head[:] = [h]
                pe.wait_ge(head_in, h * 48 + 48)

        @block.scalar
        def _(act):
            run = nc.scalar.activation
            act.sem_inc(kvT_ready, 1)
            act.sem_inc(PT_ready, 2)
            act.wait_ge(pick_ready, 2)

            def a_copy(u):
                act.wait_ge(scored, u + 1)
                act.wait_ge(cut_turned, u + 1)
                run(S[:].rearrange("p c k -> p (c k)"), ps_a[0:CP, 0:CH * 128], ACT.Copy).then_inc(S_ready, 1)

            def a_terms(u):
                act.wait_ge(best_ready, u + 1)
                run(terms[:], terms[:], ACT.Exp, bias=lift[0:CP, 0:1]).then_inc(terms_ready, 1)

            def a_high(u, par):
                act.wait_ge(cut_turned, u + 2)
                run(Zh[:, par, 0:TOK], ps_a[:, 0:TOK], ACT.Copy).then_inc(high_ready, 1)

            def q(u, par):
                act.wait_ge(q_done, u + 1)
                run(qT[:, par], ps_c[0:C, 0:TOK], ACT.Copy, scale=C ** -0.5).then_inc(q_ready, 1)

            def b_exp(u, n):
                act.wait_ge(z_done, u * NT4 + (n + 1))
                act.wait_ge(wt_ready, before(u, n))
                run(ex[:, n % 3], ps_z[n % 3][:, 0:TOK], ACT.Exp, bias=lift[:, 0:1]).then_inc(ex_ready, 1)

            def c_copy_kvT(u):
                act.wait_ge(kv_done, u * NT4 + (NT4 + 3))
                act.wait_ge(kv_turned, u + 1)
                run(kvT[:], ps_kv[:, 0:TOK], ACT.Copy).then_inc(kvT_ready, 1)

            def c_copy_kT(u):
                act.wait_ge(k_turned, u + 1)
                run(kT[:], ps_c[0:C, 0:TOK], ACT.Copy).then_inc(kT_ready, 1)

            def c_exp(u):
                act.wait_ge(max_ready, u + 1)
                for c in range(CH):
                    last = run(pr[:, c, 0:(c + 1) * CP], score_at[c], ACT.Exp, bias=mx[:, c:c + 1],
                               accum_out=sm[:, c:c + 1])
                last.then_inc(e_ready, 1)

            def c_copy_PT(u):
                for k in range(2):
                    act.wait_ge(p_turned, u * 2 + (k + 1))
                    run(PT[:, k], ps_s[k][:, 0:TOK], ACT.Copy).then_inc(PT_ready, 1)

            def c_copy_oT(u):
                act.wait_ge(o_done, u + 1)
                run(oT[:], ps_c[0:C, 0:TOK], ACT.Copy).then_inc(oT_ready, 1)

            def a(u, s, par):
                a_copy(u)
                a_terms(u)
                a_high(u, par)

            def body(u, s, par, with_a, with_c):
                if with_c:
                    c_copy_kvT(u - 1)
                for n in range(NT4):
                    b_exp(u, n)
                    if with_a and n == 1:
                        a_copy(u + 1)
                    if with_c and n == 4:
                        c_copy_kT(u - 1)
                    if with_c and n == 9:
                        c_exp(u - 1)
                    if with_c and n == 13:
                        c_copy_PT(u - 1)
                    if with_c and n == 16:
                        c_copy_oT(u - 1)
                    if with_a and n == 22:
                        a_terms(u + 1)
                    if n == 23:
                        q(u, par)
                    if with_a and n == 27:
                        a_high(u + 1, 1 - par)

            def c(u, s, par):
                c_copy_kvT(u)
                c_copy_kT(u)
                c_exp(u)
                c_copy_PT(u)
                c_copy_oT(u)

            for _ in units(act, a, body, c):
                pass

        @block.vector
        def _(v):
            tt, ts, stt = nc.vector.tensor_tensor, nc.vector.tensor_scalar, nc.vector.scalar_tensor_tensor
            for sem, n in ((Z_ready, 1), (wt_ready, 3), (added, 1)):
                v.sem_inc(sem, n)
            nc.vector.memset(lift[:], -LIFT).then_inc(pick_ready, 1)
            for t in (Zh, Zl):
                last = nc.vector.memset(t[:].bitcast(F32), 0.0)
            last.then_inc(dve_a, 1)
            v.wait_ge(consts_in, 64)
            nc.vector.tensor_copy(pick[:], pick_in[:]).then_inc(pick_ready, 1)
            v.wait_ge(dve_a, 1)
            chains = {}
            NA, NC = 6 * 3 + 7 + 3 * 3 + 4 + 3 + 1, 3 + 3 + 3 + 1 + 1 + 3 + 1
            wide = lambda a, n: a.unsqueeze(2).broadcast_to((CP, CH, n))

            def a_lists(u, part):
                if part == 0:
                    v.wait_ge(S_ready, u + 1)
                    v.sem_inc(held, 1)
                    chains["a"] = Chain(v, dve_a, u, NA)
                    chains["a"].n = 1
                ch = chains["a"]
                for c in range(CH):
                    for p in range(2):
                        sc, li = S[:, c, p * NK:(p + 1) * NK], lists[:, c, p]
                        if part == 0:
                            ch.step(nc.vector.max(li[:, 0:8], sc))
                        elif part == 1:
                            ch.step(nc.vector.match_replace(rest[:, c, p], li[:, 0:8], sc, -3e38))
                        else:
                            ch.step(nc.vector.max(li[:, 8:16], rest[:, c, p]))
                ch.sync()
                v.sem_inc(held, 1)

            def a_sums(u):
                ch, at = chains["a"], 0
                for i, w in ROWS:
                    ch.step(tt(cand[:, :, at:at + w], lists[:, :, 0, i:i + 1].broadcast_to((CP, CH, w)),
                               lists[:, :, 1, 0:w], ALU.add))
                    at += w
                out = cand[:, :, at:at + 6].rearrange("p c (i w) -> p c i w", w=2)
                ch.step(tt(out, lists[:, :, 0, 5:8].unsqueeze(3).broadcast_to((CP, CH, 3, 2)),
                           lists[:, :, 1, 0:2].unsqueeze(2).broadcast_to((CP, CH, 3, 2)), ALU.add))
                ch.step(tt(cand[:, :, at + 6:at + 14], lists[:, :, 0, 8:16],
                           lists[:, :, 1, 0:1].broadcast_to((CP, CH, 8)), ALU.add))
                ch.sync()
                v.sem_inc(held, 1)

            def a_best(u, part):
                ch = chains["a"]
                for c in range(CH):
                    if part == 0:
                        ch.step(nc.vector.max(best[:, c, 0:8], cand[:, c]))
                    elif part == 1:
                        ch.step(nc.vector.match_replace(cand2[:, c], best[:, c, 0:8], cand[:, c], -3e38))
                    else:
                        ch.step(nc.vector.max(best[:, c, 8:16], cand2[:, c]))
                ch.sync()
                v.sem_inc(held, 1)

            def a_cut(u):
                ch = chains["a"]
                ends = lists[:, :, :, 0:TOPK:TOPK - 1]
                ch.link(nc.vector.tensor_reduce(size[:], ends, AX.XY, ALU.add, apply_absolute_value=True))
                ch.link(stt(cut[:], size[:], -SLACK, best[:, :, TOPK - 1], ALU.mult, ALU.add))
                ch.link(stt(cut[:], best[:, :, 0], -FLOOR, cut[:], ALU.add, ALU.max))
                ch.link(tt(terms[:], best[:], wide(cut[:], TOPK), ALU.subtract))
                v.sem_inc(best_ready, 1)

            def a_shift(u, par):
                ch = chains["a"]
                ch.step(tt(S[:, :, 0:NK], S[:, :, 0:NK], wide(cut[:], NK), ALU.subtract))
                v.wait_ge(terms_ready, u + 1)
                ch.link(nc.vector.tensor_reduce(size[:], terms[:], AX.X, ALU.add))
                v.sem_inc(cut_done, 1)
                ch.link(nc.vector.reciprocal(rZ[:, par], size[:]))

            def a_low(u, par):
                ch = chains["a"]
                v.wait_ge(high_ready, u + 1)
                ch.link(tt(Zl[:, par, 0:TOK], ps_a[:, 0:TOK], Zh[:, par, 0:TOK].bitcast(F32), ALU.subtract))
                ch.n -= 1
                ch.close()
                v.sem_inc(Z_ready, 1)

            def b_weights(u, n):
                v.wait_ge(ex_ready, u * NT4 + (n + 1))
                v.wait_ge(kv_done, before(u, n))
                stt(wt[:, n % 3], ps_z[n % 3][:, 0:TOK], 0.0, ex[:, n % 3], ALU.is_ge, ALU.mult)\
                    .then_inc(wt_ready, 1)

            def c_scale(u, par):
                v.wait_ge(kv_turned, u + 2)
                chains["c"] = ch = Chain(v, dve_c, u, NC)
                for c in range(CH):
                    ch.step(ts(kv[:, c, :], ps_c[0:CP, c * 128:(c + 1) * 128], rZ[:, par, c:c + 1], None, ALU.mult))
                ch.sync()
                v.sem_inc(kv_ready, 1)

            def c_max(u):
                ch = chains["c"]
                v.wait_ge(s_done, u + 1)
                for c in range(CH):
                    ch.step(tt(diag_at[c], diag_at[c], tri[:], ALU.add))
                ch.sync()
                for c in range(CH):
                    ch.step(nc.vector.tensor_reduce(mx[:, c:c + 1], score_at[c], AX.X, ALU.max))
                ch.sync()
                ch.link(ts(mx[:], mx[:], -1.0, None, ALU.mult))
                v.sem_inc(max_ready, 1)

            def c_norm(u):
                ch = chains["c"]
                v.wait_ge(e_ready, u + 1)
                ch.link(nc.vector.reciprocal(sm[:], sm[:]))
                for c in range(CH):
                    w = (c + 1) * CP
                    ch.step(ts(pr[:, c, 0:w], pr[:, c, 0:w], sm[:, c:c + 1], None, ALU.mult))
                ch.sync()
                v.sem_inc(p_ready, 1)

            def c_add(u, s):
                ch = chains["c"]
                v.wait_ge(out_done, u + 1)
                at = acc[:, s]
                ch.link(tt(at, at, ps_c[0:CP, 0:CH * C].rearrange("p (c e) -> p c e", c=CH), ALU.add))
                ch.close()
                v.sem_inc(added, 1)

            def a(u, s, par):
                for part in range(3):
                    a_lists(u, part)
                a_sums(u)
                for part in range(3):
                    a_best(u, part)
                a_cut(u)
                a_shift(u, par)
                a_low(u, par)

            def body(u, s, par, with_a, with_c):
                for n in range(NT4):
                    b_weights(u, n)
                    if with_c and n == 2:
                        c_scale(u - 1, 1 - par)
                    if with_a and n in (3, 5, 8):
                        a_lists(u + 1, (3, 5, 8).index(n))
                    if with_c and n == 7:
                        c_max(u - 1)
                    if with_c and n == 11:
                        c_norm(u - 1)
                    if with_a and n == 14:
                        a_sums(u + 1)
                    if with_a and n in (16, 17, 18):
                        a_best(u + 1, n - 16)
                    if with_c and n == 19:
                        c_add(u - 1, s - 1)
                    if with_a and n == 21:
                        a_cut(u + 1)
                    if with_a and n == 23:
                        a_shift(u + 1, 1 - par)
                    if with_a and n == 28:
                        a_low(u + 1, 1 - par)

            def c(u, s, par):
                c_scale(u, par)
                c_max(u)
                c_norm(u)
                c_add(u, s)
                v.sem_inc(head_free, 1)

            v.sem_inc(head_free, 1)
            for _ in units(v, a, body, c):
                pass


SCRATCH = {
    "h0": (NB, CP, CH, C), "xn": (NB, CP, CH, C), "xnT": (NB, C, TOK),
    "krev": (C, TOK + CP), "conv": (NB, C, TOK),
    "h1": (NB, CP, CH, C), "x1T": (NB, C, TOK),
    "h2": (NB, CP, CH, C), "x2": (NB, CP, CH, C), "x2T": (NB, C, TOK),
    "h3": (NB, CP, CH, C), "x3T": (NB, C, TOK), "score_w": (HEADS, C, 2 * NK),
}


def program(nc, d):
    for name, shape in SCRATCH.items():
        d[name] = nc.dram_tensor(name, shape, F32, kind="Internal").ap()
    with ExitStack() as Mem.program:
        for stage in (stage_tokens, stage_ssm_kernel, stage_conv, stage_mix, stage_experts, stage_pairs,
                      stage_keys, stage_memory)[:STAGE]:
            stage(nc, d)


def lay_out(np, a):
    con = np.concatenate
    n = {k: np.asarray(v) for k, v in a.items()}
    p = n["x"].reshape(NB, 3, 14, 16, 14, 16).transpose(0, 1, 3, 5, 2, 4).reshape(NB, KT, 128, NIMG)
    two = lambda v: con([v, v])
    re_im = lambda k: con([n[k + "_re"], n[k + "_im"]])
    im_re = lambda k: con([n[k + "_im"], n[k + "_re"]])
    sign = con([np.ones(C), -np.ones(C)]).astype(np.float32)
    A = "L0_attn_"
    par = np.stack([two(n[A + "Lambda_re"]), two(n[A + "Lambda_im"]), re_im(A + "B"), im_re(A + "B"),
                    re_im(A + "P"), im_re(A + "P"), np.broadcast_to(n[A + "step"], (128,)), sign], 1)
    cq = np.stack([con([n[A + "C_" + z].T, n[A + "Q_" + z][:, None]], 1) for z in ("re", "im")], 1)
    l = np.arange(TOK)
    tan = np.tan(np.pi * l / TOK)
    lag = TOK - 1 - l
    ang = 2 * np.pi * ((l[:, None] * lag[None, :]) % TOK) / TOK
    dft = np.stack([np.cos(ang) / TOK, -np.sin(ang) / TOK], 1).reshape(CH, CP, 2, TOK).transpose(1, 0, 2, 3)
    out = {
        "patches": p.transpose(0, 2, 1, 3),
        "txtT": n["txt"].transpose(0, 2, 1),
        "tokW": n["L0_tok_W"].T.reshape(KT, 128, C).transpose(1, 0, 2),
        "tokb": n["L0_tok_b"][:, None],
        "ident": np.eye(128, dtype=np.float32),
        "par": par,
        "cq": con([cq, cq]),
        "tanr": np.broadcast_to(tan.astype(np.float32), (128, TOK)),
        "tanc": tan.astype(np.float32).reshape(CH, CP).T,
        "dft": dft.astype(np.float32),
    }
    row = lambda v: np.broadcast_to(v, (CP, CH, C))
    out["fcT"] = n[A + "W_fc"].T
    out["skipD"] = np.broadcast_to(n[A + "D"], (C, 1))
    out["mix_rows"] = np.stack([row(n[A + k]) for k in ("b_fc", "ln_g", "ln_b")], 1)
    F = "L0_ffn_"
    pad = ((0, 0), (0, NT * HT - HID), (0, 0))
    w1, w3 = (np.pad(n[F + k], pad).transpose(2, 0, 1) for k in ("w1", "w3"))
    out["routerT"] = n[F + "router_w"].T
    out["w13"] = con([w1, w3])
    out["w2"] = np.pad(n[F + "w2"].transpose(0, 2, 1), pad).reshape(E, NT, HT, C).transpose(2, 0, 1, 3)
    out["pick"] = (np.arange(E)[:, None, None] == 2 * np.arange(E // 2)[:, None] + np.arange(128) // C).astype(np.float32)
    P = "L1_attn_"
    wi = n[P + "w_itr_att"]
    mix = np.zeros((C + 1, C + 1), np.float32)
    mix[:C, C] = wi[:C]
    mix[C, :C] = wi[C:2 * C]
    mix[np.arange(C), np.arange(C)] = wi[2 * C:]
    out["pair_mix"] = mix
    w = con([n[P + k] for k in ("w1", "w2", "w3")], 1)
    bias = con([n[P + k] for k in ("b1", "b2", "b3")])
    out["pair_top"] = con([w[:C], bias[None]])
    out["pair_bot"] = w[C:]
    M = "L1_ffn_"
    out["wq_pk"] = n[M + "Wq_pk"].reshape(C, 2, HEADS, DK).transpose(3, 1, 2, 0)
    out["pk_keys"] = n[M + "pk_keys"].transpose(3, 0, 2, 1)
    out["wqT"] = n[M + "Wq"].reshape(C, HEADS, C).transpose(1, 0, 2)
    out["wo"] = n[M + "Wo"].reshape(HEADS, C, C)
    tables = con([n[M + "keys_table"], n[M + "values_table"]], 1)
    out["table"] = tables.reshape(HEADS, NT4, 128, 2 * C).transpose(0, 2, 1, 3)
    row, sl, col = np.ogrid[0:128, 0:NT4, 0:128]
    out["key_pick"] = np.where(row < NK, row == col % NK, row - NK == 2 * sl + col // NK).astype(np.float32)
    out["tri"] = np.where(np.arange(CP)[None, :] > np.arange(CP)[:, None], np.float32(HIDDEN), np.float32(0))
    return {k: np.ascontiguousarray(v) for k, v in out.items()}


def kernel(**inputs):
    import numpy as np
    import concourse.bacc as bacc
    from concourse import mybir as mb
    from concourse.bass_utils import run_bass_kernel_spmd as run

    nc = bacc.Bacc("TRN2", target_bir_lowering=False, num_devices=1)
    arrays = {"in_" + k: v for k, v in lay_out(np, inputs).items()}
    d = {k[3:]: nc.dram_tensor(k, v.shape, mb.dt.from_np(v.dtype), kind="ExternalInput").ap()
         for k, v in arrays.items()}
    d["out"] = nc.dram_tensor("out", (NB, TOK, C), mb.dt.float32, kind="ExternalOutput").ap()
    program(nc, d)
    r = run(nc, [arrays], core_ids=[0])
    return r.results[0]["out"]
```

```python
from contextlib import ExitStack

import concourse.bass as bass
from concourse import mybir
from concourse.alu_op_type import AluOpType as ALU

F32 = mybir.dt.float32
F32R = mybir.dt.float32r
ACT = mybir.ActivationFunctionType
AX = mybir.AxisListType

NB = 32
C = 64
NIMG = 196
TOK = 273
NTXT = TOK - NIMG
CP = 91
CH = 3
KT = 6
LN_EPS = 1e-5
STAGE = 8


class Mem:
    program = None

    def __init__(self, nc, stage):
        self.nc, self.stage, self.ctx, self.sems = nc, stage, ExitStack(), []

    def __enter__(self):
        return self

    def __exit__(self, *a):
        done = self.ctx.__exit__(*a)
        self.nc.clear_and_free_semaphores(self.sems)
        self.nc.all_engine_barrier()
        return done

    def sb(self, name, shape, dt=F32):
        return self.ctx.enter_context(self.nc.sbuf_tensor(f"{self.stage}_{name}", shape, dt))

    def ps(self, name, shape, dt=F32):
        return self.ctx.enter_context(self.nc.psum_tensor(f"{self.stage}_{name}", shape, dt))

    def sem(self, name):
        self.sems.append(self.nc.alloc_semaphore(name=f"{self.stage}_{name}"))
        return self.sems[-1]

    def pool_dma_sem(self, name):
        return self.program.enter_context(self.nc.semaphore(f"{self.stage}_{name}"))

    def block(self):
        return self.ctx.enter_context(self.nc.Block())


class Chain:

    def __init__(self, eng, sem, i=0, per=0):
        self.eng, self.sem, self.i, self.per, self.n = eng, sem, i, per, 0

    def step(self, ins):
        self.n += 1
        ins.then_inc(self.sem, 1)

    def sync(self):
        self.eng.wait_ge(self.sem, self.i * self.per + self.n)

    def link(self, ins):
        self.step(ins)
        self.sync()

    def close(self):
        assert self.n == self.per, (self.n, self.per)


class Norm:
    STEPS = 11

    def __init__(self, nc, m, held, name="norm"):
        self.nc, self.held = nc, held
        self.stats = m.sb(f"{name}_stats", [CP, 2, CH, 6])
        self.mv = m.sb(f"{name}_mv", [CP, 2, CH, 2])
        self.var_ready = m.sem(f"{name}_var_ready")
        self.root_ready = m.sem(f"{name}_root_ready")

    def vector(self, ch, x, out, j, s):
        nc, stats, mv = self.nc, self.stats[:, j], self.mv[:, j]
        for c in range(CH):
            ch.step(nc.vector.bn_stats(stats[:, c, :], x[:, c, :]))
        ch.sync()
        ch.eng.sem_inc(self.held, 1)
        for c in range(CH):
            ch.step(nc.vector.bn_aggr(mv[:, c, :], stats[:, c, :]))
        ch.sync()
        ch.link(nc.vector.tensor_scalar(mv[:, :, 1], mv[:, :, 1], LN_EPS, None, ALU.add))
        ch.eng.sem_inc(self.var_ready, 1)
        ch.eng.wait_ge(self.root_ready, s + 1)
        ch.link(nc.vector.reciprocal(mv[:, :, 1], mv[:, :, 1]))
        for c in range(CH):
            ch.step(nc.vector.tensor_scalar(out[:, c, :], x[:, c, :], mv[:, c, 0:1], mv[:, c, 1:2],
                                            ALU.subtract, ALU.mult))
        ch.sync()

    def scalar(self, act, j, s):
        act.wait_ge(self.var_ready, s + 1)
        sd = self.mv[:, j, :, 1]
        self.nc.scalar.activation(sd, sd, ACT.Sqrt).then_inc(self.root_ready, 1)


def stage_tokens(nc, d):
    with Mem(nc, "tok") as m:
        xp = m.sb("patches", [128, 2, KT, NIMG])
        hT = m.sb("hT", [C, 2, TOK])
        w = m.sb("w", [128, KT, C])
        b = m.sb("b", [C, 1])
        ident = m.sb("ident", [128, 128])
        h = m.sb("h", [CP, 2, CH, C])
        xn = m.sb("xn", [CP, 2, CH, C])
        xT = m.sb("xT", [C, 2, TOK])
        ps_h = [m.ps(f"ps_h{j}", [C, 512]) for j in range(2)]
        ps_t = [m.ps(f"ps_t{j}", [CP, CH, C]) for j in range(2)]
        ps_x = [m.ps(f"ps_x{j}", [C, 512]) for j in range(2)]
        held = m.sem("held")
        weights_in = m.sem("weights_in")
        pixels_in = [m.sem(f"pixels_in{j}") for j in range(2)]
        text_in = [m.sem(f"text_in{j}") for j in range(2)]
        embedded = m.sem("embedded")
        hT_ready = m.sem("hT_ready")
        h_turned = m.sem("h_turned")
        h_ready = m.sem("h_ready")
        normed = m.sem("normed")
        x_turned = m.sem("x_turned")
        xT_ready = m.sem("xT_ready")
        stored = [m.pool_dma_sem(f"stored{j}") for j in range(2)]
        out_free = m.sem("out_free")
        dve = m.sem("dve")
        norm = Norm(nc, m, held)
        block = m.block()

        @block.sync
        def _(sp):
            sp.dma_start(w[:], d["tokW"]).then_inc(weights_in, 16)
            sp.dma_start(b[:], d["tokb"]).then_inc(weights_in, 16)
            sp.dma_start(ident[:], d["ident"]).then_inc(weights_in, 16)
            with sp.Fori(0, NB // 2) as i:
                for j in range(2):
                    s = i * 2 + j
                    sp.wait_ge(h_turned, s + 1)
                    sp.dma_start(xp[:, j], d["patches"][s]).then_inc(pixels_in[j], 16)
                    sp.dma_start(hT[:, j, NIMG:TOK], d["txtT"][s]).then_inc(text_in[j], 16)

        @block.tensor
        def _(pe):
            pe.sem_inc(h_turned, 2)
            pe.sem_inc(x_turned, 2)
            pe.wait_ge(weights_in, 48)
            with pe.Fori(0, NB // 2) as i:
                for j in range(2):
                    pe.wait_ge(pixels_in[j], i * 16 + 16)
                    pe.wait_ge(hT_ready, i * 2 + j + 1)
                    for k in range(KT):
                        last = nc.tensor.matmul(ps_h[j][:, 0:NIMG], w[:, k, :], xp[:, j, k, :],
                                                start=k == 0, stop=k == KT - 1)
                    last.then_inc(embedded, 1)
                for j in range(2):
                    pe.wait_ge(hT_ready, i * 2 + j + 3)
                    pe.wait_ge(text_in[j], i * 16 + 16)
                    pe.wait_ge(h_ready, i * 2 + j + 1)
                    pe.sem_inc(held, 1)
                    for c in range(CH):
                        last = nc.tensor.transpose(ps_t[j][:, c, :], hT[:, j, c * CP:(c + 1) * CP],
                                                   ident[0:C, 0:C])
                    last.then_inc(h_turned, 1)
                for j in range(2):
                    pe.wait_ge(normed, i * 2 + j + 1)
                    pe.wait_ge(xT_ready, i * 2 + j + 1)
                    pe.sem_inc(held, 1)
                    for c in range(CH):
                        last = nc.tensor.transpose(ps_x[j][:, c * CP:(c + 1) * CP], xn[:, j, c, :],
                                                   ident[0:CP, 0:CP])
                    last.then_inc(x_turned, 1)

        @block.scalar
        def _(act):
            act.sem_inc(hT_ready, 2)
            act.sem_inc(h_ready, 2)
            act.sem_inc(xT_ready, 2)
            act.wait_ge(weights_in, 48)
            with act.Fori(0, NB // 2) as i:
                for j in range(2):
                    act.wait_ge(embedded, i * 2 + j + 1)
                    act.wait_ge(h_turned, i * 2 + j + 1)
                    nc.scalar.activation(hT[:, j, 0:NIMG], ps_h[j][:, 0:NIMG], ACT.Identity,
                                         bias=b[:, 0:1]).then_inc(hT_ready, 1)
                for j in range(2):
                    act.wait_ge(h_turned, i * 2 + j + 3)
                    act.wait_ge(out_free, i * 2 + j + 1)
                    nc.scalar.activation(h[:, j], ps_t[j][:], ACT.Copy).then_inc(h_ready, 1)
                for j in range(2):
                    norm.scalar(act, j, i * 2 + j)
                for j in range(2):
                    act.wait_ge(x_turned, i * 2 + j + 3)
                    nc.scalar.activation(xT[:, j], ps_x[j][:, 0:TOK], ACT.Copy).then_inc(xT_ready, 1)

        @block.vector
        def _(v):
            with v.Fori(0, NB // 2) as i:
                ch = Chain(v, dve, i, 2 * Norm.STEPS)
                for j in range(2):
                    v.wait_ge(h_ready, i * 2 + j + 3)
                    v.wait_ge(out_free, i * 2 + j + 1)
                    v.wait_ge(x_turned, i * 2 + j + 1)
                    norm.vector(ch, h[:, j], xn[:, j], j, i * 2 + j)
                    v.sem_inc(normed, 1)
                ch.close()

        @block.gpsimd
        def _(g):
            g.sem_inc(out_free, 2)
            with g.Fori(0, NB // 2) as i:
                for j in range(2):
                    s = i * 2 + j
                    g.wait_ge(h_ready, s + 3)
                    g.wait_ge(normed, s + 1)
                    g.sem_inc(held, 1)
                    g.dma_start(d["h0"][s], h[:, j]).then_inc(stored[j], 16)
                    g.dma_start(d["xn"][s], xn[:, j]).then_inc(stored[j], 16)
                    g.wait_ge(xT_ready, s + 3)
                    g.sem_inc(held, 1)
                    g.dma_start(d["xnT"][s], xT[:, j]).then_inc(stored[j], 16)
                for j in range(2):
                    g.wait_ge(stored[j], i * 48 + 48)
                    g.sem_inc(out_free, 1)


def stage_ssm_kernel(nc, d):
    with Mem(nc, "ssm") as m:
        par = m.sb("par", [128, 8])
        cq = m.sb("cq", [128, 2, C + 1])
        tanr = m.sb("tanr", [128, TOK])
        tanc = m.sb("tanc", [CP, CH])
        dft = m.sb("dft", [CP, CH, 2, TOK])
        g2 = m.sb("g2", [128, 6])
        den = m.sb("den", [128, TOK])
        q = m.sb("q", [128, TOK])
        V = m.sb("V", [128, TOK])
        dim = m.sb("dim", [128, TOK])
        R = m.sb("R", [128, 2, 2, C + 1])
        kk = m.sb("kk", [CP, CH, 2, 2, C + 1])
        w = m.sb("w", [CP, CH, 12])
        y = m.sb("y", [CP, CH, 2, C])
        at = m.sb("at", [CP, CH, 2, C])
        kr = m.sb("kr", [C, TOK + CP])
        ps = [m.ps(f"ps{c}", [CP, 512]) for c in range(CH)]
        psk = m.ps("psk", [C, 512])
        loaded, sums, turned, done, stored, dve = (m.sem(n) for n in
                                                   ("loaded", "sums", "turned", "done", "stored", "dve"))
        made = m.sem("made")
        spectrum = m.sem("spectrum")
        block = m.block()

        @block.sync
        def _(sp):
            for t, n in ((par, "par"), (cq, "cq"), (tanr, "tanr"), (tanc, "tanc"), (dft, "dft")):
                sp.dma_start(t[:], d[n]).then_inc(loaded, 16)
            sp.wait_ge(done, 1)
            sp.dma_start(d["krev"], kr[:]).then_inc(stored, 16)
            sp.wait_ge(stored, 16)

        @block.vector
        def _(v):
            ch = Chain(v, dve)
            tt, ts, stt = nc.vector.tensor_tensor, nc.vector.tensor_scalar, nc.vector.scalar_tensor_tensor
            v.wait_ge(loaded, 80)
            ch.step(nc.vector.memset(kr[:], 0.0))
            ch.link(ts(g2[:, 0:1], par[:, 6:7], 1e-6, None, ALU.max))
            ch.link(nc.vector.reciprocal(g2[:, 1:2], g2[:, 0:1]))
            ch.link(ts(g2[:, 1:2], g2[:, 1:2], 2.0, None, ALU.mult))
            ch.link(ts(dim[:], tanr[:], g2[:, 1:2], par[:, 1:2], ALU.mult, ALU.subtract))
            ch.link(tt(g2[:, 2:3], par[:, 0:1], par[:, 0:1], ALU.mult))
            ch.link(tt(den[:], dim[:], dim[:], ALU.mult))
            ch.link(ts(den[:], den[:], g2[:, 2:3], None, ALU.add))
            ch.link(nc.vector.reciprocal(den[:], den[:]))
            ch.step(ts(q[0:C, :], dim[0:C, :], 0.0, par[0:C, 0:1], ALU.mult, ALU.add))
            ch.step(nc.vector.tensor_copy(q[C:128, :], dim[C:128, :]))
            ch.sync()
            ch.link(stt(V[:], q[:], -1.0, den[:], ALU.mult, ALU.mult))
            for z in range(2):
                a, b = par[:, 2 + 2 * z:3 + 2 * z], par[:, 3 + 2 * z:4 + 2 * z]
                ch.link(tt(g2[:, 3:4], a, par[:, 7:8], ALU.mult))
                ch.step(ts(R[:, z, 0, :], cq[:, 0, :], g2[:, 3:4], None, ALU.mult))
                ch.step(ts(R[:, z, 1, :], cq[:, 0, :], b, None, ALU.mult))
                ch.step(ts(q[:, 0:C + 1], cq[:, 1, :], b, None, ALU.mult))
                ch.sync()
                ch.link(tt(R[:, z, 0, :], R[:, z, 0, :], q[:, 0:C + 1], ALU.subtract))
                ch.link(stt(R[:, z, 1, :], cq[:, 1, :], g2[:, 3:4], R[:, z, 1, :], ALU.mult, ALU.add))
            v.sem_inc(made, 1)
            v.wait_ge(sums, 1)
            for c in range(CH):
                ch.link(nc.vector.tensor_copy(kk[:, c].rearrange("p a b c -> p (a b c)"),
                                              ps[c][:, 0:4 * (C + 1)]))
            k10r, k10i = kk[:, :, 0, 0, C], kk[:, :, 0, 1, C]
            k11r, k11i = kk[:, :, 1, 0, C], kk[:, :, 1, 1, C]
            W = [w[:, :, n] for n in range(12)]
            ch.link(ts(W[0], k11r, 1.0, None, ALU.add))
            ch.step(tt(W[1], W[0], W[0], ALU.mult))
            ch.step(tt(W[2], k11i, k11i, ALU.mult))
            ch.sync()
            ch.link(tt(W[1], W[1], W[2], ALU.add))
            ch.step(nc.vector.reciprocal(W[3], W[1]))
            ch.step(tt(W[4], k10r, W[0], ALU.mult))
            ch.step(tt(W[5], k10i, k11i, ALU.mult))
            ch.step(tt(W[6], k10i, W[0], ALU.mult))
            ch.step(tt(W[7], k10r, k11i, ALU.mult))
            ch.sync()
            ch.step(tt(W[4], W[4], W[5], ALU.add))
            ch.step(tt(W[6], W[6], W[7], ALU.subtract))
            ch.sync()
            ch.step(tt(W[8], W[4], W[3], ALU.mult))
            ch.step(tt(W[9], W[6], W[3], ALU.mult))
            ch.sync()
            ch.step(ts(W[10], W[8], -1.0, None, ALU.mult))
            ch.step(ts(W[11], W[9], -1.0, None, ALU.mult))
            ch.sync()
            for c in range(CH):
                col = lambda n: w[:, c, n:n + 1]
                k01r, k01i = kk[:, c, 1, 0, 0:C], kk[:, c, 1, 1, 0:C]
                ch.step(stt(y[:, c, 0], k01r, col(10), kk[:, c, 0, 0, 0:C], ALU.mult, ALU.add))
                ch.step(stt(y[:, c, 1], k01r, col(11), kk[:, c, 0, 1, 0:C], ALU.mult, ALU.add))
                ch.sync()
                ch.step(stt(y[:, c, 0], k01i, col(9), y[:, c, 0], ALU.mult, ALU.add))
                ch.step(stt(y[:, c, 1], k01i, col(10), y[:, c, 1], ALU.mult, ALU.add))
                ch.sync()
                ch.link(ts(w[:, c, 0:1], tanc[:, c:c + 1], -1.0, None, ALU.mult))
                ch.step(stt(at[:, c, 0], y[:, c, 1], w[:, c, 0:1], y[:, c, 0], ALU.mult, ALU.add))
                ch.step(stt(at[:, c, 1], y[:, c, 0], tanc[:, c:c + 1], y[:, c, 1], ALU.mult, ALU.add))
                ch.sync()
            v.sem_inc(spectrum, 1)
            v.wait_ge(turned, 1)
            ch.link(nc.vector.tensor_copy(kr[:, 0:TOK], psk[:, 0:TOK]))
            v.sem_inc(done, 1)

        @block.tensor
        def _(pe):
            pe.wait_ge(made, 1)
            for c in range(CH):
                last = nc.tensor.matmul(ps[c][:, 0:4 * (C + 1)], V[:, c * CP:(c + 1) * CP],
                                        R[:].rearrange("p a b c -> p (a b c)"), start=True, stop=True)
            last.then_inc(sums, 1)
            pe.wait_ge(spectrum, 1)
            for c in range(CH):
                for z in range(2):
                    last = nc.tensor.matmul(psk[:, 0:TOK], at[:, c, z], dft[:, c, z],
                                            start=(c, z) == (0, 0), stop=(c, z) == (CH - 1, 1))
            last.then_inc(turned, 1)


def stage_conv(nc, d):
    with Mem(nc, "conv") as m:
        G = 8
        NG = C // G
        x = m.sb("x", [CP, NB, CH, C])
        toep = m.sb("toep", [CP, C, TOK])
        y = m.sb("y", [NB, 2, G, TOK])
        ps = [m.ps(f"ps{j}", [NB, 512]) for j in range(8)]
        x_in = m.sem("x_in")
        toep_in = [m.sem(f"toep_in{g}") for g in range(NG)]
        summed, taken, stored = m.sem("summed"), m.sem("taken"), [m.pool_dma_sem(f"stored{j}") for j in range(2)]
        block = m.block()
        krev = d["krev"]

        @block.sync
        def _(sp):
            sp.dma_start(x[:], d["xn"].rearrange("b p c e -> p b c e")).then_inc(x_in, 16)
            for g in range(NG):
                src = krev[g * G:(g + 1) * G, 0:TOK]
                src = bass.AP(tensor=src.tensor, offset=src.offset,
                              ap=[[1, CP], [TOK + CP, G], [1, TOK]])
                sp.dma_start(toep[:, g * G:(g + 1) * G, :], src).then_inc(toep_in[g], 16)

        @block.tensor
        def _(pe):
            pe.wait_ge(x_in, 16)
            for h in range(C):
                if h % G == 0:
                    pe.wait_ge(toep_in[h // G], 16)
                if h >= 8:
                    pe.wait_ge(taken, h - 7)
                for c in range(CH):
                    last = nc.tensor.matmul(ps[h % 8][:, 0:TOK - c * CP], x[:, :, c, h],
                                            toep[:, h, c * CP:TOK], start=c == 0, stop=c == CH - 1)
                last.then_inc(summed, 1)

        @block.scalar
        def _(act):
            for h in range(C):
                g, k = h // G, h % G
                act.wait_ge(summed, h + 1)
                if k == 0 and g >= 2:
                    act.wait_ge(stored[g % 2], g // 2 * 16)
                nc.scalar.activation(y[:, g % 2, k, :], ps[h % 8][:, 0:TOK][:, ::-1], ACT.Copy).then_inc(taken, 1)

        @block.gpsimd
        def _(g_):
            for g in range(NG):
                g_.wait_ge(taken, (g + 1) * G)
                g_.dma_start(d["conv"][:, g * G:(g + 1) * G, :], y[:, g % 2]).then_inc(stored[g % 2], 16)
            for j in range(2):
                g_.wait_ge(stored[j], NG // 2 * 16)


class Tail:

    def __init__(self, nc, m, d, held, ident, names):
        self.nc, self.d, self.held, self.ident, self.names = nc, d, held, ident, names
        self.h = m.sb("new_h", [CP, 2, CH, C])
        self.x = m.sb("new_x", [CP, 2, CH, C])
        self.xT = m.sb("new_xT", [C, 2, TOK])
        self.ps = m.ps("ps_new_xT", [C, 512])
        self.h_ready = m.sem("new_h_ready")
        self.normed = m.sem("normed")
        self.x_turned = m.sem("x_turned")
        self.xT_ready = m.sem("xT_ready")
        self.stored = [m.pool_dma_sem(f"stored{j}") for j in range(2)]
        self.out_free = m.sem("out_free")
        self.norm = Norm(nc, m, held)

    def vector_begin(self, v, s):
        v.wait_ge(self.out_free, s + 1)
        v.wait_ge(self.x_turned, s + 1)

    def vector(self, ch, j, s):
        ch.eng.sem_inc(self.h_ready, 1)
        self.norm.vector(ch, self.h[:, j], self.x[:, j], j, s)
        ch.eng.sem_inc(self.normed, 1)

    def tensor_start(self, pe):
        pe.sem_inc(self.x_turned, 2)

    def tensor(self, pe, j, s):
        pe.wait_ge(self.normed, s + 1)
        pe.wait_ge(self.xT_ready, s + 1)
        pe.sem_inc(self.held, 1)
        for c in range(CH):
            last = self.nc.tensor.transpose(self.ps[:, c * CP:(c + 1) * CP], self.x[:, j, c, :],
                                            self.ident[0:CP, 0:CP])
        last.then_inc(self.x_turned, 1)

    def scalar_start(self, act):
        act.sem_inc(self.xT_ready, 1)

    def scalar(self, act, j, s):
        act.wait_ge(self.x_turned, s + 3)
        act.wait_ge(self.out_free, s + 1)
        self.nc.scalar.activation(self.xT[:, j], self.ps[:, 0:TOK], ACT.Copy).then_inc(self.xT_ready, 1)

    def gpsimd(self, g):
        hn, xn, xTn = self.names
        g.sem_inc(self.out_free, 2)
        kinds = 3 if xn else 2
        with g.Fori(0, NB // 2) as i:
            for j in range(2):
                s = i * 2 + j
                g.wait_ge(self.normed, s + 1)
                g.sem_inc(self.held, 1)
                g.dma_start(self.d[hn][s], self.h[:, j]).then_inc(self.stored[j], 16)
                if xn:
                    g.dma_start(self.d[xn][s], self.x[:, j]).then_inc(self.stored[j], 16)
                g.wait_ge(self.xT_ready, s + 2)
                g.sem_inc(self.held, 1)
                g.dma_start(self.d[xTn][s], self.xT[:, j]).then_inc(self.stored[j], 16)
            for j in range(2):
                g.wait_ge(self.stored[j], i * (16 * kinds) + 16 * kinds)
                g.sem_inc(self.out_free, 1)


def stage_mix(nc, d):
    with Mem(nc, "mix") as m:
        ident = m.sb("ident", [128, 128])
        w = m.sb("w", [C, C])
        D = m.sb("D", [C, 1])
        rows = m.sb("rows", [CP, 3, CH, C])
        hin = m.sb("hin", [CP, 2, CH, C])
        xin = m.sb("xin", [CP, 2, CH, C])
        xT = m.sb("xT", [C, 2, TOK])
        cv = m.sb("cv", [C, 2, TOK])
        u = m.sb("u", [C, 2, TOK])
        y1 = m.sb("y1", [C, 2, TOK])
        t = m.sb("t", [CP, 2, CH, C])
        g_ = m.sb("g", [CP, 2, CH, C])
        y2 = m.sb("y2", [CP, 2, CH, C])
        ps = [m.ps(f"ps_fc{j}", [CP, CH, C]) for j in range(2)]
        held = m.sem("held")
        weights_in = m.sem("weights_in")
        loaded = [m.sem(f"loaded{j}") for j in range(2)]
        taken = m.sem("taken")
        u_ready, y1_ready, fc_done, t_ready, g_ready = (m.sem(n) for n in (
            "u_ready", "y1_ready", "fc_done", "t_ready", "g_ready"))
        dve = m.sem("dve")
        tail = Tail(nc, m, d, held, ident, ("h1", None, "x1T"))
        inner = Norm(nc, m, held, "inner")
        block = m.block()

        @block.sync
        def _(sp):
            for a, n in ((ident, "ident"), (w, "fcT"), (D, "skipD"), (rows, "mix_rows")):
                sp.dma_start(a[:], d[n]).then_inc(weights_in, 16)
            with sp.Fori(0, NB // 2) as i:
                for j in range(2):
                    s = i * 2 + j
                    sp.wait_ge(taken, s + 1)
                    sp.dma_start(hin[:, j], d["h0"][s]).then_inc(loaded[j], 16)
                    sp.dma_start(xin[:, j], d["xn"][s]).then_inc(loaded[j], 16)
                    sp.dma_start(xT[:, j], d["xnT"][s]).then_inc(loaded[j], 16)
                    sp.dma_start(cv[:, j], d["conv"][s]).then_inc(loaded[j], 16)

        @block.vector
        def _(v):
            v.sem_inc(taken, 2)
            v.wait_ge(weights_in, 64)
            with v.Fori(0, NB // 2) as i:
                ch = Chain(v, dve, i, 2 * (2 + 1 + 2 * Norm.STEPS + 3))
                for j in range(2):
                    v.wait_ge(loaded[j], i * 64 + 64)
                    v.wait_ge(y1_ready, i * 2 + j + 1)
                    ch.link(nc.vector.scalar_tensor_tensor(u[:, j], xT[:, j], D[:, 0:1], cv[:, j],
                                                           ALU.mult, ALU.add))
                    v.sem_inc(u_ready, 1)
                for j in range(2):
                    v.wait_ge(fc_done, i * 2 + j + 1)
                    v.wait_ge(g_ready, i * 2 + j + 1)
                    ch.link(nc.vector.tensor_tensor(t[:, j], ps[j][:], rows[:, 0], ALU.add))
                    v.sem_inc(t_ready, 1)
                for j in range(2):
                    v.wait_ge(g_ready, i * 2 + j + 3)
                    ch.link(nc.vector.tensor_tensor(y2[:, j], g_[:, j], xin[:, j], ALU.add))
                    inner.vector(ch, y2[:, j], y2[:, j], j, i * 2 + j)
                    tail.vector_begin(v, i * 2 + j)
                    ch.link(nc.vector.tensor_tensor(y2[:, j], y2[:, j], rows[:, 1], ALU.mult))
                    ch.link(nc.vector.tensor_tensor(y2[:, j], y2[:, j], rows[:, 2], ALU.add))
                    ch.link(nc.vector.tensor_tensor(tail.h[:, j], y2[:, j], hin[:, j], ALU.add))
                    v.sem_inc(taken, 1)
                    tail.vector(ch, j, i * 2 + j)
                ch.close()

        @block.scalar
        def _(act):
            act.sem_inc(y1_ready, 2)
            act.sem_inc(g_ready, 2)
            tail.scalar_start(act)
            with act.Fori(0, NB // 2) as i:
                for j in range(2):
                    act.wait_ge(u_ready, i * 2 + j + 1)
                    nc.scalar.activation(y1[:, j], u[:, j], ACT.Gelu).then_inc(y1_ready, 1)
                for j in range(2):
                    act.wait_ge(t_ready, i * 2 + j + 1)
                    nc.scalar.activation(g_[:, j], t[:, j], ACT.Gelu).then_inc(g_ready, 1)
                for j in range(2):
                    inner.scalar(act, j, i * 2 + j)
                    tail.norm.scalar(act, j, i * 2 + j)
                for j in range(2):
                    tail.scalar(act, j, i * 2 + j)

        @block.tensor
        def _(pe):
            tail.tensor_start(pe)
            pe.wait_ge(weights_in, 64)
            with pe.Fori(0, NB // 2) as i:
                for j in range(2):
                    pe.wait_ge(y1_ready, i * 2 + j + 3)
                    pe.sem_inc(held, 1)
                    for c in range(CH):
                        last = nc.tensor.matmul(ps[j][:, c, :], y1[:, j, c * CP:(c + 1) * CP], w[:],
                                                start=True, stop=True)
                    last.then_inc(fc_done, 1)
                for j in range(2):
                    tail.tensor(pe, j, i * 2 + j)

        @block.gpsimd
        def _(g):
            tail.gpsimd(g)


E = 8
HID = 682
HT = 114
NT = 6


def stage_experts(nc, d):
    with Mem(nc, "moe") as m:
        ident = m.sb("ident", [128, 128])
        router = m.sb("router", [C, E])
        pick = m.sb("pick", [E, E // 2, 128])
        w13 = m.sb("w13", [128, E, NT * HT])
        w2 = m.sb("w2", [HT, E, NT, C])
        x = m.sb("x", [128, 2, TOK])
        hin = m.sb("hin", [CP, 2, CH, C])
        top = m.sb("top", [CP, CH, 8])
        neg = m.sb("neg", [CP, CH])
        logit = m.sb("logit", [CP, CH, E])
        ex = m.sb("ex", [CP, CH, E])
        gate = m.sb("gate", [CP, CH, E])
        mask = m.sb("mask", [CP, CH, E])
        s1 = m.sb("s1", [CP, CH])
        gT = m.sb("gT", [E, TOK])
        G = m.sb("G", [128, 2, TOK])
        sg = m.sb("sg", [HT, 2, TOK])
        hh = m.sb("hh", [HT, 2, TOK])
        ty = m.sb("ty", [128, 2, TOK])
        acc = m.sb("acc", [128, 2, TOK])
        ps1 = [m.ps(f"ps1{k}", [HT, 512]) for k in range(2)]
        ps3 = [m.ps(f"ps3{k}", [HT, 512]) for k in range(2)]
        psy = m.ps("psy", [128, 512])
        psg = m.ps("psg", [128, 512])
        psr = m.ps("psr", [128, 512])
        held = m.sem("held")
        weights_in = m.sem("weights_in")
        loaded = [m.sem(f"loaded{j}") for j in range(2)]
        taken = m.sem("taken")
        names = ("routed", "logit_ready", "top_ready", "ex_ready", "gate_ready", "gate_turned", "gT_ready",
                 "spread", "G_ready", "G_used", "up_done", "sg_ready", "hh_ready", "down_done", "y_taken",
                 "acc_ready", "acc_turned", "acc_taken")
        (routed, logit_ready, top_ready, ex_ready, gate_ready, gate_turned, gT_ready, spread, G_ready,
         G_used, up_done, sg_ready, hh_ready, down_done, y_taken, acc_ready, acc_turned,
         acc_taken) = (m.sem(n) for n in names)
        dve = m.sem("dve")
        tail = Tail(nc, m, d, held, ident, ("h2", "x2", "x2T"))
        block = m.block()
        TILES = E * NT
        Q = E // 2

        def place(n):
            q, r = divmod(n, 2 * NT)
            return 2 * q + r % 2, r // 2

        @block.sync
        def _(sp):
            for a, n in ((ident, "ident"), (router, "routerT"), (pick, "pick"), (w13, "w13"), (w2, "w2")):
                sp.dma_start(a[:], d[n]).then_inc(weights_in, 16)
            with sp.Fori(0, NB // 2) as i:
                for j in range(2):
                    s = i * 2 + j
                    sp.wait_ge(taken, s + 1)
                    for half in range(2):
                        sp.dma_start(x[half * C:half * C + C, j], d["x1T"][s]).then_inc(loaded[j], 16)
                    sp.dma_start(hin[:, j], d["h1"][s]).then_inc(loaded[j], 16)

        @block.tensor
        def _(pe):
            tail.tensor_start(pe)
            pe.wait_ge(weights_in, 80)
            with pe.Fori(0, NB // 2) as i:
                for j in range(2):
                    s = i * 2 + j
                    base = s * TILES

                    def up(n):
                        e, t = place(n)
                        pe.wait_ge(hh_ready, base + n + 1)
                        cols = slice(t * HT, (t + 1) * HT)
                        nc.tensor.matmul(ps1[n % 2][:, 0:TOK], w13[0:C, e, cols], x[0:C, j], start=True, stop=True)
                        nc.tensor.matmul(ps3[n % 2][:, 0:TOK], w13[C:128, e, cols], x[C:128, j],
                                         start=True, stop=True).then_inc(up_done, 1)

                    pe.wait_ge(loaded[j], i * 48 + 48)
                    pe.wait_ge(gT_ready, s + 1)
                    pe.sem_inc(held, 1)
                    for c in range(CH):
                        last = nc.tensor.matmul(psr[0:CP, c * E:(c + 1) * E], x[0:C, j, c * CP:(c + 1) * CP],
                                                router[:], start=True, stop=True)
                    last.then_inc(routed, 1)
                    up(0)
                    for n in range(TILES):
                        if n + 1 < TILES:
                            up(n + 1)
                        e, t = place(n)
                        if n == NT:
                            pe.wait_ge(gate_ready, s + 1)
                            pe.sem_inc(held, 1)
                            for c in range(CH):
                                last = nc.tensor.transpose(psr[0:E, c * CP:(c + 1) * CP], gate[:, c, :],
                                                           ident[0:CP, 0:CP])
                            last.then_inc(gate_turned, 1)
                        if n % (2 * NT) == 2 * NT - 2:
                            pe.wait_ge(gT_ready, s + 2)
                            pe.wait_ge(G_ready, s * Q + n // (2 * NT) + 1)
                            pe.wait_ge(acc_taken, s + 1)
                            nc.tensor.matmul(psg[:, 0:TOK], pick[:, n // (2 * NT), :], gT[:],
                                             start=True, stop=True).then_inc(spread, 1)
                        if n % (2 * NT) == 0:
                            pe.wait_ge(y_taken, s * Q + n // (2 * NT) + 1)
                        pe.wait_ge(hh_ready, base + n + 3)
                        p = (e % 2) * C
                        nc.tensor.matmul(psy[p:p + C, 0:TOK], w2[:, e, t, :], hh[:, n % 2],
                                         start=t == 0, stop=t == NT - 1).then_inc(down_done, 1)
                    pe.wait_ge(acc_ready, s + 1)
                    pe.sem_inc(held, 1)
                    for c in range(CH):
                        last = nc.tensor.transpose(psg[0:CP, c * 128:(c + 1) * 128],
                                                   acc[:, j, c * CP:(c + 1) * CP], ident[:, :])
                    last.then_inc(acc_turned, 1)
                for j in range(2):
                    tail.tensor(pe, j, i * 2 + j)

        @block.scalar
        def _(act):
            act.sem_inc(gT_ready, 1)
            act.sem_inc(G_ready, 1)
            tail.scalar_start(act)
            with act.Fori(0, NB // 2) as i:
                for j in range(2):
                    s = i * 2 + j
                    base = s * TILES

                    def tiles(a, b):
                        for n in range(a, b):
                            act.wait_ge(up_done, base + n + 1)
                            act.wait_ge(hh_ready, base + n + 1)
                            nc.scalar.activation(sg[:, n % 2], ps1[n % 2][:, 0:TOK], ACT.Silu)\
                                .then_inc(sg_ready, 1)

                    act.wait_ge(top_ready, s + 1)
                    for c in range(CH):
                        last = nc.scalar.activation(ex[:, c, :], logit[:, c, :], ACT.Exp,
                                                    bias=neg[:, c:c + 1])
                    last.then_inc(ex_ready, 1)
                    tiles(0, NT + 1)
                    act.wait_ge(gate_turned, s + 1)
                    act.wait_ge(G_ready, s * Q + 1)
                    nc.scalar.activation(gT[:], psr[0:E, 0:TOK], ACT.Copy).then_inc(gT_ready, 1)
                    for q in range(Q):
                        tiles(max(NT + 1, q * 2 * NT), (q + 1) * 2 * NT)
                        act.wait_ge(spread, s * Q + q + 1)
                        act.wait_ge(G_used, s * Q + q + 1)
                        nc.scalar.activation(G[:, q % 2], psg[:, 0:TOK], ACT.Copy).then_inc(G_ready, 1)
                    tail.norm.scalar(act, j, s)
                for j in range(2):
                    tail.scalar(act, j, i * 2 + j)

        @block.vector
        def _(v):
            tt, ts = nc.vector.tensor_tensor, nc.vector.tensor_scalar
            v.sem_inc(taken, 2)
            v.sem_inc(hh_ready, 2)
            v.sem_inc(y_taken, 1)
            v.sem_inc(G_used, 2)
            v.sem_inc(acc_taken, 1)
            v.wait_ge(weights_in, 80)
            with v.Fori(0, NB // 2) as i:
                ch = Chain(v, dve, i, 2 * (1 + 3 + 1 + 9 + 7 + 2 + Norm.STEPS))
                for j in range(2):
                    s = i * 2 + j
                    base = s * TILES

                    def tiles(a, b):
                        for n in range(a, b):
                            v.wait_ge(sg_ready, base + n + 1)
                            if n >= 2:
                                v.wait_ge(down_done, base + n - 1)
                            tt(hh[:, n % 2], sg[:, n % 2], ps3[n % 2][:, 0:TOK], ALU.mult).then_inc(hh_ready, 1)

                    wide = lambda a: a.unsqueeze(2).broadcast_to((CP, CH, E))
                    v.wait_ge(routed, s + 1)
                    ch.link(nc.vector.tensor_copy(logit[:].rearrange("p c e -> p (c e)"), psr[0:CP, 0:CH * E]))
                    v.sem_inc(held, 1)
                    for c in range(CH):
                        ch.step(nc.vector.max(top[:, c, :], logit[:, c, :]))
                    ch.sync()
                    ch.link(ts(neg[:], top[:, :, 0], -1.0, None, ALU.mult))
                    v.sem_inc(top_ready, 1)
                    v.wait_ge(ex_ready, s + 1)
                    ch.link(nc.vector.tensor_reduce(s1[:], ex[:], AX.X, ALU.add))
                    ch.link(nc.vector.reciprocal(s1[:], s1[:]))
                    ch.step(tt(gate[:], ex[:], wide(s1[:]), ALU.mult))
                    ch.link(tt(mask[:], logit[:], wide(top[:, :, 1]), ALU.is_ge))
                    ch.link(tt(gate[:], gate[:], mask[:], ALU.mult))
                    ch.link(nc.vector.tensor_reduce(s1[:], gate[:], AX.X, ALU.add))
                    ch.link(ts(s1[:], s1[:], 1e-9, None, ALU.add))
                    ch.link(nc.vector.reciprocal(s1[:], s1[:]))
                    ch.link(tt(gate[:], gate[:], wide(s1[:]), ALU.mult))
                    v.sem_inc(gate_ready, 1)
                    for q in range(Q):
                        tiles(q * 2 * NT, (q + 1) * 2 * NT)
                        v.wait_ge(down_done, base + (q + 1) * 2 * NT)
                        v.wait_ge(G_ready, s * Q + q + 2)
                        if q == 0:
                            ch.link(tt(acc[:, j], psy[:, 0:TOK], G[:, q % 2], ALU.mult))
                        else:
                            ch.link(tt(ty[:, 0], psy[:, 0:TOK], G[:, q % 2], ALU.mult))
                            ch.link(tt(acc[:, j], acc[:, j], ty[:, 0], ALU.add))
                        v.sem_inc(y_taken, 1)
                        v.sem_inc(G_used, 1)
                    v.sem_inc(acc_ready, 1)
                    v.wait_ge(acc_turned, s + 1)
                    tail.vector_begin(v, s)
                    both = psg[0:CP, 0:CH * 128].rearrange("p (c h e) -> p c h e", c=CH, h=2)
                    ch.link(tt(tail.h[:, j], both[:, :, 0, :], hin[:, j], ALU.add))
                    ch.link(tt(tail.h[:, j], both[:, :, 1, :], tail.h[:, j], ALU.add))
                    v.sem_inc(acc_taken, 1)
                    v.sem_inc(taken, 1)
                    tail.vector(ch, j, s)
                ch.close()

        @block.gpsimd
        def _(g):
            tail.gpsimd(g)


def stage_pairs(nc, d):
    with Mem(nc, "pair") as m:
        K1 = C + 1
        ident = m.sb("ident", [128, 128])
        mix = m.sb("mix", [K1, K1])
        wtop = m.sb("wtop", [K1, 3 * C])
        wbot = m.sb("wbot", [C, 3 * C])
        xT = m.sb("xT", [K1, 2, TOK])
        x = m.sb("x", [CP, 2, CH, C])
        hin = m.sb("hin", [CP, 2, CH, C])
        L = m.sb("L", [K1, TOK])
        mx = m.sb("mx", [CP, 2, CH])
        sm = m.sb("sm", [CP, 2, CH])
        ex = m.sb("ex", [CP, 2, CH, TOK])
        AT = m.sb("AT", [CP, CH, TOK])
        it = m.sb("it", [C, TOK])
        zr = m.sb("zr", [CP, CH, 3 * C])
        t1 = m.sb("t1", [CP, CH, C])
        t2 = m.sb("t2", [CP, CH, C])
        psA = [m.ps(f"psA{c}", [CP, 512]) for c in range(CH)]
        psT = [m.ps(f"psT{c}", [CP, 512]) for c in range(CH)]
        psL = m.ps("psL", [K1, 512])
        held = m.sem("held")
        weights_in = m.sem("weights_in")
        loaded = [m.sem(f"loaded{j}") for j in range(2)]
        (taken, ones, left_done, left_ready, A_done, max_ready, ex_ready, probs_ready, probs_turned, AT_ready,
         it_done, it_ready, gates_done, gates_ready, mixed) = (m.sem(n) for n in (
             "taken", "ones", "left_done", "left_ready", "A_done", "max_ready", "ex_ready", "probs_ready",
             "probs_turned", "AT_ready", "it_done", "it_ready", "gates_done", "gates_ready", "mixed"))
        dve = m.sem("dve")
        tail = Tail(nc, m, d, held, ident, ("h3", None, "x3T"))
        block = m.block()

        @block.sync
        def _(sp):
            for a, n in ((ident, "ident"), (mix, "pair_mix"), (wtop, "pair_top"), (wbot, "pair_bot")):
                sp.dma_start(a[:], d[n]).then_inc(weights_in, 16)
            with sp.Fori(0, NB // 2) as i:
                for j in range(2):
                    s = i * 2 + j
                    sp.wait_ge(taken, s + 1)
                    sp.dma_start(xT[0:C, j], d["x2T"][s]).then_inc(loaded[j], 16)
                    sp.dma_start(x[:, j], d["x2"][s]).then_inc(loaded[j], 16)
                    sp.dma_start(hin[:, j], d["h2"][s]).then_inc(loaded[j], 16)

        @block.tensor
        def _(pe):
            tail.tensor_start(pe)
            pe.wait_ge(weights_in, 64)
            pe.wait_ge(ones, 1)
            with pe.Fori(0, NB // 2) as i:
                for j in range(2):
                    s = i * 2 + j
                    chunk = lambda c: slice(c * CP, (c + 1) * CP)
                    pe.wait_ge(loaded[j], i * 48 + 48)
                    pe.wait_ge(it_ready, s + 1)
                    pe.wait_ge(gates_ready, s + 1)
                    pe.sem_inc(held, 1)
                    nc.tensor.matmul(psL[:, 0:TOK], mix[:], xT[:, j], start=True, stop=True).then_inc(left_done, 1)
                    pe.wait_ge(left_ready, s + 1)
                    for c in range(CH):
                        last = nc.tensor.matmul(psA[c][:, 0:TOK], L[:, chunk(c)], xT[:, j], start=True, stop=True)
                    last.then_inc(A_done, 1)
                    pe.wait_ge(probs_ready, s + 1)
                    pe.sem_inc(held, 1)
                    for jc in range(CH):
                        for c in range(CH):
                            last = nc.tensor.transpose(psT[jc][:, chunk(c)], ex[:, j, c, chunk(jc)],
                                                       ident[0:CP, 0:CP])
                        last.then_inc(probs_turned, 1)
                    for jc in range(CH):
                        pe.wait_ge(AT_ready, s * 3 + jc + 1)
                        last = nc.tensor.matmul(psL[0:C, 0:TOK], x[:, j, jc, :], AT[:, jc, :],
                                                start=jc == 0, stop=jc == CH - 1)
                    last.then_inc(it_done, 1)
                    pe.wait_ge(it_ready, s + 2)
                    pe.sem_inc(held, 1)
                    for c in range(CH):
                        nc.tensor.matmul(psA[c][:, 0:3 * C], xT[:, j, chunk(c)], wtop[:], start=True, stop=False)
                        last = nc.tensor.matmul(psA[c][:, 0:3 * C], it[:, chunk(c)], wbot[:], start=False, stop=True)
                    last.then_inc(gates_done, 1)
                for j in range(2):
                    tail.tensor(pe, j, i * 2 + j)

        @block.scalar
        def _(act):
            act.sem_inc(it_ready, 1)
            act.sem_inc(gates_ready, 1)
            tail.scalar_start(act)
            with act.Fori(0, NB // 2) as i:
                for j in range(2):
                    s = i * 2 + j
                    act.wait_ge(left_done, s + 1)
                    nc.scalar.activation(L[:], psL[:, 0:TOK], ACT.Copy).then_inc(left_ready, 1)
                    act.wait_ge(max_ready, s + 1)
                    for c in range(CH):
                        last = nc.scalar.activation(ex[:, j, c, :], psA[c][:, 0:TOK], ACT.Exp,
                                                    bias=mx[:, j, c:c + 1], accum_out=sm[:, j, c:c + 1])
                    last.then_inc(ex_ready, 1)
                    for jc in range(CH):
                        act.wait_ge(probs_turned, s * 3 + jc + 1)
                        nc.scalar.activation(AT[:, jc, :], psT[jc][:, 0:TOK], ACT.Copy).then_inc(AT_ready, 1)
                    act.wait_ge(it_done, s + 1)
                    nc.scalar.activation(it[:], psL[0:C, 0:TOK], ACT.Copy).then_inc(it_ready, 1)
                    act.wait_ge(gates_done, s + 1)
                    act.wait_ge(mixed, s + 1)
                    for c in range(CH):
                        nc.scalar.activation(zr[:, c, 0:C], psA[c][:, 0:C], ACT.Tanh)
                        last = nc.scalar.activation(zr[:, c, C:3 * C], psA[c][:, C:3 * C], ACT.Tanh, scale=0.5)
                    last.then_inc(gates_ready, 1)
                    tail.norm.scalar(act, j, s)
                for j in range(2):
                    tail.scalar(act, j, i * 2 + j)

        @block.vector
        def _(v):
            tt, ts = nc.vector.tensor_tensor, nc.vector.tensor_scalar
            nc.vector.memset(xT[C:K1], 1.0).then_inc(ones, 1)
            v.sem_inc(taken, 2)
            v.sem_inc(mixed, 1)
            v.wait_ge(weights_in, 64)
            with v.Fori(0, NB // 2) as i:
                ch = Chain(v, dve, i, 2 * (3 + 1 + 1 + 3 + 5 + Norm.STEPS))
                for j in range(2):
                    s = i * 2 + j
                    v.wait_ge(A_done, s + 1)
                    for c in range(CH):
                        ch.step(nc.vector.tensor_reduce(mx[:, j, c:c + 1], psA[c][:, 0:TOK], AX.X, ALU.max))
                    ch.sync()
                    ch.link(ts(mx[:, j], mx[:, j], -1.0, None, ALU.mult))
                    v.sem_inc(max_ready, 1)
                    v.wait_ge(ex_ready, s + 1)
                    ch.link(nc.vector.reciprocal(sm[:, j], sm[:, j]))
                    for c in range(CH):
                        ch.step(ts(ex[:, j, c, :], ex[:, j, c, :], sm[:, j, c:c + 1], None, ALU.mult))
                    ch.sync()
                    v.sem_inc(probs_ready, 1)
                    v.wait_ge(gates_ready, s + 2)
                    tail.vector_begin(v, s)
                    ch.link(ts(zr[:, :, C:3 * C], zr[:, :, C:3 * C], 0.5, 0.5, ALU.mult, ALU.add))
                    ch.step(tt(t1[:], zr[:, :, C:2 * C], x[:, j], ALU.mult))
                    ch.link(tt(t2[:], zr[:, :, 2 * C:3 * C], zr[:, :, 0:C], ALU.mult))
                    ch.step(tt(t1[:], t1[:], hin[:, j], ALU.add))
                    ch.sync()
                    ch.link(tt(tail.h[:, j], t1[:], t2[:], ALU.add))
                    v.sem_inc(mixed, 1)
                    v.sem_inc(taken, 1)
                    tail.vector(ch, j, s)
                ch.close()

        @block.gpsimd
        def _(g):
            tail.gpsimd(g)


HEADS = 8
NK = 64
DK = 32
TOPK = 16
NT4 = NK * NK // 128
ROWS = [(i, TOPK // (i + 1)) for i in range(5)]
NCAND = sum(w for _, w in ROWS) + 3 * 2 + 8
FLOOR = 87.0
LIFT = 40.0
SLACK = 2.0 ** -21
HIDDEN = -1e30


def stage_keys(nc, d):
    with Mem(nc, "keys") as m:
        wq = m.sb("wq", [DK, 2, HEADS, C])
        keys = m.sb("keys", [DK, 2, HEADS, NK])
        both = m.sb("both", [C, HEADS, 2, NK])
        proj = m.sb("proj", [128, HEADS, 128])
        raw = m.sb("raw", [128, 2, NT4, 128])
        new = m.sb("new", [128, 2, NT4, 128])
        ps = [m.ps(f"ps{k}", [C, 4, 2, NK]) for k in range(2)]
        pst = [m.ps(f"pst{k}", [128, 4, 128]) for k in range(4)]
        loaded, done, copied, stored, scaled = (m.sem(n) for n in ("loaded", "done", "copied", "stored", "scaled"))
        raw_in = [m.sem(f"raw_in{j}") for j in range(2)]
        new_out = [m.sem(f"new_out{j}") for j in range(2)]
        projected = m.sem("projected")
        taken = [m.sem(f"taken{k}") for k in range(2)]
        stored_table = [m.pool_dma_sem(f"stored_table{j}") for j in range(2)]
        block = m.block()
        QUADS = NT4 // 4

        @block.sync
        def _(sp):
            sp.dma_start(wq[:], d["wq_pk"]).then_inc(loaded, 16)
            sp.dma_start(keys[:], d["pk_keys"]).then_inc(loaded, 16)
            sp.dma_start(proj[:], d["head_proj"]).then_inc(loaded, 16)
            for h in range(HEADS):
                if h >= 2:
                    sp.wait_ge(projected, (h - 1) * QUADS)
                sp.dma_start(raw[:, h % 2], d["tableT"][h]).then_inc(raw_in[h % 2], 16)
            sp.wait_ge(copied, 2)
            sp.dma_start(d["score_w"].rearrange("h c k -> c h k"),
                         both[:].rearrange("c h p k -> c h (p k)")).then_inc(stored, 16)
            sp.wait_ge(stored, 16)

        @block.tensor
        def _(pe):
            pe.wait_ge(loaded, 48)
            for h in range(HEADS):
                for p in range(2):
                    last = nc.tensor.matmul(ps[h // 4][:, h % 4, p, :], wq[:, p, h, :], keys[:, p, h, :],
                                            start=True, stop=True)
                if h % 4 == 3:
                    last.then_inc(done, 1)
            pe.wait_ge(scaled, 1)
            for h in range(HEADS):
                pe.wait_ge(raw_in[h % 2], h // 2 * 16 + 16)
                for g in range(QUADS):
                    at = h * QUADS + g
                    if at >= 4:
                        pe.wait_ge(taken[at % 2], at // 2 - 1)
                    for k in range(4):
                        last = nc.tensor.matmul(pst[at % 4][:, k], raw[:, h % 2, 4 * g + k], proj[:, h],
                                                start=True, stop=True)
                    last.then_inc(projected, 1)

        def take(eng, which, copy):
            for h in range(HEADS):
                if h >= 2:
                    eng.wait_ge(new_out[h % 2], h // 2 * 16)
                for g in range(which, QUADS, 2):
                    at = h * QUADS + g
                    eng.wait_ge(projected, at + 1)
                    copy(new[:, h % 2, 4 * g:4 * g + 4], pst[at % 4][:]).then_inc(taken[which], 1)

        @block.scalar
        def _(act):
            for k in range(2):
                act.wait_ge(done, k + 1)
                nc.scalar.activation(both[:, 4 * k:4 * k + 4], ps[k][:], ACT.Copy).then_inc(copied, 1)
            take(act, 0, lambda out, in_: nc.scalar.activation(out, in_, ACT.Copy))

        @block.vector
        def _(v):
            v.wait_ge(loaded, 48)
            nc.vector.tensor_scalar(proj[0:C], proj[0:C], C ** -0.5, None, ALU.mult).then_inc(scaled, 1)
            take(v, 1, nc.vector.tensor_copy)

        @block.gpsimd
        def _(g_):
            for h in range(HEADS):
                for k in range(2):
                    g_.wait_ge(taken[k], (h + 1) * QUADS // 2)
                g_.dma_start(d["table"][h], new[:, h % 2]).then_inc(stored_table[h % 2], 16)
                g_.wait_ge(stored_table[h % 2], h // 2 * 16 + 16)
                g_.sem_inc(new_out[h % 2], 16)


def stage_memory(nc, d):
    with Mem(nc, "mem") as m:
        ident = m.sb("ident", [128, 128])
        tri = m.sb("tri", [CP, CH, TOK])
        acc = m.sb("acc", [CP, NB, CH, C])
        pick_in = m.sb("pick_in", [128, NT4 // 4, 128])
        pick = m.sb("pick", [128, NT4, 128], F32R)
        table = m.sb("table", [128, NT4, 128])
        score_w = m.sb("score_w", [C, 2 * NK])
        lift = m.sb("lift", [128, 1])
        xa = m.sb("xa", [C, 2, TOK])
        xc = m.sb("xc", [C, 2, TOK])
        S = m.sb("S", [CP, CH, 2 * NK])
        rest = m.sb("rest", [CP, CH, 2, NK])
        lists = m.sb("lists", [CP, CH, 2, TOPK])
        cand = m.sb("cand", [CP, CH, NCAND])
        cand2 = m.sb("cand2", [CP, CH, NCAND])
        best = m.sb("best", [CP, CH, TOPK])
        size = m.sb("size", [CP, CH])
        cut = m.sb("cut", [CP, CH])
        terms = m.sb("terms", [CP, CH, TOPK])
        rZ = m.sb("rZ", [CP, 2, CH])
        Zh = m.sb("Zh", [128, 2, TOK + 1], F32R)
        Zl = m.sb("Zl", [128, 2, TOK + 1], F32R)
        RING = 4
        ex = m.sb("ex", [128, RING, TOK])
        wt = m.sb("wt", [128, RING, TOK])
        kvT = m.sb("kvT", [128, TOK])
        kv = m.sb("kv", [CP, CH, 128])
        kT = m.sb("kT", [C, TOK])
        mx = m.sb("mx", [CP, CH])
        sm = m.sb("sm", [CP, CH])
        pr = m.sb("pr", [CP, CH, TOK])
        PT = m.sb("PT", [CP, 2, TOK])
        ps_z = [m.ps(f"ps_z{k}", [128, 512]) for k in range(RING)]
        ps_kv = m.ps("ps_kv", [128, 512])
        ps_a = m.ps("ps_a", [128, 512])
        ps_c = m.ps("ps_c", [128, 512])
        ps_s = m.ps("ps_s", [CP, 512])
        held = m.sem("held")
        consts_in = m.sem("consts_in")
        pick_part = m.sem("pick_part")
        pick_ready = m.sem("pick_ready")
        head_in = m.sem("head_in")
        table_in = [m.sem(f"table_in{k}") for k in range(4)]
        xa_in = [m.sem(f"xa_in{j}") for j in range(2)]
        xc_in = [m.sem(f"xc_in{j}") for j in range(2)]
        (scored, S_ready, lists_ready, sums_ready, best_ready, terms_ready, cut_ready, cut_done, cut_turned,
         high_ready, Z_ready) = (m.sem(n) for n in (
             "scored", "S_ready", "lists_ready", "sums_ready", "best_ready", "terms_ready", "cut_ready",
             "cut_done", "cut_turned", "high_ready", "Z_ready"))
        z_done, ex_ready, wt_ready, kv_done = (m.sem(n) for n in ("z_done", "ex_ready", "wt_ready", "kv_done"))
        (kvT_ready, kv_turned, kv_ready, k_turned, kT_ready, s_done, max_ready, e_ready, p_turned, PT_ready,
         out_done, added) = (m.sem(n) for n in (
             "kvT_ready", "kv_turned", "kv_ready", "k_turned", "kT_ready", "s_done", "max_ready", "e_ready",
             "p_turned", "PT_ready", "out_done", "added"))
        head_free = m.sem("head_free")
        stored = m.sem("stored")
        dve_a, dve_c = m.sem("dve_a"), m.sem("dve_c")
        block = m.block()
        chunk = lambda c: slice(c * CP, (c + 1) * CP)
        score_at = [ps_c[0:CP, 0:CP], ps_c[0:CP, CP:3 * CP], ps_s[:, 0:TOK]]
        turned_at = {(0, c): ps_c[0:CP, chunk(c)] for c in range(CH)}
        turned_at |= {(1, 1): ps_s[:, chunk(0)], (1, 2): ps_s[:, chunk(1)], (2, 2): ps_s[:, chunk(2)]}
        PT_at = {(0, c): PT[:, 0, chunk(c)] for c in range(CH)}
        PT_at |= {(1, 1): PT[:, 1, chunk(0)], (1, 2): PT[:, 1, chunk(1)], (2, 2): PT[:, 1, chunk(2)]}

        def units(eng, a, body, c):
            with eng.Fori(0, HEADS) as h:
                u0 = h * NB
                yield h
                a(u0, 0)
                body(u0, 0, 0, True, False)
                with eng.Fori(0, (NB - 2) // 2) as i:
                    for j in range(2):
                        s = i * 2 + (1 + j)
                        body(u0 + s, s, (1 + j) % 2, True, True)
                body(u0 + (NB - 1), NB - 1, 1, False, True)
                c(u0 + (NB - 1), NB - 1, 1)

        @block.sync
        def _(sp):
            for t, n in ((ident, "ident"), (tri, "tri")):
                sp.dma_start(t[:], d[n]).then_inc(consts_in, 16)
            sp.dma_start(acc[:], d["h3"].rearrange("b p c e -> p b c e")).then_inc(consts_in, 16)
            for k in range(4):
                if k:
                    sp.wait_ge(pick_ready, k)
                sp.dma_start(pick_in[:], d["key_pick"][:, k * 8:k * 8 + 8]).then_inc(pick_part, 16)
            with sp.Fori(0, HEADS) as h:
                sp.wait_ge(head_free, h + 1)
                sp.dma_start(score_w[:], d["score_w"][h]).then_inc(head_in, 16)
                for j in range(2):
                    sp.dma_start(xa[:, j], d["x3T"][j]).then_inc(xa_in[j], 16)
                for k in range(4):
                    sp.dma_start(table[:, k * 8:k * 8 + 8], d["table"][h][:, k * 8:k * 8 + 8])\
                        .then_inc(table_in[k], 16)
                for j in range(2):
                    sp.dma_start(xc[:, j], d["x3T"][j]).then_inc(xc_in[j], 16)
                with sp.Fori(0, NB // 2 - 1) as i:
                    for j in range(2):
                        sp.wait_ge(scored, h * NB + i * 2 + (j + 1))
                        sp.dma_start(xa[:, j], d["x3T"][i * 2 + (2 + j)]).then_inc(xa_in[j], 16)
                        sp.wait_ge(s_done, h * NB + i * 2 + (j + 1))
                        sp.dma_start(xc[:, j], d["x3T"][i * 2 + (2 + j)]).then_inc(xc_in[j], 16)
            sp.wait_ge(added, HEADS * NB + 1)
            sp.dma_start(d["out"].rearrange("b (c p) e -> p b c e", p=CP), acc[:]).then_inc(stored, 16)
            sp.wait_ge(stored, 16)

        @block.tensor
        def _(pe):
            mm, tp = nc.tensor.matmul, nc.tensor.transpose
            for sem, n in ((cut_turned, 1), (kv_turned, 1), (kv_done, RING)):
                pe.sem_inc(sem, n)
            pe.wait_ge(consts_in, 48)
            pe.wait_ge(pick_ready, 5)

            def arrived(sems, u, par):
                pe.wait_ge(sems[par], u * 8 + (16 if par == 0 else 8))

            def a_scores(u, par):
                arrived(xa_in, u, par)
                pe.wait_ge(Z_ready, u + 1)
                pe.sem_inc(held, 1)
                for c in range(CH):
                    last = mm(ps_a[0:CP, c * 128:(c + 1) * 128], xa[:, par, chunk(c)], score_w[:],
                              start=True, stop=True)
                last.then_inc(scored, 1)

            def a_turn(u):
                pe.wait_ge(cut_done, u + 1)
                pe.sem_inc(held, 1)
                for c in range(CH):
                    last = tp(ps_a[:, chunk(c)], S[:, c, :], ident[0:CP, 0:CP])
                last.then_inc(cut_turned, 1)

            def b_sum(u, n, par):
                if n == 0:
                    pe.wait_ge(Z_ready, u + 2)
                    pe.sem_inc(held, 1)
                pe.wait_ge(wt_ready, u * NT4 + (n + 1))
                mm(ps_z[n % RING][:, 0:TOK + 1], pick[:, n, :], Zh[:, par], start=True, stop=False)
                mm(ps_z[n % RING][:, 0:TOK + 1], pick[:, n, :], Zl[:, par], start=False, stop=True)\
                    .then_inc(z_done, 1)

            def b_product(u, n):
                pe.wait_ge(wt_ready, u * NT4 + (n + 1 + RING))
                mm(ps_kv[:, 0:TOK], table[:, n, :], wt[:, n % RING], start=n == 0, stop=n == NT4 - 1)\
                    .then_inc(kv_done, 1)

            def c_turn_kv(u):
                pe.wait_ge(kvT_ready, u + 2)
                pe.wait_ge(added, u + 1)
                pe.sem_inc(held, 1)
                for c in range(CH):
                    last = tp(ps_c[0:CP, c * 128:(c + 1) * 128], kvT[:, chunk(c)], ident[:])
                last.then_inc(kv_turned, 1)

            def c_turn_k(u):
                pe.wait_ge(kv_ready, u + 1)
                pe.sem_inc(held, 1)
                for c in range(CH):
                    last = tp(ps_c[0:C, chunk(c)], kv[:, c, 0:C], ident[0:CP, 0:CP])
                last.then_inc(k_turned, 1)

            def c_scores(u, par):
                arrived(xc_in, u, par)
                pe.wait_ge(kT_ready, u + 1)
                pe.wait_ge(PT_ready, u * 2 + 2)
                pe.sem_inc(held, 1)
                for c in range(CH):
                    last = mm(score_at[c], xc[:, par, chunk(c)], kT[:, 0:(c + 1) * CP], start=True, stop=True)
                last.then_inc(s_done, 1)

            def c_turn_p(u):
                pe.wait_ge(e_ready, u + 1)
                pe.sem_inc(held, 1)
                for jc in range(CH):
                    for c in range(jc, CH):
                        last = tp(turned_at[jc, c], pr[:, c, chunk(jc)], ident[0:CP, 0:CP])
                    if jc != 1:
                        last.then_inc(p_turned, 1)

            def c_attend(u):
                pe.wait_ge(PT_ready, u * 2 + 4)
                pe.sem_inc(held, 1)
                for c in range(CH):
                    for jc in range(c + 1):
                        last = mm(ps_c[0:CP, c * C:(c + 1) * C], PT_at[jc, c], kv[:, jc, C:128],
                                  start=jc == 0, stop=jc == c)
                last.then_inc(out_done, 1)

            def a(u, par):
                a_scores(u, par)
                a_turn(u)
                for n in range(RING - 1):
                    b_sum(u, n, par)

            def body(u, s, par, with_a, with_c):
                for n in range(NT4):
                    ahead = n + RING - 1
                    if ahead < NT4:
                        b_sum(u, ahead, par)
                    elif with_a:
                        b_sum(u + 1, ahead - NT4, 1 - par)
                    if with_a and n == 0:
                        a_scores(u + 1, 1 - par)
                    if n == 0:
                        pe.wait_ge(kvT_ready, u + 1)
                    if n % 8 == 0:
                        pe.wait_ge(table_in[n // 8], head[0] * 16 + 16)
                    b_product(u, n)
                    if with_c and n == 3:
                        c_turn_kv(u - 1)
                    if with_c and n == 6:
                        c_turn_k(u - 1)
                    if with_c and n == 9:
                        c_scores(u - 1, 1 - par)
                    if with_c and n == 17:
                        c_turn_p(u - 1)
                    if with_c and n == 20:
                        c_attend(u - 1)
                    if with_a and n == 22:
                        a_turn(u + 1)

            def c(u, s, par):
                c_turn_kv(u)
                c_turn_k(u)
                c_scores(u, par)
                c_turn_p(u)
                c_attend(u)

            head = [None]
            for head[0] in units(pe, a, body, c):
                pe.wait_ge(head_in, head[0] * 16 + 16)

        @block.scalar
        def _(act):
            run = nc.scalar.activation
            act.sem_inc(kvT_ready, 1)
            act.sem_inc(PT_ready, 2)
            act.wait_ge(pick_ready, 5)

            def a_copy(u):
                act.wait_ge(scored, u + 1)
                act.wait_ge(cut_turned, u + 1)
                run(S[:].rearrange("p c k -> p (c k)"), ps_a[0:CP, 0:CH * 128], ACT.Copy).then_inc(S_ready, 1)

            def a_terms(u):
                act.wait_ge(best_ready, u + 1)
                run(terms[:], terms[:], ACT.Exp, bias=lift[0:CP, 0:1]).then_inc(terms_ready, 1)

            def a_high(u, par):
                act.wait_ge(cut_turned, u + 2)
                run(Zh[:, par, 0:TOK], ps_a[:, 0:TOK], ACT.Copy).then_inc(high_ready, 1)

            def b_exp(u, n):
                act.wait_ge(z_done, u * NT4 + (n + 1))
                act.wait_ge(wt_ready, u * NT4 + (n + 1))
                run(ex[:, n % RING], ps_z[n % RING][:, 0:TOK], ACT.Exp, bias=lift[:, 0:1]).then_inc(ex_ready, 1)

            def c_copy_kvT(u):
                act.wait_ge(kv_done, u * NT4 + (NT4 + RING))
                act.wait_ge(kv_turned, u + 1)
                run(kvT[:], ps_kv[:, 0:TOK], ACT.Copy).then_inc(kvT_ready, 1)

            def c_copy_kT(u):
                act.wait_ge(k_turned, u + 1)
                run(kT[:], ps_c[0:C, 0:TOK], ACT.Copy).then_inc(kT_ready, 1)

            def c_exp(u):
                act.wait_ge(max_ready, u + 1)
                for c in range(CH):
                    last = run(pr[:, c, 0:(c + 1) * CP], score_at[c], ACT.Exp, bias=mx[:, c:c + 1],
                               accum_out=sm[:, c:c + 1])
                last.then_inc(e_ready, 1)

            def c_copy_PT(u, k):
                act.wait_ge(p_turned, u * 2 + (k + 1))
                run(PT[:, k], (ps_c, ps_s)[k][0:CP, 0:TOK], ACT.Copy).then_inc(PT_ready, 1)

            def a(u, par):
                a_copy(u)
                a_terms(u)
                a_high(u, par)

            def body(u, s, par, with_a, with_c):
                for n in range(NT4):
                    b_exp(u, n)
                    if with_c and n == 0:
                        c_copy_kvT(u - 1)
                    if with_a and n == 1:
                        a_copy(u + 1)
                    if with_c and n == 7:
                        c_copy_kT(u - 1)
                    if with_c and n == 15:
                        c_exp(u - 1)
                    if with_c and n in (18, 19):
                        c_copy_PT(u - 1, n - 18)
                    if with_a and n == 21:
                        a_terms(u + 1)
                    if with_a and n == 24:
                        a_high(u + 1, 1 - par)

            def c(u, s, par):
                c_copy_kvT(u)
                c_copy_kT(u)
                c_exp(u)
                c_copy_PT(u, 0)
                c_copy_PT(u, 1)

            for _ in units(act, a, body, c):
                pass

        @block.vector
        def _(v):
            tt, ts, stt = nc.vector.tensor_tensor, nc.vector.tensor_scalar, nc.vector.scalar_tensor_tensor
            v.sem_inc(Z_ready, 1)
            v.sem_inc(wt_ready, RING)
            v.sem_inc(head_free, 1)
            v.sem_inc(added, 1)
            for t in (Zh, Zl):
                last = nc.vector.memset(t[:].bitcast(F32), 0.0)
            last.then_inc(dve_a, 1)
            for k in range(4):
                v.wait_ge(pick_part, k * 16 + 16)
                nc.vector.tensor_copy(pick[:, k * 8:k * 8 + 8], pick_in[:]).then_inc(pick_ready, 1)
            nc.vector.memset(lift[:], -LIFT).then_inc(pick_ready, 1)
            v.wait_ge(consts_in, 48)
            v.wait_ge(dve_a, 1)
            NA, NC = 6 * 3 + 3 * 3 + 4 + 2 + 1, 3 + 3 + 1 + 1 + 3
            chains = {}
            wide = lambda a, n: a.unsqueeze(2).broadcast_to((CP, CH, n))

            def a_lists(u, part, c):
                if (part, c) == (0, 0):
                    v.wait_ge(S_ready, u + 1)
                    v.sem_inc(held, 1)
                    chains["a"] = Chain(v, dve_a, u, NA)
                    chains["a"].n = 1
                ch = chains["a"]
                if part and c == 0:
                    ch.sync()
                    v.sem_inc(held, 1)
                for p in range(2):
                    sc, li = S[:, c, p * NK:(p + 1) * NK], lists[:, c, p]
                    if part == 0:
                        ch.step(nc.vector.max(li[:, 0:8], sc))
                    elif part == 1:
                        ch.step(nc.vector.match_replace(rest[:, c, p], li[:, 0:8], sc, -3e38))
                    else:
                        ch.step(nc.vector.max(li[:, 8:16], rest[:, c, p]))
                if (part, c) == (2, CH - 1):
                    ch.sync()
                    v.sem_inc(lists_ready, 1)

            def a_best(u, part):
                ch = chains["a"]
                if part == 0:
                    v.wait_ge(sums_ready, u + 1)
                else:
                    ch.sync()
                v.sem_inc(held, 1)
                for c in range(CH):
                    if part == 0:
                        ch.step(nc.vector.max(best[:, c, 0:8], cand[:, c]))
                    elif part == 1:
                        ch.step(nc.vector.match_replace(cand2[:, c], best[:, c, 0:8], cand[:, c], -3e38))
                    else:
                        ch.step(nc.vector.max(best[:, c, 8:16], cand2[:, c]))

            def a_cut(u):
                ch = chains["a"]
                ends = lists[:, :, :, 0:TOPK:TOPK - 1]
                ch.link(nc.vector.tensor_reduce(size[:], ends, AX.XY, ALU.add, apply_absolute_value=True))
                ch.link(stt(cut[:], size[:], -SLACK, best[:, :, TOPK - 1], ALU.mult, ALU.add))
                ch.link(stt(cut[:], best[:, :, 0], -FLOOR, cut[:], ALU.add, ALU.max))
                v.sem_inc(cut_ready, 1)
                ch.link(tt(terms[:], best[:], wide(cut[:], TOPK), ALU.subtract))
                v.sem_inc(best_ready, 1)

            def a_norm(u, par):
                ch = chains["a"]
                v.wait_ge(terms_ready, u + 1)
                ch.link(nc.vector.tensor_reduce(size[:], terms[:], AX.X, ALU.add))
                ch.link(nc.vector.reciprocal(rZ[:, par], size[:]))

            def a_low(u, par):
                ch = chains["a"]
                v.wait_ge(high_ready, u + 1)
                ch.link(tt(Zl[:, par, 0:TOK], ps_a[:, 0:TOK], Zh[:, par, 0:TOK].bitcast(F32), ALU.subtract))
                ch.n -= 1
                ch.close()
                v.sem_inc(Z_ready, 1)

            def b_weights(u, n):
                v.wait_ge(ex_ready, u * NT4 + (n + 1))
                v.wait_ge(kv_done, u * NT4 + (n + 1))
                stt(wt[:, n % RING], ps_z[n % RING][:, 0:TOK], 0.0, ex[:, n % RING], ALU.is_ge, ALU.mult)\
                    .then_inc(wt_ready, 1)

            def c_scale(u, par):
                v.wait_ge(kv_turned, u + 2)
                chains["c"] = ch = Chain(v, dve_c, u, NC)
                for c in range(CH):
                    ch.step(ts(kv[:, c, :], ps_c[0:CP, c * 128:(c + 1) * 128], rZ[:, par, c:c + 1], None, ALU.mult))
                ch.sync()
                v.sem_inc(kv_ready, 1)

            def c_max(u, cs):
                ch = chains["c"]
                if 0 in cs:
                    v.wait_ge(s_done, u + 1)
                    v.sem_inc(held, 1)
                for c in cs:
                    w = (c + 1) * CP
                    ch.step(nc.vector.tensor_tensor_reduce(
                        out=score_at[c], in0=score_at[c], in1=tri[:, c, 0:w], scale=1.0, scalar=-3e38,
                        op0=ALU.add, op1=ALU.max, accum_out=mx[:, c:c + 1]))
                if CH - 1 in cs:
                    ch.sync()
                    ch.link(ts(mx[:], mx[:], -1.0, None, ALU.mult))
                    v.sem_inc(max_ready, 1)

            def c_norm(u):
                v.wait_ge(e_ready, u + 1)
                chains["c"].link(nc.vector.reciprocal(sm[:], sm[:]))

            def c_add(u, s):
                ch = chains["c"]
                v.wait_ge(out_done, u + 1)
                for c in range(CH):
                    at = acc[:, s, c]
                    ch.step(stt(at, ps_c[0:CP, c * C:(c + 1) * C], sm[:, c:c + 1], at, ALU.mult, ALU.add))
                ch.sync()
                ch.close()
                v.sem_inc(added, 1)

            def a(u, par):
                for part in range(3):
                    for c in range(CH):
                        a_lists(u, part, c)
                for part in range(3):
                    a_best(u, part)
                chains["a"].sync()
                a_cut(u)
                a_norm(u, par)
                a_low(u, par)

            def body(u, s, par, with_a, with_c):
                lists_slots = {2: (0, 0), 3: (0, 1), 4: (0, 2), 6: (1, 0), 7: (1, 1), 8: (1, 2),
                               9: (2, 0), 10: (2, 1), 11: (2, 2)}
                for n in range(NT4):
                    b_weights(u, n)
                    if with_a and n in lists_slots:
                        a_lists(u + 1, *lists_slots[n])
                    if with_c and n == 5:
                        c_scale(u - 1, 1 - par)
                    if with_c and n == 12:
                        c_max(u - 1, (0, 1))
                    if with_c and n == 13:
                        c_max(u - 1, (2,))
                    if with_a and n in (15, 16, 17):
                        a_best(u + 1, n - 15)
                    if with_c and n == 18:
                        c_norm(u - 1)
                    if with_a and n == 19:
                        chains["a"].sync()
                        a_cut(u + 1)
                    if with_c and n == 22:
                        c_add(u - 1, s - 1)
                    if with_a and n == 23:
                        a_norm(u + 1, 1 - par)
                    if with_a and n == 25:
                        a_low(u + 1, 1 - par)

            def c(u, s, par):
                c_scale(u, par)
                c_max(u, (0, 1, 2))
                c_norm(u)
                c_add(u, s)
                v.sem_inc(head_free, 1)

            for _ in units(v, a, body, c):
                pass

        @block.gpsimd
        def _(g):
            tt = nc.gpsimd.tensor_tensor

            def a_sums(u):
                g.wait_ge(lists_ready, u + 1)
                at = 0
                for i, w in ROWS:
                    tt(cand[:, :, at:at + w], lists[:, :, 0, i:i + 1].broadcast_to((CP, CH, w)),
                       lists[:, :, 1, 0:w], ALU.add)
                    at += w
                tt(cand[:, :, at:at + 6].rearrange("p c (i w) -> p c i w", w=2),
                   lists[:, :, 0, 5:8].unsqueeze(3).broadcast_to((CP, CH, 3, 2)),
                   lists[:, :, 1, 0:2].unsqueeze(2).broadcast_to((CP, CH, 3, 2)), ALU.add)
                tt(cand[:, :, at + 6:at + 14], lists[:, :, 0, 8:16],
                   lists[:, :, 1, 0:1].broadcast_to((CP, CH, 8)), ALU.add).then_inc(sums_ready, 1)

            def a_shift(u):
                g.wait_ge(cut_ready, u + 1)
                tt(S[:, :, 0:NK], S[:, :, 0:NK], cut[:].unsqueeze(2).broadcast_to((CP, CH, NK)), ALU.subtract)\
                    .then_inc(cut_done, 1)

            with g.Fori(0, HEADS * NB) as u:
                a_sums(u)
                a_shift(u)


SCRATCH = {
    "h0": (NB, CP, CH, C), "xn": (NB, CP, CH, C), "xnT": (NB, C, TOK),
    "krev": (C, TOK + CP), "conv": (NB, C, TOK),
    "h1": (NB, CP, CH, C), "x1T": (NB, C, TOK),
    "h2": (NB, CP, CH, C), "x2": (NB, CP, CH, C), "x2T": (NB, C, TOK),
    "h3": (NB, CP, CH, C), "x3T": (NB, C, TOK), "score_w": (HEADS, C, 2 * NK),
    "table": (HEADS, 128, NT4, 128),
}


def program(nc, d):
    for name, shape in SCRATCH.items():
        d[name] = nc.dram_tensor(name, shape, F32, kind="Internal").ap()
    with ExitStack() as Mem.program:
        for stage in (stage_tokens, stage_ssm_kernel, stage_conv, stage_mix, stage_experts, stage_pairs,
                      stage_keys, stage_memory)[:STAGE]:
            stage(nc, d)


def lay_out(np, a):
    con = np.concatenate
    n = {k: np.asarray(v) for k, v in a.items()}
    p = n["x"].reshape(NB, 3, 14, 16, 14, 16).transpose(0, 1, 3, 5, 2, 4).reshape(NB, KT, 128, NIMG)
    two = lambda v: con([v, v])
    re_im = lambda k: con([n[k + "_re"], n[k + "_im"]])
    im_re = lambda k: con([n[k + "_im"], n[k + "_re"]])
    sign = con([np.ones(C), -np.ones(C)]).astype(np.float32)
    A = "L0_attn_"
    par = np.stack([two(n[A + "Lambda_re"]), two(n[A + "Lambda_im"]), re_im(A + "B"), im_re(A + "B"),
                    re_im(A + "P"), im_re(A + "P"), np.broadcast_to(n[A + "step"], (128,)), sign], 1)
    cq = np.stack([con([n[A + "C_" + z].T, n[A + "Q_" + z][:, None]], 1) for z in ("re", "im")], 1)
    l = np.arange(TOK)
    tan = np.tan(np.pi * l / TOK)
    lag = TOK - 1 - l
    ang = 2 * np.pi * ((l[:, None] * lag[None, :]) % TOK) / TOK
    dft = np.stack([np.cos(ang) / TOK, -np.sin(ang) / TOK], 1).reshape(CH, CP, 2, TOK).transpose(1, 0, 2, 3)
    out = {
        "patches": p.transpose(0, 2, 1, 3),
        "txtT": n["txt"].transpose(0, 2, 1),
        "tokW": n["L0_tok_W"].T.reshape(KT, 128, C).transpose(1, 0, 2),
        "tokb": n["L0_tok_b"][:, None],
        "ident": np.eye(128, dtype=np.float32),
        "par": par,
        "cq": con([cq, cq]),
        "tanr": np.broadcast_to(tan.astype(np.float32), (128, TOK)),
        "tanc": tan.astype(np.float32).reshape(CH, CP).T,
        "dft": dft.astype(np.float32),
    }
    row = lambda v: np.broadcast_to(v, (CP, CH, C))
    out["fcT"] = n[A + "W_fc"].T
    out["skipD"] = np.broadcast_to(n[A + "D"], (C, 1))
    out["mix_rows"] = np.stack([row(n[A + k]) for k in ("b_fc", "ln_g", "ln_b")], 1)
    F = "L0_ffn_"
    pad = ((0, 0), (0, NT * HT - HID), (0, 0))
    w1, w3 = (np.pad(n[F + k], pad).transpose(2, 0, 1) for k in ("w1", "w3"))
    out["routerT"] = n[F + "router_w"].T
    out["w13"] = con([w1, w3])
    out["w2"] = np.pad(n[F + "w2"].transpose(0, 2, 1), pad).reshape(E, NT, HT, C).transpose(2, 0, 1, 3)
    out["pick"] = (np.arange(E)[:, None, None] == 2 * np.arange(E // 2)[:, None] + np.arange(128) // C).astype(np.float32)
    P = "L1_attn_"
    wi = n[P + "w_itr_att"]
    mix = np.zeros((C + 1, C + 1), np.float32)
    mix[:C, C] = wi[:C]
    mix[C, :C] = wi[C:2 * C]
    mix[np.arange(C), np.arange(C)] = wi[2 * C:]
    out["pair_mix"] = mix
    w = con([n[P + k] for k in ("w1", "w2", "w3")], 1)
    bias = con([n[P + k] for k in ("b1", "b2", "b3")])
    out["pair_top"] = con([w[:C], bias[None]])
    out["pair_bot"] = w[C:]
    M = "L1_ffn_"
    out["wq_pk"] = n[M + "Wq_pk"].reshape(C, 2, HEADS, DK).transpose(3, 1, 2, 0)
    out["pk_keys"] = n[M + "pk_keys"].transpose(3, 0, 2, 1)
    proj = np.zeros((128, HEADS, 128), np.float32)
    proj[:C, :, :C] = n[M + "Wq"].reshape(C, HEADS, C).transpose(2, 1, 0)
    proj[C:, :, C:] = n[M + "Wo"].reshape(HEADS, C, C).transpose(1, 0, 2)
    out["head_proj"] = proj
    tables = con([n[M + "keys_table"], n[M + "values_table"]], 1)
    out["tableT"] = tables.reshape(HEADS, NT4, 128, 2 * C).transpose(0, 3, 1, 2)
    row, sl, col = np.ogrid[0:128, 0:NT4, 0:128]
    out["key_pick"] = np.where(row < NK, row == col % NK, row - NK == 2 * sl + col // NK).astype(np.float32)
    t = np.arange(TOK)
    out["tri"] = np.where(t[None, None, :] > t.reshape(CH, CP).T[:, :, None], np.float32(HIDDEN), np.float32(0))
    return {k: np.ascontiguousarray(v) for k, v in out.items()}


def kernel(**inputs):
    import numpy as np
    import concourse.bacc as bacc
    from concourse import mybir as mb
    from concourse.bass_utils import run_bass_kernel_spmd as run

    nc = bacc.Bacc("TRN2", target_bir_lowering=False, num_devices=1)
    arrays = {"in_" + k: v for k, v in lay_out(np, inputs).items()}
    d = {k[3:]: nc.dram_tensor(k, v.shape, mb.dt.from_np(v.dtype), kind="ExternalInput").ap()
         for k, v in arrays.items()}
    d["out"] = nc.dram_tensor("out", (NB, TOK, C), mb.dt.float32, kind="ExternalOutput").ap()
    program(nc, d)
    r = run(nc, [arrays], core_ids=[0])
    return r.results[0]["out"]
```

```python
from contextlib import ExitStack

import concourse.bass as bass
from concourse import mybir
from concourse.alu_op_type import AluOpType as ALU

F32 = mybir.dt.float32
F32R = mybir.dt.float32r
ACT = mybir.ActivationFunctionType
AX = mybir.AxisListType

NB = 32
C = 64
NIMG = 196
TOK = 273
NTXT = TOK - NIMG
CP = 91
CH = 3
KT = 6
LN_EPS = 1e-5
W = 4


class Mem:
    program = None

    def __init__(self, nc, stage):
        self.nc, self.stage, self.ctx, self.sems = nc, stage, ExitStack(), []

    def __enter__(self):
        return self

    def __exit__(self, *a):
        done = self.ctx.__exit__(*a)
        self.nc.clear_and_free_semaphores(self.sems)
        self.nc.all_engine_barrier()
        return done

    def sb(self, name, shape, dt=F32):
        return self.ctx.enter_context(self.nc.sbuf_tensor(f"{self.stage}_{name}", shape, dt))

    def ps(self, name, shape, dt=F32):
        return self.ctx.enter_context(self.nc.psum_tensor(f"{self.stage}_{name}", shape, dt))

    def sem(self, name):
        self.sems.append(self.nc.alloc_semaphore(name=f"{self.stage}_{name}"))
        return self.sems[-1]

    def pool_dma_sem(self, name):
        return self.program.enter_context(self.nc.semaphore(f"{self.stage}_{name}"))

    def block(self):
        return self.ctx.enter_context(self.nc.Block())


class Chain:

    def __init__(self, eng, sem, i=0, per=0, done=0):
        self.eng, self.sem, self.i, self.per, self.n = eng, sem, i, per, done

    def step(self, ins):
        self.n += 1
        ins.then_inc(self.sem, 1)

    def sync(self):
        self.eng.wait_ge(self.sem, self.i * self.per + self.n)

    def link(self, ins):
        self.step(ins)
        self.sync()

    def close(self):
        assert self.n == self.per, (self.n, self.per)


class Norm:
    STEPS = 11

    def __init__(self, nc, m, held, name="norm", depth=2):
        self.nc, self.held = nc, held
        self.stats = m.sb(f"{name}_stats", [CP, depth, CH, 6])
        self.mv = m.sb(f"{name}_mv", [CP, depth, CH, 2])
        self.var_ready = m.sem(f"{name}_var_ready")
        self.root_ready = m.sem(f"{name}_root_ready")

    def vector(self, ch, x, out, j, s):
        self.vector_stats(ch, x, j)
        self.vector_var(ch, j)
        self.vector_scale(ch, x, out, j, s)

    def vector_stats(self, ch, x, j):
        for c in range(CH):
            ch.step(self.nc.vector.bn_stats(self.stats[:, j, c, :], x[:, c, :]))

    def vector_var(self, ch, j):
        nc, stats, mv = self.nc, self.stats[:, j], self.mv[:, j]
        ch.sync()
        ch.eng.sem_inc(self.held, 1)
        for c in range(CH):
            ch.step(nc.vector.bn_aggr(mv[:, c, :], stats[:, c, :]))
        ch.sync()
        ch.link(nc.vector.tensor_scalar(mv[:, :, 1], mv[:, :, 1], LN_EPS, None, ALU.add))
        ch.eng.sem_inc(self.var_ready, 1)

    def vector_scale(self, ch, x, out, j, s):
        self.vector_rstd(ch, j, s)
        for c in range(CH):
            self.vector_scale_chunk(ch, x, out, j, c)
        ch.sync()

    def vector_rstd(self, ch, j, s):
        ch.eng.wait_ge(self.root_ready, s + 1)
        sd = self.mv[:, j, :, 1]
        ch.step(self.nc.vector.reciprocal(sd, sd))

    def vector_scale_chunk(self, ch, x, out, j, c):
        if c == 0:
            ch.sync()
        mv = self.mv[:, j, c]
        ch.step(self.nc.vector.tensor_scalar(out[:, c, :], x[:, c, :], mv[:, 0:1], mv[:, 1:2],
                                             ALU.subtract, ALU.mult))

    JOINT = 3 * W * CH + 2

    def vector_var_joint(self, ch, x):
        nc, mv = self.nc, self.mv
        for j in range(W):
            self.vector_stats(ch, x[:, j], j)
        ch.sync()
        ch.eng.sem_inc(self.held, 1)
        for j in range(W):
            for c in range(CH):
                ch.step(nc.vector.bn_aggr(mv[:, j, c, :], self.stats[:, j, c, :]))
        ch.sync()
        ch.link(nc.vector.tensor_scalar(mv[:, :, :, 1], mv[:, :, :, 1], LN_EPS, None, ALU.add))
        ch.eng.sem_inc(self.var_ready, W)

    def vector_scale_joint(self, ch, x, out, s):
        nc, mv = self.nc, self.mv
        ch.eng.wait_ge(self.root_ready, s + W)
        ch.link(nc.vector.reciprocal(mv[:, :, :, 1], mv[:, :, :, 1]))
        for j in range(W):
            for c in range(CH):
                ch.step(nc.vector.tensor_scalar(out[:, j, c, :], x[:, j, c, :], mv[:, j, c, 0:1], mv[:, j, c, 1:2],
                                                ALU.subtract, ALU.mult))
        ch.sync()

    def scalar_joint(self, act, s):
        act.wait_ge(self.var_ready, s + W)
        sd = self.mv[:, :, :, 1]
        self.nc.scalar.activation(sd, sd, ACT.Sqrt).then_inc(self.root_ready, W)

    def scalar(self, act, j, s):
        act.wait_ge(self.var_ready, s + 1)
        sd = self.mv[:, j, :, 1]
        self.nc.scalar.activation(sd, sd, ACT.Sqrt).then_inc(self.root_ready, 1)


def stage_tokens(nc, d):
    with Mem(nc, "tok") as m:
        xp = m.sb("patches", [128, W, KT, NIMG])
        hT = m.sb("hT", [C, W, TOK])
        w = m.sb("w", [128, KT, C])
        b = m.sb("b", [C, 1])
        ident = m.sb("ident", [128, 128])
        h = m.sb("h", [CP, W, CH, C])
        xn = m.sb("xn", [CP, W, CH, C])
        xT = m.sb("xT", [C, W, TOK])
        ps = [m.ps(f"ps{j}", [C, 512]) for j in range(W)]
        ps_h = [p[:, 0:NIMG] for p in ps]
        ps_t = [m.ps(f"ps_t{j}", [CP, CH, C]) for j in range(W)]
        ps_x = [p[:, NIMG:NIMG + TOK] for p in ps]
        held = m.sem("held")
        weights_in = m.sem("weights_in")
        pixels_in = [m.sem(f"pixels_in{j}") for j in range(W)]
        text_in = [m.sem(f"text_in{j}") for j in range(W)]
        embedded = m.sem("embedded")
        hT_ready = m.sem("hT_ready")
        h_turned = m.sem("h_turned")
        h_ready = m.sem("h_ready")
        normed = m.sem("normed")
        x_turned = m.sem("x_turned")
        xT_ready = m.sem("xT_ready")
        stored = [m.pool_dma_sem(f"stored{j}") for j in range(W)]
        out_free = m.sem("out_free")
        dve = m.sem("dve")
        norm = Norm(nc, m, held, depth=W)
        block = m.block()

        @block.sync
        def _(sp):
            sp.dma_start(w[:], d["tokW"]).then_inc(weights_in, 16)
            sp.dma_start(b[:], d["tokb"]).then_inc(weights_in, 16)
            sp.dma_start(ident[:], d["ident"]).then_inc(weights_in, 16)
            with sp.Fori(0, NB // W) as i:
                for j in range(W):
                    s = i * W + j
                    sp.wait_ge(h_turned, s + 1)
                    sp.dma_start(xp[:, j], d["patches"][s]).then_inc(pixels_in[j], 16)
                    sp.dma_start(hT[:, j, NIMG:TOK], d["txtT"][s]).then_inc(text_in[j], 16)

        @block.tensor
        def _(pe):
            pe.sem_inc(h_turned, W)
            pe.sem_inc(x_turned, W)
            pe.wait_ge(weights_in, 48)
            with pe.Fori(0, NB // W) as i:
                for j in range(W):
                    pe.wait_ge(pixels_in[j], i * 16 + 16)
                    pe.wait_ge(hT_ready, i * W + (j + 1))
                    pe.wait_ge(xT_ready, i * W + (j + 1))
                    for k in range(KT):
                        last = nc.tensor.matmul(ps_h[j][:, 0:NIMG], w[:, k, :], xp[:, j, k, :],
                                                start=k == 0, stop=k == KT - 1)
                    last.then_inc(embedded, 1)
                for j in range(W):
                    pe.wait_ge(hT_ready, i * W + (j + W + 1))
                    pe.wait_ge(text_in[j], i * 16 + 16)
                    pe.wait_ge(h_ready, i * W + (j + 1))
                    pe.sem_inc(held, 1)
                    for c in range(CH):
                        last = nc.tensor.transpose(ps_t[j][:, c, :], hT[:, j, c * CP:(c + 1) * CP],
                                                   ident[0:C, 0:C])
                    last.then_inc(h_turned, 1)
                for j in range(W):
                    pe.wait_ge(normed, i * W + (j + 1))
                    pe.wait_ge(xT_ready, i * W + (j + 1))
                    pe.sem_inc(held, 1)
                    for c in range(CH):
                        last = nc.tensor.transpose(ps_x[j][:, c * CP:(c + 1) * CP], xn[:, j, c, :],
                                                   ident[0:CP, 0:CP])
                    last.then_inc(x_turned, 1)

        @block.scalar
        def _(act):
            act.sem_inc(hT_ready, W)
            act.sem_inc(h_ready, W)
            act.sem_inc(xT_ready, W)
            act.wait_ge(weights_in, 48)
            with act.Fori(0, NB // W) as i:
                for j in range(W):
                    act.wait_ge(embedded, i * W + (j + 1))
                    act.wait_ge(h_turned, i * W + (j + 1))
                    nc.scalar.activation(hT[:, j, 0:NIMG], ps_h[j][:, 0:NIMG], ACT.Identity,
                                         bias=b[:, 0:1]).then_inc(hT_ready, 1)
                for j in range(W):
                    act.wait_ge(h_turned, i * W + (j + W + 1))
                    act.wait_ge(out_free, i * W + (j + 1))
                    nc.scalar.activation(h[:, j], ps_t[j][:], ACT.Copy).then_inc(h_ready, 1)
                norm.scalar_joint(act, i * W)
                for j in range(W):
                    act.wait_ge(x_turned, i * W + (j + W + 1))
                    nc.scalar.activation(xT[:, j], ps_x[j][:, 0:TOK], ACT.Copy).then_inc(xT_ready, 1)

        @block.vector
        def _(v):
            with v.Fori(0, NB // W) as i:
                ch = Chain(v, dve, i, Norm.JOINT)
                for j in range(W):
                    v.wait_ge(h_ready, i * W + (j + W + 1))
                    v.wait_ge(out_free, i * W + (j + 1))
                    v.wait_ge(x_turned, i * W + (j + 1))
                norm.vector_var_joint(ch, h)
                norm.vector_scale_joint(ch, h, xn, i * W)
                v.sem_inc(normed, W)
                ch.close()

        @block.gpsimd
        def _(g):
            g.sem_inc(out_free, W)
            with g.Fori(0, NB // W) as i:
                for j in range(W):
                    s = i * W + j
                    g.wait_ge(h_ready, s + W + 1)
                    g.wait_ge(normed, s + 1)
                    g.sem_inc(held, 1)
                    g.dma_start(d["h0"][s], h[:, j]).then_inc(stored[j], 16)
                    g.dma_start(d["xn"][s], xn[:, j]).then_inc(stored[j], 16)
                    g.wait_ge(xT_ready, s + W + 1)
                    g.sem_inc(held, 1)
                    g.dma_start(d["xnT"][s], xT[:, j]).then_inc(stored[j], 16)
                for j in range(W):
                    g.wait_ge(stored[j], i * 48 + 48)
                    g.sem_inc(out_free, 1)


def stage_ssm_kernel(nc, d):
    with Mem(nc, "ssm") as m:
        par = m.sb("par", [128, 8])
        cq = m.sb("cq", [128, 2, C + 1])
        tanr = m.sb("tanr", [128, TOK])
        tanc = m.sb("tanc", [CP, CH])
        dft = m.sb("dft", [CP, CH, 2, TOK])
        g2 = m.sb("g2", [128, 6])
        den = m.sb("den", [128, TOK])
        q = m.sb("q", [128, TOK])
        V = m.sb("V", [128, TOK])
        dim = m.sb("dim", [128, TOK])
        R = m.sb("R", [128, 2, 2, C + 1])
        kk = m.sb("kk", [CP, CH, 2, 2, C + 1])
        w = m.sb("w", [CP, CH, 12])
        y = m.sb("y", [CP, CH, 2, C])
        at = m.sb("at", [CP, CH, 2, C])
        kr = m.sb("kr", [C, TOK + CP])
        ps = [m.ps(f"ps{c}", [CP, 512]) for c in range(CH)]
        psk = m.ps("psk", [C, 512])
        loaded, sums, turned, done, stored, dve = (m.sem(n) for n in
                                                   ("loaded", "sums", "turned", "done", "stored", "dve"))
        made = m.sem("made")
        spectrum = m.sem("spectrum")
        block = m.block()

        @block.sync
        def _(sp):
            for t, n in ((par, "par"), (cq, "cq"), (tanr, "tanr"), (tanc, "tanc"), (dft, "dft")):
                sp.dma_start(t[:], d[n]).then_inc(loaded, 16)
            sp.wait_ge(done, 1)
            sp.dma_start(d["krev"], kr[:]).then_inc(stored, 16)
            sp.wait_ge(stored, 16)

        @block.vector
        def _(v):
            ch = Chain(v, dve)
            tt, ts, stt = nc.vector.tensor_tensor, nc.vector.tensor_scalar, nc.vector.scalar_tensor_tensor
            v.wait_ge(loaded, 80)
            ch.step(nc.vector.memset(kr[:], 0.0))
            ch.link(ts(g2[:, 0:1], par[:, 6:7], 1e-6, None, ALU.max))
            ch.link(nc.vector.reciprocal(g2[:, 1:2], g2[:, 0:1]))
            ch.link(ts(g2[:, 1:2], g2[:, 1:2], 2.0, None, ALU.mult))
            ch.link(ts(dim[:], tanr[:], g2[:, 1:2], par[:, 1:2], ALU.mult, ALU.subtract))
            ch.link(tt(g2[:, 2:3], par[:, 0:1], par[:, 0:1], ALU.mult))
            ch.link(tt(den[:], dim[:], dim[:], ALU.mult))
            ch.link(ts(den[:], den[:], g2[:, 2:3], None, ALU.add))
            ch.link(nc.vector.reciprocal(den[:], den[:]))
            ch.step(ts(q[0:C, :], dim[0:C, :], 0.0, par[0:C, 0:1], ALU.mult, ALU.add))
            ch.step(nc.vector.tensor_copy(q[C:128, :], dim[C:128, :]))
            ch.sync()
            ch.link(stt(V[:], q[:], -1.0, den[:], ALU.mult, ALU.mult))
            for z in range(2):
                a, b = par[:, 2 + 2 * z:3 + 2 * z], par[:, 3 + 2 * z:4 + 2 * z]
                ch.link(tt(g2[:, 3:4], a, par[:, 7:8], ALU.mult))
                ch.step(ts(R[:, z, 0, :], cq[:, 0, :], g2[:, 3:4], None, ALU.mult))
                ch.step(ts(R[:, z, 1, :], cq[:, 0, :], b, None, ALU.mult))
                ch.step(ts(q[:, 0:C + 1], cq[:, 1, :], b, None, ALU.mult))
                ch.sync()
                ch.link(tt(R[:, z, 0, :], R[:, z, 0, :], q[:, 0:C + 1], ALU.subtract))
                ch.link(stt(R[:, z, 1, :], cq[:, 1, :], g2[:, 3:4], R[:, z, 1, :], ALU.mult, ALU.add))
            v.sem_inc(made, 1)
            v.wait_ge(sums, 1)
            for c in range(CH):
                ch.link(nc.vector.tensor_copy(kk[:, c].rearrange("p a b c -> p (a b c)"),
                                              ps[c][:, 0:4 * (C + 1)]))
            k10r, k10i = kk[:, :, 0, 0, C], kk[:, :, 0, 1, C]
            k11r, k11i = kk[:, :, 1, 0, C], kk[:, :, 1, 1, C]
            W = [w[:, :, n] for n in range(12)]
            ch.link(ts(W[0], k11r, 1.0, None, ALU.add))
            ch.step(tt(W[1], W[0], W[0], ALU.mult))
            ch.step(tt(W[2], k11i, k11i, ALU.mult))
            ch.sync()
            ch.link(tt(W[1], W[1], W[2], ALU.add))
            ch.step(nc.vector.reciprocal(W[3], W[1]))
            ch.step(tt(W[4], k10r, W[0], ALU.mult))
            ch.step(tt(W[5], k10i, k11i, ALU.mult))
            ch.step(tt(W[6], k10i, W[0], ALU.mult))
            ch.step(tt(W[7], k10r, k11i, ALU.mult))
            ch.sync()
            ch.step(tt(W[4], W[4], W[5], ALU.add))
            ch.step(tt(W[6], W[6], W[7], ALU.subtract))
            ch.sync()
            ch.step(tt(W[8], W[4], W[3], ALU.mult))
            ch.step(tt(W[9], W[6], W[3], ALU.mult))
            ch.sync()
            ch.step(ts(W[10], W[8], -1.0, None, ALU.mult))
            ch.step(ts(W[11], W[9], -1.0, None, ALU.mult))
            ch.sync()
            for c in range(CH):
                col = lambda n: w[:, c, n:n + 1]
                k01r, k01i = kk[:, c, 1, 0, 0:C], kk[:, c, 1, 1, 0:C]
                ch.step(stt(y[:, c, 0], k01r, col(10), kk[:, c, 0, 0, 0:C], ALU.mult, ALU.add))
                ch.step(stt(y[:, c, 1], k01r, col(11), kk[:, c, 0, 1, 0:C], ALU.mult, ALU.add))
                ch.sync()
                ch.step(stt(y[:, c, 0], k01i, col(9), y[:, c, 0], ALU.mult, ALU.add))
                ch.step(stt(y[:, c, 1], k01i, col(10), y[:, c, 1], ALU.mult, ALU.add))
                ch.sync()
                ch.link(ts(w[:, c, 0:1], tanc[:, c:c + 1], -1.0, None, ALU.mult))
                ch.step(stt(at[:, c, 0], y[:, c, 1], w[:, c, 0:1], y[:, c, 0], ALU.mult, ALU.add))
                ch.step(stt(at[:, c, 1], y[:, c, 0], tanc[:, c:c + 1], y[:, c, 1], ALU.mult, ALU.add))
                ch.sync()
            v.sem_inc(spectrum, 1)
            v.wait_ge(turned, 1)
            ch.link(nc.vector.tensor_copy(kr[:, 0:TOK], psk[:, 0:TOK]))
            v.sem_inc(done, 1)

        @block.tensor
        def _(pe):
            pe.wait_ge(made, 1)
            for c in range(CH):
                last = nc.tensor.matmul(ps[c][:, 0:4 * (C + 1)], V[:, c * CP:(c + 1) * CP],
                                        R[:].rearrange("p a b c -> p (a b c)"), start=True, stop=True)
            last.then_inc(sums, 1)
            pe.wait_ge(spectrum, 1)
            for c in range(CH):
                for z in range(2):
                    last = nc.tensor.matmul(psk[:, 0:TOK], at[:, c, z], dft[:, c, z],
                                            start=(c, z) == (0, 0), stop=(c, z) == (CH - 1, 1))
            last.then_inc(turned, 1)


def stage_conv(nc, d):
    with Mem(nc, "conv") as m:
        G = 8
        NG = C // G
        x = m.sb("x", [CP, NB, CH, C])
        toep = m.sb("toep", [CP, C, TOK])
        y = m.sb("y", [NB, 2, G, TOK])
        ps = [m.ps(f"ps{j}", [NB, 512]) for j in range(8)]
        x_in = m.sem("x_in")
        toep_in = [m.sem(f"toep_in{g}") for g in range(NG)]
        summed, taken, stored = m.sem("summed"), m.sem("taken"), [m.pool_dma_sem(f"stored{j}") for j in range(2)]
        block = m.block()
        krev = d["krev"]

        @block.sync
        def _(sp):
            sp.dma_start(x[:], d["xn"].rearrange("b p c e -> p b c e")).then_inc(x_in, 16)
            for g in range(NG):
                src = krev[g * G:(g + 1) * G, 0:TOK]
                src = bass.AP(tensor=src.tensor, offset=src.offset,
                              ap=[[1, CP], [TOK + CP, G], [1, TOK]])
                sp.dma_start(toep[:, g * G:(g + 1) * G, :], src).then_inc(toep_in[g], 16)

        @block.tensor
        def _(pe):
            pe.wait_ge(x_in, 16)
            for h in range(C):
                if h % G == 0:
                    pe.wait_ge(toep_in[h // G], 16)
                if h >= 8:
                    pe.wait_ge(taken, h - 7)
                for c in range(CH):
                    last = nc.tensor.matmul(ps[h % 8][:, 0:TOK - c * CP], x[:, :, c, h],
                                            toep[:, h, c * CP:TOK], start=c == 0, stop=c == CH - 1)
                last.then_inc(summed, 1)

        @block.scalar
        def _(act):
            for h in range(C):
                g, k = h // G, h % G
                act.wait_ge(summed, h + 1)
                if k == 0 and g >= 2:
                    act.wait_ge(stored[g % 2], g // 2 * 16)
                nc.scalar.activation(y[:, g % 2, k, :], ps[h % 8][:, 0:TOK][:, ::-1], ACT.Copy).then_inc(taken, 1)

        @block.gpsimd
        def _(g_):
            for g in range(NG):
                g_.wait_ge(taken, (g + 1) * G)
                g_.dma_start(d["conv"][:, g * G:(g + 1) * G, :], y[:, g % 2]).then_inc(stored[g % 2], 16)
            for j in range(2):
                g_.wait_ge(stored[j], NG // 2 * 16)


class Tail:

    def __init__(self, nc, m, d, held, ident, names, depth=2):
        self.nc, self.d, self.held, self.ident, self.names, self.depth = nc, d, held, ident, names, depth
        self.h = m.sb("new_h", [CP, depth, CH, C])
        self.x = m.sb("new_x", [CP, depth, CH, C])
        self.xT = m.sb("new_xT", [C, depth, TOK])
        self.ps = m.ps("ps_new_xT", [C, 512])
        self.h_ready = m.sem("new_h_ready")
        self.normed = m.sem("normed")
        self.x_turned = m.sem("x_turned")
        self.xT_ready = m.sem("xT_ready")
        self.stored = [m.pool_dma_sem(f"stored{j}") for j in range(depth)]
        self.out_free = m.sem("out_free")
        self.norm = Norm(nc, m, held, depth=depth)

    def vector_begin(self, v, s):
        v.wait_ge(self.out_free, s + 1)
        v.wait_ge(self.x_turned, s + 1)

    def vector(self, ch, j, s):
        ch.eng.sem_inc(self.h_ready, 1)
        self.norm.vector(ch, self.h[:, j], self.x[:, j], j, s)
        ch.eng.sem_inc(self.normed, 1)

    def tensor_start(self, pe):
        pe.sem_inc(self.x_turned, self.depth)

    def tensor(self, pe, j, s):
        pe.wait_ge(self.normed, s + 1)
        pe.wait_ge(self.xT_ready, s + 1)
        pe.sem_inc(self.held, 1)
        for c in range(CH):
            last = self.nc.tensor.transpose(self.ps[:, c * CP:(c + 1) * CP], self.x[:, j, c, :],
                                            self.ident[0:CP, 0:CP])
        last.then_inc(self.x_turned, 1)

    def scalar_start(self, act):
        act.sem_inc(self.xT_ready, 1)

    def scalar(self, act, j, s):
        act.wait_ge(self.x_turned, s + (self.depth + 1))
        act.wait_ge(self.out_free, s + 1)
        self.nc.scalar.activation(self.xT[:, j], self.ps[:, 0:TOK], ACT.Copy).then_inc(self.xT_ready, 1)

    def store(self, g, j, s):
        hn, xn, xTn = self.names
        g.wait_ge(self.normed, s + 1)
        g.sem_inc(self.held, 1)
        g.dma_start(self.d[hn][s], self.h[:, j]).then_inc(self.stored[j], 16)
        if xn:
            g.dma_start(self.d[xn][s], self.x[:, j]).then_inc(self.stored[j], 16)
        g.wait_ge(self.xT_ready, s + 2)
        g.sem_inc(self.held, 1)
        g.dma_start(self.d[xTn][s], self.xT[:, j]).then_inc(self.stored[j], 16)

    def free(self, g, j, i):
        kinds = 3 if self.names[1] else 2
        g.wait_ge(self.stored[j], i * (16 * kinds) + 16 * kinds)
        g.sem_inc(self.out_free, 1)

    def gpsimd(self, g):
        g.sem_inc(self.out_free, self.depth)
        with g.Fori(0, NB // self.depth) as i:
            for j in range(self.depth):
                self.store(g, j, i * self.depth + j)
            for j in range(self.depth):
                self.free(g, j, i)


def stage_mix(nc, d):
    with Mem(nc, "mix") as m:
        ident = m.sb("ident", [128, 128])
        w = m.sb("w", [C, C])
        D = m.sb("D", [C, 1])
        rows = m.sb("rows", [CP, 3, CH, C])
        hin = m.sb("hin", [CP, W, CH, C])
        xin = m.sb("xin", [CP, W, CH, C])
        xT = m.sb("xT", [C, W, TOK])
        cv = m.sb("cv", [C, W, TOK])
        u = m.sb("u", [C, W, TOK])
        y1 = m.sb("y1", [C, W, TOK])
        t = m.sb("t", [CP, W, CH, C])
        g_ = m.sb("g", [CP, W, CH, C])
        y2 = m.sb("y2", [CP, W, CH, C])
        ps = [m.ps(f"ps_fc{j}", [CP, CH, C]) for j in range(W)]
        held = m.sem("held")
        weights_in = m.sem("weights_in")
        channels_in = [m.sem(f"channels_in{j}") for j in range(W)]
        tokens_in = [m.sem(f"tokens_in{j}") for j in range(W)]
        channels_taken, tokens_taken = m.sem("channels_taken"), m.sem("tokens_taken")
        u_ready, y1_ready, fc_done, t_ready, g_ready = (m.sem(n) for n in (
            "u_ready", "y1_ready", "fc_done", "t_ready", "g_ready"))
        dve = m.sem("dve")
        tail = Tail(nc, m, d, held, ident, ("h1", None, "x1T"), depth=W)
        inner = Norm(nc, m, held, "inner", depth=W)
        block = m.block()

        @block.sync
        def _(sp):
            for a, n in ((ident, "ident"), (w, "fcT"), (D, "skipD"), (rows, "mix_rows")):
                sp.dma_start(a[:], d[n]).then_inc(weights_in, 16)
            with sp.Fori(0, NB // W) as i:
                for j in range(W):
                    s = i * W + j
                    sp.wait_ge(channels_taken, s + 1)
                    sp.dma_start(xT[:, j], d["xnT"][s]).then_inc(channels_in[j], 16)
                    sp.dma_start(cv[:, j], d["conv"][s]).then_inc(channels_in[j], 16)
                for j in range(W):
                    s = i * W + j
                    sp.wait_ge(tokens_taken, s + 1)
                    sp.dma_start(xin[:, j], d["xn"][s]).then_inc(tokens_in[j], 16)
                    sp.dma_start(hin[:, j], d["h0"][s]).then_inc(tokens_in[j], 16)

        @block.vector
        def _(v):
            v.sem_inc(channels_taken, W)
            v.sem_inc(tokens_taken, W)
            v.wait_ge(weights_in, 64)
            with v.Fori(0, NB // W) as i:
                ch = Chain(v, dve, i, W * 5 + 1 + 2 * Norm.JOINT)
                for j in range(W):
                    v.wait_ge(channels_in[j], i * 32 + 32)
                    v.wait_ge(y1_ready, i * W + (j + 1))
                    ch.link(nc.vector.scalar_tensor_tensor(u[:, j], xT[:, j], D[:, 0:1], cv[:, j],
                                                           ALU.mult, ALU.add))
                    v.sem_inc(u_ready, 1)
                    v.sem_inc(channels_taken, 1)
                for j in range(W):
                    v.wait_ge(fc_done, i * W + (j + 1))
                    v.wait_ge(g_ready, i * W + (j + 1))
                    ch.link(nc.vector.tensor_tensor(t[:, j], ps[j][:], rows[:, 0], ALU.add))
                    v.sem_inc(t_ready, 1)
                for j in range(W):
                    v.wait_ge(g_ready, i * W + (j + W + 1))
                    v.wait_ge(tokens_in[j], i * 32 + 32)
                    ch.step(nc.vector.tensor_tensor(y2[:, j], g_[:, j], xin[:, j], ALU.add))
                ch.sync()
                inner.vector_var_joint(ch, y2)
                inner.vector_scale_joint(ch, y2, y2, i * W)
                for j in range(W):
                    tail.vector_begin(v, i * W + j)
                for k, op in ((1, ALU.mult), (2, ALU.add)):
                    for j in range(W):
                        ch.step(nc.vector.tensor_tensor(y2[:, j], y2[:, j], rows[:, k], op))
                    ch.sync()
                ch.link(nc.vector.tensor_tensor(tail.h[:], y2[:], hin[:], ALU.add))
                v.sem_inc(tokens_taken, W)
                v.sem_inc(tail.h_ready, W)
                tail.norm.vector_var_joint(ch, tail.h)
                tail.norm.vector_scale_joint(ch, tail.h, tail.x, i * W)
                v.sem_inc(tail.normed, W)
                ch.close()

        @block.scalar
        def _(act):
            act.sem_inc(y1_ready, W)
            act.sem_inc(g_ready, W)
            tail.scalar_start(act)
            with act.Fori(0, NB // W) as i:
                for j in range(W):
                    act.wait_ge(u_ready, i * W + (j + 1))
                    nc.scalar.activation(y1[:, j], u[:, j], ACT.Gelu).then_inc(y1_ready, 1)
                for j in range(W):
                    act.wait_ge(t_ready, i * W + (j + 1))
                    nc.scalar.activation(g_[:, j], t[:, j], ACT.Gelu).then_inc(g_ready, 1)
                inner.scalar_joint(act, i * W)
                tail.norm.scalar_joint(act, i * W)
                for j in range(W):
                    tail.scalar(act, j, i * W + j)

        @block.tensor
        def _(pe):
            tail.tensor_start(pe)
            pe.wait_ge(weights_in, 64)
            with pe.Fori(0, NB // W) as i:
                for j in range(W):
                    pe.wait_ge(y1_ready, i * W + (j + W + 1))
                    pe.sem_inc(held, 1)
                    for c in range(CH):
                        last = nc.tensor.matmul(ps[j][:, c, :], y1[:, j, c * CP:(c + 1) * CP], w[:],
                                                start=True, stop=True)
                    last.then_inc(fc_done, 1)
                for j in range(W):
                    tail.tensor(pe, j, i * W + j)

        @block.gpsimd
        def _(g):
            tail.gpsimd(g)


E = 8
HID = 682
HT = 114
NT = 6
GB = 8


def stage_gates(nc, d):
    with Mem(nc, "gates") as m:
        G3 = GB * CH
        ident = m.sb("ident", [128, 128])
        router = m.sb("router", [C, E])
        x = m.sb("x", [C, 2, GB, TOK])
        top = m.sb("top", [CP, G3, 8])
        logit = m.sb("logit", [CP, G3, E])
        ex = m.sb("ex", [CP, G3, E])
        mask = m.sb("mask", [CP, G3, E])
        gate = m.sb("gate", [CP, 2, G3, E])
        s1 = m.sb("s1", [CP, G3])
        gT = m.sb("gT", [E, 2, GB, TOK])
        ps_l = [m.ps(f"ps_l{j}", [CP, 512]) for j in range(2)]
        ps_t = [m.ps(f"ps_t{k}", [E, 512]) for k in range(4)]
        held = m.sem("held")
        consts_in = m.sem("consts_in")
        loaded = [m.sem(f"loaded{j}") for j in range(2)]
        routed, lifted, ex_ready, gate_ready, turned, copied, blocks_turned, dve = (m.sem(n) for n in (
            "routed", "lifted", "ex_ready", "gate_ready", "turned", "copied", "blocks_turned", "dve"))
        stored = [m.pool_dma_sem(f"stored{j}") for j in range(2)]
        out_free = m.sem("out_free")
        block = m.block()

        @block.sync
        def _(sp):
            sp.dma_start(ident[:], d["ident"]).then_inc(consts_in, 16)
            sp.dma_start(router[:], d["routerT"]).then_inc(consts_in, 16)
            with sp.Fori(0, NB // GB // 2) as i:
                for j in range(2):
                    sp.wait_ge(routed, i * 2 + (j + 1))
                    for k in range(GB):
                        sp.dma_start(x[:, j, k], d["x1T"][i * (2 * GB) + (j * GB + k)]).then_inc(loaded[j], 16)

        @block.tensor
        def _(pe):
            pe.sem_inc(routed, 2)
            pe.wait_ge(consts_in, 32)

            def route(b, i, j):
                pe.wait_ge(loaded[j], i * (16 * GB) + 16 * GB)
                pe.wait_ge(lifted, b + 1)
                pe.sem_inc(held, 1)
                for k in range(GB):
                    for c in range(CH):
                        n = k * CH + c
                        last = nc.tensor.matmul(ps_l[j][:, n * E:(n + 1) * E], x[:, j, k, c * CP:(c + 1) * CP],
                                                router[:], start=True, stop=True)
                last.then_inc(routed, 1)

            with pe.Fori(0, NB // GB // 2) as i:
                for j in range(2):
                    route(i * 2 + j, i, j)
                for j in range(2):
                    b = i * 2 + j
                    pe.wait_ge(gate_ready, b + 1)
                    for k in range(GB):
                        pe.wait_ge(copied, b * GB + (k + 1))
                        pe.sem_inc(held, 1)
                        for c in range(CH):
                            last = nc.tensor.transpose(ps_t[k % 4][:, c * CP:(c + 1) * CP],
                                                       gate[:, j, k * CH + c, :], ident[0:CP, 0:CP])
                        last.then_inc(turned, 1)

        @block.scalar
        def _(act):
            act.sem_inc(copied, 4)
            act.sem_inc(blocks_turned, 2)
            with act.Fori(0, NB // GB // 2) as i:
                for j in range(2):
                    act.wait_ge(lifted, i * 2 + (j + 3))
                    nc.scalar.activation(ex[:], logit[:], ACT.Exp).then_inc(ex_ready, 1)
                for j in range(2):
                    act.wait_ge(out_free, i * 2 + (j + 1))
                    for k in range(GB):
                        act.wait_ge(turned, i * (2 * GB) + (j * GB + k + 1))
                        nc.scalar.activation(gT[:, j, k], ps_t[k % 4][:, 0:TOK], ACT.Copy).then_inc(copied, 1)
                    act.sem_inc(blocks_turned, 1)

        @block.vector
        def _(v):
            tt, ts = nc.vector.tensor_tensor, nc.vector.tensor_scalar
            v.sem_inc(lifted, 2)
            wide = lambda a: a.unsqueeze(2).broadcast_to((CP, G3, E))
            with v.Fori(0, NB // GB // 2) as i:
                ch = Chain(v, dve, i, 2 * (1 + G3 + 10))
                for j in range(2):
                    v.wait_ge(routed, i * 2 + (j + 3))
                    ch.link(nc.vector.tensor_copy(logit[:].rearrange("p c e -> p (c e)"), ps_l[j][:, 0:G3 * E]))
                    v.sem_inc(held, 1)
                    for n in range(G3):
                        ch.step(nc.vector.max(top[:, n, :], logit[:, n, :]))
                    ch.sync()
                    ch.link(tt(mask[:], logit[:], wide(top[:, :, 1]), ALU.is_ge))
                    ch.link(tt(logit[:], logit[:], wide(top[:, :, 0]), ALU.subtract))
                    v.sem_inc(lifted, 1)
                    v.wait_ge(ex_ready, i * 2 + (j + 1))
                    v.wait_ge(blocks_turned, i * 2 + (j + 1))
                    ch.link(nc.vector.tensor_reduce(s1[:], ex[:], AX.X, ALU.add))
                    ch.link(nc.vector.reciprocal(s1[:], s1[:]))
                    ch.link(tt(ex[:], ex[:], wide(s1[:]), ALU.mult))
                    ch.link(tt(ex[:], ex[:], mask[:], ALU.mult))
                    ch.link(nc.vector.tensor_reduce(s1[:], ex[:], AX.X, ALU.add))
                    ch.link(ts(s1[:], s1[:], 1e-9, None, ALU.add))
                    ch.link(nc.vector.reciprocal(s1[:], s1[:]))
                    ch.link(tt(gate[:, j], ex[:], wide(s1[:]), ALU.mult))
                    v.sem_inc(gate_ready, 1)
                ch.close()

        @block.gpsimd
        def _(g):
            g.sem_inc(out_free, 2)
            with g.Fori(0, NB // GB // 2) as i:
                for j in range(2):
                    for k in range(GB):
                        g.wait_ge(copied, i * (2 * GB) + (j * GB + k + 5))
                        g.sem_inc(held, 1)
                        to = d["gates"][i * (2 * GB) + (j * GB + k)].rearrange("q h t -> (q h) t")
                        g.dma_start(to, gT[:, j, k]).then_inc(stored[j], 16)
                for j in range(2):
                    g.wait_ge(stored[j], i * (16 * GB) + 16 * GB)
                    g.sem_inc(out_free, 1)


def stage_experts(nc, d):
    with Mem(nc, "moe") as m:
        TILES = E * NT
        Q = E // 2
        HALF = TILES // 2
        ident = m.sb("ident", [128, 128])
        RAW = 4
        raw = m.sb("raw", [128, RAW, 2, NT * HT])
        high = [m.sb(f"high{k}", [128, E, NT * HT], F32R) for k in (1, 3)]
        low = [m.sb(f"low{k}", [128, E, NT * HT], F32R) for k in (1, 3)]
        w2 = m.sb("w2", [HT, E, NT, C])
        x = m.sb("x", [128, 2, TOK])
        X = m.sb("X", [128, 2, TOK + 1], F32R)
        hin = m.sb("hin", [CP, 2, CH, C])
        G = m.sb("G", [128, 2, Q, TOK])
        sg = m.sb("sg", [HT, 2, TOK])
        hh = m.sb("hh", [HT, 4, TOK])
        ty = m.sb("ty", [128, TOK])
        acc = m.sb("acc", [128, 2, TOK])
        ps1 = [m.ps(f"ps1{k}", [HT, 512]) for k in range(2)]
        ps3 = [m.ps(f"ps3{k}", [HT, 512]) for k in range(2)]
        psy = [m.ps(f"psy{k}", [128, 512]) for k in range(2)]
        psg = m.ps("psg", [128, 512])
        held = m.sem("held")
        weights_in = m.sem("weights_in")
        raw_in = [[m.sem(f"raw_in{k}{b}") for b in range(RAW)] for k in range(2)]
        x_in = [m.sem(f"x_in{j}") for j in range(2)]
        rest_in = [m.sem(f"rest_in{j}") for j in range(2)]
        names = ("high_ready", "split", "x_high", "X_ready", "up1_done", "up3_done", "sg_ready", "hh_ready",
                 "down_done", "y_taken", "acc_ready", "acc_turned", "acc_taken")
        (high_ready, split, x_high, X_ready, up1_done, up3_done, sg_ready, hh_ready, down_done, y_taken,
         acc_ready, acc_turned, acc_taken) = (m.sem(n) for n in names)
        dve_y, dve_t = m.sem("dve_y"), m.sem("dve_t")
        tail = Tail(nc, m, d, held, ident, ("h2", "x2", "x2T"))
        block = m.block()

        def place(n):
            q, r = divmod(n, 2 * NT)
            return 2 * q + r % 2, r // 2

        def samples(eng, sample, end):
            sample(0, 0, 0, False)
            sample(0, 1, 1, True)
            with eng.Fori(1, NB // 2) as i:
                for j in range(2):
                    sample(i, j, i * 2 + j, True)
            end(NB - 1, 1)

        @block.sync
        def _(sp):
            sp.dma_start(ident[:], d["ident"]).then_inc(weights_in, 16)
            for e in range(E):
                for k in range(2):
                    if e >= RAW:
                        sp.wait_ge(split, 2 * (e - RAW) + 1 + k)
                    for half in range(2):
                        sp.dma_start(raw[half * C:half * C + C, e % RAW, k], d[("w1T", "w3T")[k]][:, e])\
                            .then_inc(raw_in[k][e % RAW], 16)
            sp.dma_start(w2[:], d["w2"]).then_inc(weights_in, 16)
            with sp.Fori(0, NB // 2) as i:
                for j in range(2):
                    s = i * 2 + j
                    sp.wait_ge(X_ready, s + 1)
                    for half in range(2):
                        sp.dma_start(x[half * C:half * C + C, j], d["x1T"][s]).then_inc(x_in[j], 16)
                    sp.wait_ge(acc_taken, s + 1)
                    sp.dma_start(hin[:, j], d["h1"][s]).then_inc(rest_in[j], 16)
                    for half in range(2):
                        sp.dma_start(G[half * C:half * C + C, j],
                                     d["gates"][s][:, half].unsqueeze(0).broadcast_to((C, Q, TOK)))\
                            .then_inc(rest_in[j], 16)

        @block.tensor
        def _(pe):
            tail.tensor_start(pe)
            pe.wait_ge(weights_in, 32)
            pe.wait_ge(split, 2 * E)

            def up(s, j, n):
                e, t = place(n)
                cols = slice(t * HT, (t + 1) * HT)
                for k, ps, free, off in ((0, ps1, sg_ready, 1), (1, ps3, hh_ready, 3)):
                    pe.wait_ge(free, s * TILES + (n + off))
                    nc.tensor.matmul(ps[n % 2][:, 0:TOK + 1], high[k][:, e, cols], X[:, j], start=True, stop=False)
                    nc.tensor.matmul(ps[n % 2][:, 0:TOK + 1], low[k][:, e, cols], X[:, j], start=False, stop=True)\
                        .then_inc((up1_done, up3_done)[k], 1)

            def down(s, n):
                q = n // (2 * NT)
                if n % (2 * NT) == 0:
                    pe.wait_ge(y_taken, s * Q + (q + 1))
                pe.wait_ge(hh_ready, s * TILES + (n + 6))
                for p in range(2):
                    e, t = place(n + p)
                    last = nc.tensor.matmul(psy[q % 2][p * C:p * C + C, 0:TOK], w2[:, e, t, :], hh[:, (n + p) % 4],
                                            start=t == 0, stop=t == NT - 1)
                last.then_inc(down_done, 1)

            def turn_sums(s, j):
                pe.wait_ge(acc_ready, s + 1)
                pe.wait_ge(acc_taken, s + 2)
                pe.sem_inc(held, 1)
                for c in range(CH):
                    last = nc.tensor.transpose(psg[0:CP, c * 128:(c + 1) * 128],
                                               acc[:, j, c * CP:(c + 1) * CP], ident[:, :])
                last.then_inc(acc_turned, 1)

            def sample(i, j, s, behind):
                pe.wait_ge(X_ready, s + 3)
                for n in range(0, TILES, 2):
                    up(s, j, n)
                    up(s, j, n + 1)
                    if n:
                        down(s, n - 2)
                    elif behind:
                        down(s - 1, TILES - 2)
                    if behind and n == 6:
                        turn_sums(s - 1, 1 - j)
                    if behind and n == 24:
                        tail.tensor(pe, 1 - j, s - 1)

            def end(s, j):
                down(s, TILES - 2)
                turn_sums(s, j)
                tail.tensor(pe, j, s)

            samples(pe, sample, end)

        @block.scalar
        def _(act):
            tail.scalar_start(act)
            for e in range(E):
                for k in range(2):
                    act.wait_ge(raw_in[k][e % RAW], e // RAW * 32 + 32)
                    nc.scalar.activation(high[k][:, e], raw[:, e % RAW, k], ACT.Copy).then_inc(high_ready, 1)
            act.sem_inc(sg_ready, 2)

            def sample(i, j, s, behind):
                for n in range(TILES):
                    act.wait_ge(up1_done, s * TILES + (n + 1))
                    act.wait_ge(hh_ready, s * TILES + (n + 3))
                    nc.scalar.activation(sg[:, n % 2], ps1[n % 2][:, 0:TOK], ACT.Silu).then_inc(sg_ready, 1)
                    if behind and n == 14:
                        tail.norm.scalar(act, 1 - j, s - 1)
                    if behind and n == 27:
                        tail.scalar(act, 1 - j, s - 1)

            def end(s, j):
                tail.norm.scalar(act, j, s)
                tail.scalar(act, j, s)

            samples(act, sample, end)

        @block.vector
        def _(v):
            tt = nc.vector.tensor_tensor
            for e in range(E):
                for k in range(2):
                    v.wait_ge(high_ready, 2 * e + k + 1)
                    tt(low[k][:, e], raw[:, e % RAW, k], high[k][:, e].bitcast(F32), ALU.subtract).then_inc(split, 1)
            v.sem_inc(hh_ready, 4)
            v.sem_inc(y_taken, 2)
            v.sem_inc(down_done, 2)
            v.sem_inc(acc_taken, 2)
            chains = {}

            def take(s, j, q, part):
                ch = Chain(v, dve_y, s, 2 * Q - 1, done=max(2 * q - 1 + part, 0))
                if part == 0:
                    v.wait_ge(down_done, s * HALF + ((q + 1) * NT + 2))
                    ch.step(tt(ty[:] if q else acc[:, j], psy[q % 2][:, 0:TOK], G[:, j, q], ALU.mult))
                elif q:
                    ch.sync()
                    v.sem_inc(y_taken, 1)
                    ch.step(tt(acc[:, j], acc[:, j], ty[:], ALU.add))
                else:
                    ch.n += 1
                    ch.sync()
                    v.sem_inc(y_taken, 1)
                if (q, part) == (Q - 1, 1):
                    ch.sync()
                    v.sem_inc(acc_ready, 1)

            def add(s, j, half):
                both = psg[0:CP, 0:CH * 128].rearrange("p (c h e) -> p c h e", c=CH, h=2)
                if half == 0:
                    chains["t"] = Chain(v, dve_t, s, 2 + Norm.STEPS)
                    v.wait_ge(acc_turned, s + 1)
                    tail.vector_begin(v, s)
                    chains["t"].step(tt(tail.h[:, j], both[:, :, 0, :], hin[:, j], ALU.add))
                else:
                    chains["t"].sync()
                    chains["t"].link(tt(tail.h[:, j], both[:, :, 1, :], tail.h[:, j], ALU.add))
                    v.sem_inc(acc_taken, 1)
                    v.sem_inc(tail.h_ready, 1)

            def scale(s, j, c):
                tail.norm.vector_scale_chunk(chains["t"], tail.h[:, j], tail.x[:, j], j, c)
                if c == CH - 1:
                    chains["t"].sync()
                    v.sem_inc(tail.normed, 1)
                    chains["t"].close()

            def sample(i, j, s, behind):
                v.wait_ge(rest_in[j], i * 48 + 48)
                for n in range(TILES):
                    v.wait_ge(up3_done, s * TILES + (n + 1))
                    v.wait_ge(sg_ready, s * TILES + (n + 3))
                    if n % 2 == 0:
                        v.wait_ge(down_done, s * HALF + (n // 2 + 1))
                    tt(hh[:, n % 4], sg[:, n % 2], ps3[n % 2][:, 0:TOK], ALU.mult).then_inc(hh_ready, 1)
                    if behind and n in (2, 4):
                        take(s - 1, 1 - j, Q - 1, n // 2 - 1)
                    if behind and n in (8, 9):
                        add(s - 1, 1 - j, n - 8)
                    if behind and n == 10:
                        tail.norm.vector_stats(chains["t"], tail.h[:, 1 - j], 1 - j)
                    if behind and n == 11:
                        tail.norm.vector_var(chains["t"], 1 - j)
                    if behind and n == 19:
                        tail.norm.vector_rstd(chains["t"], 1 - j, s - 1)
                    if behind and n in (20, 21, 22):
                        scale(s - 1, 1 - j, n - 20)
                    if n > 12 and n % 12 in (2, 4):
                        take(s, j, n // 12 - 1, n % 12 // 2 - 1)

            def end(s, j):
                for part in range(2):
                    take(s, j, Q - 1, part)
                for half in range(2):
                    add(s, j, half)
                tail.norm.vector_stats(chains["t"], tail.h[:, j], j)
                tail.norm.vector_var(chains["t"], j)
                tail.norm.vector_rstd(chains["t"], j, s)
                for c in range(CH):
                    scale(s, j, c)

            samples(v, sample, end)

        @block.gpsimd
        def _(g):
            nc.gpsimd.memset(X[:].bitcast(F32), 0.0).then_inc(x_high, 1)
            g.sem_inc(tail.out_free, 2)
            g.sem_inc(X_ready, 2)
            g.wait_ge(x_high, 1)

            def sample(i, j, s, behind):
                first = type(i) is int
                g.wait_ge(x_in[j], i * 32 + 32)
                if not first:
                    g.wait_ge(up3_done, (s - 1) * TILES)
                g.sem_inc(held, 1)
                nc.gpsimd.tensor_copy(X[:, j, 0:TOK], x[:, j]).then_inc(x_high, 1)
                g.wait_ge(x_high, s + 2)
                nc.gpsimd.tensor_tensor(X[C:128, j, 0:TOK], x[C:128, j], X[C:128, j, 0:TOK].bitcast(F32),
                                        ALU.subtract).then_inc(X_ready, 1)
                g.wait_ge(X_ready, s + 3)
                if not first:
                    tail.store(g, j, s - 2)
                    tail.free(g, j, i - 1)

            def end(s, j):
                for j in range(2):
                    tail.store(g, j, NB - 2 + j)
                    tail.free(g, j, NB // 2 - 1)

            samples(g, sample, end)


def stage_pairs(nc, d):
    with Mem(nc, "pair") as m:
        K1 = C + 1
        IN = 4
        ident = m.sb("ident", [128, 128])
        mix = m.sb("mix", [K1, K1])
        wtop = m.sb("wtop", [K1, 3 * C])
        wbot = m.sb("wbot", [C, 3 * C])
        xT = m.sb("xT", [K1, IN, TOK])
        x = m.sb("x", [CP, IN, CH, C])
        hin = m.sb("hin", [CP, IN, CH, C])
        L = m.sb("L", [K1, TOK])
        mx = m.sb("mx", [CP, 2, CH])
        sm = m.sb("sm", [CP, 2, CH])
        ex = m.sb("ex", [CP, 2, CH, TOK])
        AT = m.sb("AT", [CP, CH, TOK])
        it = m.sb("it", [C, TOK])
        zr = m.sb("zr", [CP, CH, 3 * C])
        t1 = m.sb("t1", [CP, CH, C])
        t2 = m.sb("t2", [CP, CH, C])
        spare = m.sb("spare", [1, 2])
        psA = [m.ps(f"psA{c}", [CP, 512]) for c in range(CH)]
        psT = [m.ps(f"psT{c}", [CP, 512]) for c in range(CH)]
        psL = m.ps("psL", [K1, 512])
        held = m.sem("held")
        weights_in = m.sem("weights_in")
        loaded = [m.sem(f"loaded{b}") for b in range(IN)]
        (taken, ones, left_done, left_ready, A_done, max_ready, ex_ready, probs_ready, probs_turned, AT_ready,
         it_done, it_ready, gates_done, gates_ready, mixed) = (m.sem(n) for n in (
             "taken", "ones", "left_done", "left_ready", "A_done", "max_ready", "ex_ready", "probs_ready",
             "probs_turned", "AT_ready", "it_done", "it_ready", "gates_done", "gates_ready", "mixed"))
        dve_f, dve_b, dve_v, dve_t = (m.sem(n) for n in ("dve_f", "dve_b", "dve_v", "dve_t"))
        tail = Tail(nc, m, d, held, ident, ("h3", None, "x3T"), depth=IN)
        block = m.block()
        chunk = lambda c: slice(c * CP, (c + 1) * CP)

        def samples(eng, front, body, end):
            front(0, 0, 0)
            body(0, 0, 0, 0)
            body(1, 1, 0, 1)
            with eng.Fori(0, NB // IN - 1) as i:
                for k in range(2, IN + 2):
                    body(i * IN + k, k % IN, i + k // IN, 2)
            for s in range(NB - IN + 2, NB):
                body(s, s % IN, s // IN, 2)
            end()

        @block.sync
        def _(sp):
            for a, n in ((ident, "ident"), (mix, "pair_mix"), (wtop, "pair_top"), (wbot, "pair_bot")):
                sp.dma_start(a[:], d[n]).then_inc(weights_in, 16)
            with sp.Fori(0, NB // IN) as i:
                for b in range(IN):
                    s = i * IN + b
                    sp.wait_ge(taken, s + 1)
                    sp.dma_start(xT[0:C, b], d["x2T"][s]).then_inc(loaded[b], 16)
                    sp.dma_start(x[:, b], d["x2"][s]).then_inc(loaded[b], 16)
                    sp.dma_start(hin[:, b], d["h2"][s]).then_inc(loaded[b], 16)

        @block.tensor
        def _(pe):
            tail.tensor_start(pe)
            pe.wait_ge(weights_in, 64)
            pe.wait_ge(ones, 1)

            def left(s, b, g):
                pe.wait_ge(loaded[b], g * 48 + 48)
                pe.wait_ge(it_ready, s + 1)
                pe.sem_inc(held, 1)
                nc.tensor.matmul(psL[:, 0:TOK], mix[:], xT[:, b], start=True, stop=True).then_inc(left_done, 1)

            def scores(s, b):
                pe.wait_ge(left_ready, s + 1)
                pe.wait_ge(ex_ready, s + 1)
                for c in range(CH):
                    last = nc.tensor.matmul(psA[c][:, 0:TOK], L[:, chunk(c)], xT[:, b], start=True, stop=True)
                last.then_inc(A_done, 1)

            def front(s, b, g):
                left(s, b, g)
                scores(s, b)

            def body(s, b, g, lag):
                more = not (type(s) is int and s == NB - 1)
                if more:
                    left(s + 1, (b + 1) % IN, g + (b + 1) // IN)
                pe.wait_ge(probs_ready, s + 1)
                pe.wait_ge(gates_ready, s + 1)
                pe.sem_inc(held, 1)
                for jc in range(CH):
                    for c in range(CH):
                        last = nc.tensor.transpose(psT[jc][:, chunk(c)], ex[:, b % 2, c, chunk(jc)],
                                                   ident[0:CP, 0:CP])
                    last.then_inc(probs_turned, 1)
                if more:
                    scores(s + 1, (b + 1) % IN)
                if lag == 2:
                    tail.tensor(pe, (b + 2) % IN, s - 2)
                for jc in range(CH):
                    pe.wait_ge(AT_ready, s * 3 + (jc + 1))
                    last = nc.tensor.matmul(psL[0:C, 0:TOK], x[:, b, jc, :], AT[:, jc, :],
                                            start=jc == 0, stop=jc == CH - 1)
                last.then_inc(it_done, 1)
                pe.wait_ge(it_ready, s + 3)
                pe.sem_inc(held, 1)
                for c in range(CH):
                    nc.tensor.matmul(psT[c][:, 0:3 * C], xT[:, b, chunk(c)], wtop[:], start=True, stop=False)
                    last = nc.tensor.matmul(psT[c][:, 0:3 * C], it[:, chunk(c)], wbot[:], start=False, stop=True)
                last.then_inc(gates_done, 1)

            def end():
                for s in (NB - 2, NB - 1):
                    tail.tensor(pe, s % IN, s)

            samples(pe, front, body, end)

        @block.scalar
        def _(act):
            act.sem_inc(it_ready, 2)
            act.sem_inc(gates_ready, 1)
            act.sem_inc(ex_ready, 1)
            tail.scalar_start(act)

            def left(s):
                act.wait_ge(left_done, s + 1)
                nc.scalar.activation(L[:], psL[:, 0:TOK], ACT.Copy).then_inc(left_ready, 1)

            def softmax(s, j):
                act.wait_ge(max_ready, s + 1)
                for c in range(CH):
                    last = nc.scalar.activation(ex[:, j, c, :], psA[c][:, 0:TOK], ACT.Exp,
                                                bias=mx[:, j, c:c + 1], accum_out=sm[:, j, c:c + 1])
                last.then_inc(ex_ready, 1)

            def front(s, b, g):
                left(s)
                softmax(s, b % 2)

            def body(s, b, g, lag):
                more = not (type(s) is int and s == NB - 1)
                if more:
                    left(s + 1)
                for jc in range(CH):
                    act.wait_ge(probs_turned, s * 3 + (jc + 1))
                    nc.scalar.activation(AT[:, jc, :], psT[jc][:, 0:TOK], ACT.Copy).then_inc(AT_ready, 1)
                act.wait_ge(it_done, s + 1)
                nc.scalar.activation(it[:], psL[0:C, 0:TOK], ACT.Copy).then_inc(it_ready, 1)
                if more:
                    softmax(s + 1, (b + 1) % 2)
                if lag == 2:
                    tail.scalar(act, (b + 2) % IN, s - 2)
                act.wait_ge(gates_done, s + 1)
                act.wait_ge(mixed, s + 1)
                for c in range(CH):
                    nc.scalar.activation(zr[:, c, 0:C], psT[c][:, 0:C], ACT.Tanh)
                    last = nc.scalar.activation(zr[:, c, C:3 * C], psT[c][:, C:3 * C], ACT.Tanh, scale=0.5)
                last.then_inc(gates_ready, 1)
                if lag:
                    tail.norm.scalar(act, (b + 1) % 2, s - 1)
                    nc.scalar.activation(spare[:, 0:1], spare[:, 1:2], ACT.Exp)

            def end():
                tail.norm.scalar(act, (NB - 1) % 2, NB - 1)
                for s in (NB - 2, NB - 1):
                    tail.scalar(act, s % IN, s)

            samples(act, front, body, end)

        @block.vector
        def _(v):
            tt, ts = nc.vector.tensor_tensor, nc.vector.tensor_scalar
            nc.vector.memset(spare[:], 0.0)
            nc.vector.memset(xT[C:K1], 1.0).then_inc(ones, 1)
            v.sem_inc(taken, IN)
            v.sem_inc(mixed, 1)
            v.wait_ge(weights_in, 64)
            chains = {}

            def maxima(s, j):
                chains["f"] = ch = Chain(v, dve_f, s, 3 + 1 + 1 + 3)
                v.wait_ge(A_done, s + 1)
                for c in range(CH):
                    ch.step(nc.vector.tensor_reduce(mx[:, j, c:c + 1], psA[c][:, 0:TOK], AX.X, ALU.max))
                ch.sync()
                ch.link(ts(mx[:, j], mx[:, j], -1.0, None, ALU.mult))
                v.sem_inc(max_ready, 1)

            def probs(s, j):
                ch = chains["f"]
                v.wait_ge(ex_ready, s + 2)
                ch.link(nc.vector.reciprocal(sm[:, j], sm[:, j]))
                for c in range(CH):
                    ch.step(ts(ex[:, j, c, :], ex[:, j, c, :], sm[:, j, c:c + 1], None, ALU.mult))
                ch.sync()
                ch.close()
                v.sem_inc(probs_ready, 1)

            def combine(s, b):
                ch = Chain(v, dve_b, s, 5)
                v.wait_ge(gates_ready, s + 2)
                tail.vector_begin(v, s)
                ch.link(ts(zr[:, :, C:3 * C], zr[:, :, C:3 * C], 0.5, 0.5, ALU.mult, ALU.add))
                ch.step(tt(t1[:], zr[:, :, C:2 * C], x[:, b], ALU.mult))
                ch.step(tt(t2[:], zr[:, :, 2 * C:3 * C], zr[:, :, 0:C], ALU.mult))
                ch.sync()
                ch.link(tt(t1[:], t1[:], hin[:, b], ALU.add))
                ch.link(tt(tail.h[:, b], t1[:], t2[:], ALU.add))
                ch.close()
                v.sem_inc(mixed, 1)
                v.sem_inc(taken, 1)

            def front(s, b, g):
                maxima(s, b % 2)
                probs(s, b % 2)

            def body(s, b, g, lag):
                more = not (type(s) is int and s == NB - 1)
                if more:
                    maxima(s + 1, (b + 1) % 2)
                    probs(s + 1, (b + 1) % 2)
                combine(s, b)
                begin_norm(s, b)
                if lag:
                    end_norm(s - 1, (b + 3) % IN)

            def begin_norm(s, b):
                ch = Chain(v, dve_v, s, 2 * CH + 1)
                tail.norm.vector_stats(ch, tail.h[:, b], b % 2)
                tail.norm.vector_var(ch, b % 2)
                ch.close()

            def end_norm(s, b):
                ch = Chain(v, dve_t, s, CH + 1)
                tail.norm.vector_scale(ch, tail.h[:, b], tail.x[:, b], b % 2, s)
                ch.close()
                v.sem_inc(tail.normed, 1)

            samples(v, front, body, lambda: end_norm(NB - 1, (NB - 1) % IN))

        @block.gpsimd
        def _(g):
            g.sem_inc(tail.out_free, IN)
            with g.Fori(0, NB // IN) as i:
                for b in range(IN):
                    tail.store(g, b, i * IN + b)
                    tail.free(g, b, i)


HEADS = 8
NK = 64
DK = 32
TOPK = 16
NT4 = NK * NK // 128
ROWS = [(i, TOPK // (i + 1)) for i in range(5)]
NCAND = sum(w for _, w in ROWS) + 3 * 2 + 8
FLOOR = 87.0
LIFT = 40.0
SLACK = 2.0 ** -21
HIDDEN = -1e30


PE_AT = {"a_scores": 0, "turn_kv": 2, "turn_k": 8, "c_scores": 12, "turn_p": 21, "attend": 26, "a_turn": 24}
ACT_AT = {"kvT": 1, "a_copy": 2, "kT": 11, "exp": (18, 19, 20), "PT": (24, 25), "terms": 23, "high": 26}
DVE_AT = {"lists": ((3, 7, 8), (9, 10, 11), (12, 13, 14)), "best": (17, 18, 19), "size": 15, "cut": 20,
          "lower": 21, "norm": (25, 26), "low": 27,
          "scale": (4, 5, 6), "max": (15, 16, 16), "max_done": 17, "c_norm": 22, "add": (28, 29, 30)}


def stage_keys(nc, d):
    with Mem(nc, "keys") as m:
        wq = m.sb("wq", [DK, 2, HEADS, C])
        keys = m.sb("keys", [DK, 2, HEADS, NK])
        both = m.sb("both", [C, HEADS, 2, NK])
        proj = m.sb("proj", [128, HEADS, 128])
        raw = m.sb("raw", [128, 2, NT4, 128])
        new = m.sb("new", [128, 2, NT4, 128])
        ps = [m.ps(f"ps{k}", [C, 4, 2, NK]) for k in range(2)]
        pst = [m.ps(f"pst{k}", [128, 4, 128]) for k in range(4)]
        loaded, done, copied, stored, scaled = (m.sem(n) for n in ("loaded", "done", "copied", "stored", "scaled"))
        raw_in = [m.sem(f"raw_in{j}") for j in range(2)]
        new_out = [m.sem(f"new_out{j}") for j in range(2)]
        projected = m.sem("projected")
        taken = [m.sem(f"taken{k}") for k in range(2)]
        stored_table = [m.pool_dma_sem(f"stored_table{j}") for j in range(2)]
        block = m.block()
        QUADS = NT4 // 4

        @block.sync
        def _(sp):
            sp.dma_start(wq[:], d["wq_pk"]).then_inc(loaded, 16)
            sp.dma_start(keys[:], d["pk_keys"]).then_inc(loaded, 16)
            sp.dma_start(proj[:], d["head_proj"]).then_inc(loaded, 16)
            for h in range(HEADS):
                if h >= 2:
                    sp.wait_ge(projected, (h - 1) * QUADS)
                sp.dma_start(raw[:, h % 2], d["tableT"][h]).then_inc(raw_in[h % 2], 16)
            sp.wait_ge(copied, 2)
            sp.dma_start(d["score_w"].rearrange("h c k -> c h k"),
                         both[:].rearrange("c h p k -> c h (p k)")).then_inc(stored, 16)
            sp.wait_ge(stored, 16)

        @block.tensor
        def _(pe):
            pe.wait_ge(loaded, 48)
            for h in range(HEADS):
                for p in range(2):
                    last = nc.tensor.matmul(ps[h // 4][:, h % 4, p, :], wq[:, p, h, :], keys[:, p, h, :],
                                            start=True, stop=True)
                if h % 4 == 3:
                    last.then_inc(done, 1)
            pe.wait_ge(scaled, 1)
            for h in range(HEADS):
                pe.wait_ge(raw_in[h % 2], h // 2 * 16 + 16)
                for g in range(QUADS):
                    at = h * QUADS + g
                    if at >= 4:
                        pe.wait_ge(taken[at % 2], at // 2 - 1)
                    for k in range(4):
                        last = nc.tensor.matmul(pst[at % 4][:, k], raw[:, h % 2, 4 * g + k], proj[:, h],
                                                start=True, stop=True)
                    last.then_inc(projected, 1)

        def take(eng, which, copy):
            for h in range(HEADS):
                if h >= 2:
                    eng.wait_ge(new_out[h % 2], h // 2 * 16)
                for g in range(which, QUADS, 2):
                    at = h * QUADS + g
                    eng.wait_ge(projected, at + 1)
                    copy(new[:, h % 2, 4 * g:4 * g + 4], pst[at % 4][:]).then_inc(taken[which], 1)

        @block.scalar
        def _(act):
            for k in range(2):
                act.wait_ge(done, k + 1)
                nc.scalar.activation(both[:, 4 * k:4 * k + 4], ps[k][:], ACT.Copy).then_inc(copied, 1)
            take(act, 0, lambda out, in_: nc.scalar.activation(out, in_, ACT.Copy))

        @block.vector
        def _(v):
            v.wait_ge(loaded, 48)
            nc.vector.tensor_scalar(proj[0:C], proj[0:C], C ** -0.5, None, ALU.mult).then_inc(scaled, 1)
            take(v, 1, nc.vector.tensor_copy)

        @block.gpsimd
        def _(g_):
            for h in range(HEADS):
                for k in range(2):
                    g_.wait_ge(taken[k], (h + 1) * QUADS // 2)
                g_.dma_start(d["table"][h], new[:, h % 2]).then_inc(stored_table[h % 2], 16)
                g_.wait_ge(stored_table[h % 2], h // 2 * 16 + 16)
                g_.sem_inc(new_out[h % 2], 16)


def stage_memory(nc, d):
    with Mem(nc, "mem") as m:
        ident = m.sb("ident", [128, 128])
        tri = m.sb("tri", [CP, CH, TOK])
        acc = m.sb("acc", [CP, NB, CH, C])
        pick_in = m.sb("pick_in", [128, NT4 // 4, 128])
        pick = m.sb("pick", [128, NT4, 128], F32R)
        table = m.sb("table", [128, NT4, 128])
        score_w = m.sb("score_w", [C, 2 * NK])
        lift = m.sb("lift", [128, 1])
        xa = m.sb("xa", [C, 2, TOK])
        xc = m.sb("xc", [C, 2, TOK])
        S = m.sb("S", [CP, CH, 2 * NK])
        rest = m.sb("rest", [CP, CH, 2, NK])
        lists = m.sb("lists", [CP, CH, 2, TOPK])
        cand = m.sb("cand", [CP, CH, NCAND])
        cand2 = m.sb("cand2", [CP, CH, NCAND])
        best = m.sb("best", [CP, CH, TOPK])
        size = m.sb("size", [CP, CH])
        cut = m.sb("cut", [CP, CH])
        terms = m.sb("terms", [CP, CH, TOPK])
        rZ = m.sb("rZ", [CP, 2, CH])
        Zh = m.sb("Zh", [128, 2, TOK + 1], F32R)
        Zl = m.sb("Zl", [128, 2, TOK + 1], F32R)
        RING = 4
        ex = m.sb("ex", [128, RING, TOK])
        wt = m.sb("wt", [128, RING, TOK])
        kvT = m.sb("kvT", [128, TOK])
        kv = m.sb("kv", [CP, CH, 128])
        kT = m.sb("kT", [C, TOK])
        mx = m.sb("mx", [CP, CH])
        sm = m.sb("sm", [CP, CH])
        pr = m.sb("pr", [CP, CH, TOK])
        PT = m.sb("PT", [CP, 2, TOK])
        ps_z = [m.ps(f"ps_z{k}", [128, 512]) for k in range(RING)]
        ps_kv = m.ps("ps_kv", [128, 512])
        ps_a = m.ps("ps_a", [128, 512])
        ps_c = m.ps("ps_c", [128, 512])
        ps_s = m.ps("ps_s", [CP, 512])
        held = m.sem("held")
        consts_in = m.sem("consts_in")
        pick_part = m.sem("pick_part")
        pick_ready = m.sem("pick_ready")
        head_in = m.sem("head_in")
        table_in = [m.sem(f"table_in{k}") for k in range(4)]
        xa_in = [m.sem(f"xa_in{j}") for j in range(2)]
        xc_in = [m.sem(f"xc_in{j}") for j in range(2)]
        (scored, S_ready, lists_ready, sums_ready, best_ready, terms_ready, cut_ready, cut_done, cut_turned,
         high_ready, Z_ready) = (m.sem(n) for n in (
             "scored", "S_ready", "lists_ready", "sums_ready", "best_ready", "terms_ready", "cut_ready",
             "cut_done", "cut_turned", "high_ready", "Z_ready"))
        z_done, ex_ready, wt_ready, kv_done = (m.sem(n) for n in ("z_done", "ex_ready", "wt_ready", "kv_done"))
        (kvT_ready, kv_turned, kv_ready, k_turned, kT_ready, s_done, max_ready, e_ready, p_turned, PT_ready,
         out_done, added) = (m.sem(n) for n in (
             "kvT_ready", "kv_turned", "kv_ready", "k_turned", "kT_ready", "s_done", "max_ready", "e_ready",
             "p_turned", "PT_ready", "out_done", "added"))
        stored = m.sem("stored")
        dve_a, dve_c = m.sem("dve_a"), m.sem("dve_c")
        block = m.block()
        chunk = lambda c: slice(c * CP, (c + 1) * CP)
        score_at = [ps_c[0:CP, 0:CP], ps_c[0:CP, CP:3 * CP], ps_s[:, 0:TOK]]
        turned_at = {(0, c): ps_c[0:CP, chunk(c)] for c in range(CH)}
        turned_at |= {(1, 1): ps_s[:, chunk(0)], (1, 2): ps_s[:, chunk(1)], (2, 2): ps_s[:, chunk(2)]}
        PT_at = {(0, c): PT[:, 0, chunk(c)] for c in range(CH)}
        PT_at |= {(1, 1): PT[:, 1, chunk(0)], (1, 2): PT[:, 1, chunk(1)], (2, 2): PT[:, 1, chunk(2)]}

        def units(eng, a, body, c):

            def inner(h, u0):
                with eng.Fori(0, NB // 2 - 1) as i:
                    for j in range(2):
                        s = i * 2 + (1 + j)
                        body(h, u0 + s, s, (1 + j) % 2, True, True)

            a(0, 0)
            body(0, 0, 0, 0, True, False)
            inner(0, 0)
            with eng.Fori(1, HEADS) as h:
                u0 = h * NB
                body(h - 1, u0 - 1, NB - 1, 1, True, True)
                body(h, u0, 0, 0, True, True)
                inner(h, u0)
            u = HEADS * NB - 1
            body(HEADS - 1, u, NB - 1, 1, False, True)
            c(u, NB - 1, 1)

        def before(s):
            return NB - 1 if type(s) is int and s == 0 else s - 1

        @block.sync
        def _(sp):
            for t, n in ((ident, "ident"), (tri, "tri")):
                sp.dma_start(t[:], d[n]).then_inc(consts_in, 16)
            sp.dma_start(acc[:], d["h3"].rearrange("b p c e -> p b c e")).then_inc(consts_in, 16)
            for k in range(4):
                if k:
                    sp.wait_ge(pick_ready, k)
                sp.dma_start(pick_in[:], d["key_pick"][:, k * 8:k * 8 + 8]).then_inc(pick_part, 16)
            sp.dma_start(score_w[:], d["score_w"][0]).then_inc(head_in, 16)
            for j in range(2):
                sp.dma_start(xa[:, j], d["x3T"][j]).then_inc(xa_in[j], 16)

            def load_table(h, k):
                sp.dma_start(table[:, k * 8:k * 8 + 8], d["table"][h][:, k * 8:k * 8 + 8]).then_inc(table_in[k], 16)

            for k in range(4):
                load_table(0, k)
            for j in range(2):
                sp.dma_start(xc[:, j], d["x3T"][j]).then_inc(xc_in[j], 16)

            def inner(u0):
                with sp.Fori(0, NB // 2 - 1) as i:
                    for j in range(2):
                        sp.wait_ge(scored, u0 + i * 2 + (j + 1))
                        sp.dma_start(xa[:, j], d["x3T"][i * 2 + (2 + j)]).then_inc(xa_in[j], 16)
                        sp.wait_ge(s_done, u0 + i * 2 + (j + 1))
                        sp.dma_start(xc[:, j], d["x3T"][i * 2 + (2 + j)]).then_inc(xc_in[j], 16)

            inner(0)
            with sp.Fori(1, HEADS) as h:
                u0 = h * NB
                sp.wait_ge(scored, u0 - 1)
                sp.dma_start(xa[:, 0], d["x3T"][0]).then_inc(xa_in[0], 16)
                sp.wait_ge(scored, u0)
                sp.dma_start(score_w[:], d["score_w"][h]).then_inc(head_in, 16)
                sp.dma_start(xa[:, 1], d["x3T"][1]).then_inc(xa_in[1], 16)
                for k in range(4):
                    sp.wait_ge(kv_done, u0 * NT4 + (8 * k + 8 - NT4 + RING))
                    load_table(h, k)
                    if k == 0:
                        sp.wait_ge(s_done, u0 - 1)
                        sp.dma_start(xc[:, 0], d["x3T"][0]).then_inc(xc_in[0], 16)
                sp.wait_ge(s_done, u0)
                sp.dma_start(xc[:, 1], d["x3T"][1]).then_inc(xc_in[1], 16)
                inner(u0)
            sp.wait_ge(added, HEADS * NB + 1)
            sp.dma_start(d["out"].rearrange("b (c p) e -> p b c e", p=CP), acc[:]).then_inc(stored, 16)
            sp.wait_ge(stored, 16)

        @block.tensor
        def _(pe):
            mm, tp = nc.tensor.matmul, nc.tensor.transpose
            for sem, n in ((cut_turned, 1), (kv_turned, 1), (kv_done, RING)):
                pe.sem_inc(sem, n)
            pe.wait_ge(consts_in, 48)
            pe.wait_ge(pick_ready, 5)

            def arrived(sems, u, par):
                pe.wait_ge(sems[par], u * 8 + (16 if par == 0 else 8))

            def a_scores(u, par):
                arrived(xa_in, u, par)
                pe.wait_ge(Z_ready, u + 1)
                pe.sem_inc(held, 1)
                for c in range(CH):
                    last = mm(ps_a[0:CP, c * 128:(c + 1) * 128], xa[:, par, chunk(c)], score_w[:],
                              start=True, stop=True)
                last.then_inc(scored, 1)

            def a_turn(u):
                pe.wait_ge(cut_done, u + 1)
                pe.sem_inc(held, 1)
                for c in range(CH):
                    last = tp(ps_a[:, chunk(c)], S[:, c, :], ident[0:CP, 0:CP])
                last.then_inc(cut_turned, 1)

            def b_sum(u, n, par):
                if n == 0:
                    pe.wait_ge(Z_ready, u + 2)
                    pe.sem_inc(held, 1)
                pe.wait_ge(wt_ready, u * NT4 + (n + 1))
                mm(ps_z[n % RING][:, 0:TOK + 1], pick[:, n, :], Zh[:, par], start=True, stop=False)
                mm(ps_z[n % RING][:, 0:TOK + 1], pick[:, n, :], Zl[:, par], start=False, stop=True)\
                    .then_inc(z_done, 1)

            def b_product(u, n):
                pe.wait_ge(wt_ready, u * NT4 + (n + 1 + RING))
                mm(ps_kv[:, 0:TOK], table[:, n, :], wt[:, n % RING], start=n == 0, stop=n == NT4 - 1)\
                    .then_inc(kv_done, 1)

            def c_turn_kv(u):
                pe.wait_ge(kvT_ready, u + 2)
                pe.wait_ge(added, u + 1)
                pe.sem_inc(held, 1)
                for c in range(CH):
                    last = tp(ps_c[0:CP, c * 128:(c + 1) * 128], kvT[:, chunk(c)], ident[:])
                last.then_inc(kv_turned, 1)

            def c_turn_k(u):
                pe.wait_ge(kv_ready, u + 1)
                pe.sem_inc(held, 1)
                for c in range(CH):
                    last = tp(ps_c[0:C, chunk(c)], kv[:, c, 0:C], ident[0:CP, 0:CP])
                last.then_inc(k_turned, 1)

            def c_scores(u, par):
                arrived(xc_in, u, par)
                pe.wait_ge(kT_ready, u + 1)
                pe.wait_ge(PT_ready, u * 2 + 2)
                pe.sem_inc(held, 1)
                for c in range(CH):
                    last = mm(score_at[c], xc[:, par, chunk(c)], kT[:, 0:(c + 1) * CP], start=True, stop=True)
                last.then_inc(s_done, 1)

            def c_turn_p(u):
                pe.wait_ge(e_ready, u * 3 + 3)
                pe.sem_inc(held, 1)
                for jc in range(CH):
                    for c in range(jc, CH):
                        last = tp(turned_at[jc, c], pr[:, c, chunk(jc)], ident[0:CP, 0:CP])
                    if jc != 1:
                        last.then_inc(p_turned, 1)

            def c_attend(u):
                pe.wait_ge(PT_ready, u * 2 + 4)
                pe.sem_inc(held, 1)
                for c in range(CH):
                    for jc in range(c + 1):
                        last = mm(ps_c[0:CP, c * C:(c + 1) * C], PT_at[jc, c], kv[:, jc, C:128],
                                  start=jc == 0, stop=jc == c)
                last.then_inc(out_done, 1)

            def a(u, par):
                a_scores(u, par)
                a_turn(u)
                for n in range(RING - 1):
                    b_sum(u, n, par)

            def body(h, u, s, par, with_a, with_c):
                for n in range(NT4):
                    ahead = n + RING - 1
                    if ahead < NT4:
                        b_sum(u, ahead, par)
                    elif with_a:
                        b_sum(u + 1, ahead - NT4, 1 - par)
                    if with_a and n == PE_AT["a_scores"]:
                        if type(s) is int and s == NB - 1:
                            pe.wait_ge(head_in, h * 16 + 32)
                        a_scores(u + 1, 1 - par)
                    if n == 0:
                        pe.wait_ge(kvT_ready, u + 1)
                    if type(s) is int and s == 0 and n % 8 == 0:
                        pe.wait_ge(table_in[n // 8], h * 16 + 16)
                    b_product(u, n)
                    if with_c and n == PE_AT["turn_kv"]:
                        c_turn_kv(u - 1)
                    if with_c and n == PE_AT["turn_k"]:
                        c_turn_k(u - 1)
                    if with_c and n == PE_AT["c_scores"]:
                        c_scores(u - 1, 1 - par)
                    if with_c and n == PE_AT["turn_p"]:
                        c_turn_p(u - 1)
                    if with_a and n == PE_AT["a_turn"]:
                        a_turn(u + 1)
                    if with_c and n == PE_AT["attend"]:
                        c_attend(u - 1)

            def c(u, s, par):
                c_turn_kv(u)
                c_turn_k(u)
                c_scores(u, par)
                c_turn_p(u)
                c_attend(u)

            pe.wait_ge(head_in, 16)
            units(pe, a, body, c)

        @block.scalar
        def _(act):
            run = nc.scalar.activation
            act.sem_inc(kvT_ready, 1)
            act.sem_inc(PT_ready, 2)
            act.wait_ge(pick_ready, 5)

            def a_copy(u):
                act.wait_ge(scored, u + 1)
                act.wait_ge(cut_turned, u + 1)
                run(S[:].rearrange("p c k -> p (c k)"), ps_a[0:CP, 0:CH * 128], ACT.Copy).then_inc(S_ready, 1)

            def a_terms(u):
                act.wait_ge(best_ready, u + 1)
                run(terms[:], terms[:], ACT.Exp, bias=lift[0:CP, 0:1]).then_inc(terms_ready, 1)

            def a_high(u, par):
                act.wait_ge(cut_turned, u + 2)
                run(Zh[:, par, 0:TOK], ps_a[:, 0:TOK], ACT.Copy).then_inc(high_ready, 1)

            def b_exp(u, n):
                act.wait_ge(z_done, u * NT4 + (n + 1))
                act.wait_ge(wt_ready, u * NT4 + (n + 1))
                run(ex[:, n % RING], ps_z[n % RING][:, 0:TOK], ACT.Exp, bias=lift[:, 0:1]).then_inc(ex_ready, 1)

            def c_copy_kvT(u):
                act.wait_ge(kv_done, u * NT4 + (NT4 + RING))
                act.wait_ge(kv_turned, u + 1)
                run(kvT[:], ps_kv[:, 0:TOK], ACT.Copy).then_inc(kvT_ready, 1)

            def c_copy_kT(u):
                act.wait_ge(k_turned, u + 1)
                run(kT[:], ps_c[0:C, 0:TOK], ACT.Copy).then_inc(kT_ready, 1)

            def c_exp(u, c):
                if c == 0:
                    act.wait_ge(max_ready, u + 1)
                run(pr[:, c, 0:(c + 1) * CP], score_at[c], ACT.Exp, bias=mx[:, c:c + 1],
                    accum_out=sm[:, c:c + 1]).then_inc(e_ready, 1)

            def c_copy_PT(u, k):
                act.wait_ge(p_turned, u * 2 + (k + 1))
                run(PT[:, k], (ps_c, ps_s)[k][0:CP, 0:TOK], ACT.Copy).then_inc(PT_ready, 1)

            def a(u, par):
                a_copy(u)
                a_terms(u)
                a_high(u, par)

            def body(h, u, s, par, with_a, with_c):
                for n in range(NT4):
                    b_exp(u, n)
                    if with_c and n == ACT_AT["kvT"]:
                        c_copy_kvT(u - 1)
                    if with_a and n == ACT_AT["a_copy"]:
                        a_copy(u + 1)
                    if with_c and n == ACT_AT["kT"]:
                        c_copy_kT(u - 1)
                    if with_c and n in ACT_AT["exp"]:
                        c_exp(u - 1, ACT_AT["exp"].index(n))
                    if with_a and n == ACT_AT["terms"]:
                        a_terms(u + 1)
                    if with_c and n in ACT_AT["PT"]:
                        c_copy_PT(u - 1, ACT_AT["PT"].index(n))
                    if with_a and n == ACT_AT["high"]:
                        a_high(u + 1, 1 - par)

            def c(u, s, par):
                c_copy_kvT(u)
                c_copy_kT(u)
                for c in range(CH):
                    c_exp(u, c)
                c_copy_PT(u, 0)
                c_copy_PT(u, 1)

            units(act, a, body, c)

        @block.vector
        def _(v):
            tt, ts, stt = nc.vector.tensor_tensor, nc.vector.tensor_scalar, nc.vector.scalar_tensor_tensor
            v.sem_inc(Z_ready, 1)
            v.sem_inc(wt_ready, RING)
            v.sem_inc(added, 1)
            for t in (Zh, Zl):
                last = nc.vector.memset(t[:].bitcast(F32), 0.0)
            last.then_inc(dve_a, 1)
            for k in range(4):
                v.wait_ge(pick_part, k * 16 + 16)
                nc.vector.tensor_copy(pick[:, k * 8:k * 8 + 8], pick_in[:]).then_inc(pick_ready, 1)
            nc.vector.memset(lift[:], -LIFT).then_inc(pick_ready, 1)
            v.wait_ge(consts_in, 48)
            v.wait_ge(dve_a, 1)
            NA, NC = 6 * 3 + 3 * 3 + 4 + 2 + 1, 3 + 3 + 1 + 1 + 3
            chains = {}
            wide = lambda a, n: a.unsqueeze(2).broadcast_to((CP, CH, n))

            def a_lists(u, part, c):
                if (part, c) == (0, 0):
                    v.wait_ge(S_ready, u + 1)
                    v.sem_inc(held, 1)
                    chains["a"] = Chain(v, dve_a, u, NA)
                    chains["a"].n = 1
                ch = chains["a"]
                if part and c == 0:
                    ch.sync()
                    v.sem_inc(held, 1)
                for p in range(2):
                    sc, li = S[:, c, p * NK:(p + 1) * NK], lists[:, c, p]
                    if part == 0:
                        ch.step(nc.vector.max(li[:, 0:8], sc))
                    elif part == 1:
                        ch.step(nc.vector.match_replace(rest[:, c, p], li[:, 0:8], sc, -3e38))
                    else:
                        ch.step(nc.vector.max(li[:, 8:16], rest[:, c, p]))
                if (part, c) == (2, CH - 1):
                    ch.sync()
                    v.sem_inc(lists_ready, 1)

            def a_best(u, part):
                ch = chains["a"]
                if part == 0:
                    v.wait_ge(sums_ready, u + 1)
                else:
                    ch.sync()
                v.sem_inc(held, 1)
                for c in range(CH):
                    if part == 0:
                        ch.step(nc.vector.max(best[:, c, 0:8], cand[:, c]))
                    elif part == 1:
                        ch.step(nc.vector.match_replace(cand2[:, c], best[:, c, 0:8], cand[:, c], -3e38))
                    else:
                        ch.step(nc.vector.max(best[:, c, 8:16], cand2[:, c]))

            def a_size(u):
                ends = lists[:, :, :, 0:TOPK:TOPK - 1]
                chains["a"].step(nc.vector.tensor_reduce(size[:], ends, AX.XY, ALU.add, apply_absolute_value=True))

            def a_cut(u):
                ch = chains["a"]
                ch.sync()
                ch.link(stt(cut[:], size[:], -SLACK, best[:, :, TOPK - 1], ALU.mult, ALU.add))
                ch.link(stt(cut[:], best[:, :, 0], -FLOOR, cut[:], ALU.add, ALU.max))
                v.sem_inc(cut_ready, 1)

            def a_lower(u):
                ch = chains["a"]
                ch.link(tt(terms[:], best[:], wide(cut[:], TOPK), ALU.subtract))
                v.sem_inc(best_ready, 1)

            def a_norm(u, par, part):
                ch = chains["a"]
                if part == 0:
                    v.wait_ge(terms_ready, u + 1)
                    ch.step(nc.vector.tensor_reduce(size[:], terms[:], AX.X, ALU.add))
                else:
                    ch.sync()
                    ch.step(nc.vector.reciprocal(rZ[:, par], size[:]))

            def a_low(u, par):
                ch = chains["a"]
                v.wait_ge(high_ready, u + 1)
                ch.link(tt(Zl[:, par, 0:TOK], ps_a[:, 0:TOK], Zh[:, par, 0:TOK].bitcast(F32), ALU.subtract))
                ch.n -= 1
                ch.close()
                v.sem_inc(Z_ready, 1)

            def b_weights(u, n):
                v.wait_ge(ex_ready, u * NT4 + (n + 1))
                v.wait_ge(kv_done, u * NT4 + (n + 1))
                stt(wt[:, n % RING], ps_z[n % RING][:, 0:TOK], 0.0, ex[:, n % RING], ALU.is_ge, ALU.mult)\
                    .then_inc(wt_ready, 1)

            def c_scale(u, par, c):
                if c == 0:
                    v.wait_ge(kv_turned, u + 2)
                    chains["c"] = Chain(v, dve_c, u, NC)
                ch = chains["c"]
                ch.step(ts(kv[:, c, :], ps_c[0:CP, c * 128:(c + 1) * 128], rZ[:, par, c:c + 1], None, ALU.mult))
                if c == CH - 1:
                    ch.sync()
                    v.sem_inc(kv_ready, 1)

            def c_max(u, c):
                if c == 0:
                    v.wait_ge(s_done, u + 1)
                    v.sem_inc(held, 1)
                chains["c"].step(nc.vector.tensor_tensor_reduce(
                    out=score_at[c], in0=score_at[c], in1=tri[:, c, 0:(c + 1) * CP], scale=1.0, scalar=-3e38,
                    op0=ALU.add, op1=ALU.max, accum_out=mx[:, c:c + 1]))

            def c_max_done(u):
                ch = chains["c"]
                ch.sync()
                ch.link(ts(mx[:], mx[:], -1.0, None, ALU.mult))
                v.sem_inc(max_ready, 1)

            def c_norm(u):
                v.wait_ge(e_ready, u * 3 + 3)
                chains["c"].link(nc.vector.reciprocal(sm[:], sm[:]))

            def c_add(u, s, c):
                ch = chains["c"]
                if c == 0:
                    v.wait_ge(out_done, u + 1)
                at = acc[:, s, c]
                ch.step(stt(at, ps_c[0:CP, c * C:(c + 1) * C], sm[:, c:c + 1], at, ALU.mult, ALU.add))
                if c == CH - 1:
                    ch.sync()
                    ch.close()
                    v.sem_inc(added, 1)

            def a(u, par):
                for part in range(3):
                    for c in range(CH):
                        a_lists(u, part, c)
                for part in range(3):
                    a_best(u, part)
                a_size(u)
                a_cut(u)
                a_lower(u)
                for part in range(2):
                    a_norm(u, par, part)
                a_low(u, par)

            def body(h, u, s, par, with_a, with_c):
                at = DVE_AT
                for n in range(NT4):
                    b_weights(u, n)
                    for part in range(3):
                        if with_a and n in at["lists"][part]:
                            a_lists(u + 1, part, at["lists"][part].index(n))
                    for c in range(CH):
                        if with_c and n == at["scale"][c]:
                            c_scale(u - 1, 1 - par, c)
                        if with_c and n == at["max"][c]:
                            c_max(u - 1, c)
                    if with_a and n == at["size"]:
                        a_size(u + 1)
                    if with_c and n == at["max_done"]:
                        c_max_done(u - 1)
                    if with_a and n in at["best"]:
                        a_best(u + 1, at["best"].index(n))
                    if with_a and n == at["cut"]:
                        a_cut(u + 1)
                    if with_a and n == at["lower"]:
                        a_lower(u + 1)
                    if with_c and n == at["c_norm"]:
                        c_norm(u - 1)
                    if with_a and n in at["norm"]:
                        a_norm(u + 1, 1 - par, at["norm"].index(n))
                    if with_a and n == at["low"]:
                        a_low(u + 1, 1 - par)
                    for c in range(CH):
                        if with_c and n == at["add"][c]:
                            c_add(u - 1, before(s), c)

            def c(u, s, par):
                for k in range(CH):
                    c_scale(u, par, k)
                for k in range(CH):
                    c_max(u, k)
                c_max_done(u)
                c_norm(u)
                for k in range(CH):
                    c_add(u, s, k)

            units(v, a, body, c)

        @block.gpsimd
        def _(g):
            tt = nc.gpsimd.tensor_tensor

            def a_sums(u):
                g.wait_ge(lists_ready, u + 1)
                at = 0
                for i, w in ROWS:
                    tt(cand[:, :, at:at + w], lists[:, :, 0, i:i + 1].broadcast_to((CP, CH, w)),
                       lists[:, :, 1, 0:w], ALU.add)
                    at += w
                tt(cand[:, :, at:at + 6].rearrange("p c (i w) -> p c i w", w=2),
                   lists[:, :, 0, 5:8].unsqueeze(3).broadcast_to((CP, CH, 3, 2)),
                   lists[:, :, 1, 0:2].unsqueeze(2).broadcast_to((CP, CH, 3, 2)), ALU.add)
                tt(cand[:, :, at + 6:at + 14], lists[:, :, 0, 8:16],
                   lists[:, :, 1, 0:1].broadcast_to((CP, CH, 8)), ALU.add).then_inc(sums_ready, 1)

            def a_shift(u):
                g.wait_ge(cut_ready, u + 1)
                tt(S[:, :, 0:NK], S[:, :, 0:NK], cut[:].unsqueeze(2).broadcast_to((CP, CH, NK)), ALU.subtract)\
                    .then_inc(cut_done, 1)

            with g.Fori(0, HEADS * NB) as u:
                a_sums(u)
                a_shift(u)


SCRATCH = {
    "h0": (NB, CP, CH, C), "xn": (NB, CP, CH, C), "xnT": (NB, C, TOK),
    "krev": (C, TOK + CP), "conv": (NB, C, TOK),
    "h1": (NB, CP, CH, C), "x1T": (NB, C, TOK), "gates": (NB, E // 2, 2, TOK),
    "h2": (NB, CP, CH, C), "x2": (NB, CP, CH, C), "x2T": (NB, C, TOK),
    "h3": (NB, CP, CH, C), "x3T": (NB, C, TOK), "score_w": (HEADS, C, 2 * NK),
    "table": (HEADS, 128, NT4, 128),
}


def program(nc, d):
    for name, shape in SCRATCH.items():
        d[name] = nc.dram_tensor(name, shape, F32, kind="Internal").ap()
    with ExitStack() as Mem.program:
        for stage in (stage_tokens, stage_ssm_kernel, stage_conv, stage_mix, stage_gates, stage_experts,
                      stage_pairs, stage_keys, stage_memory):
            stage(nc, d)


def lay_out(np, a):
    con = np.concatenate
    n = {k: np.asarray(v) for k, v in a.items()}
    p = n["x"].reshape(NB, 3, 14, 16, 14, 16).transpose(0, 1, 3, 5, 2, 4).reshape(NB, KT, 128, NIMG)
    two = lambda v: con([v, v])
    re_im = lambda k: con([n[k + "_re"], n[k + "_im"]])
    im_re = lambda k: con([n[k + "_im"], n[k + "_re"]])
    sign = con([np.ones(C), -np.ones(C)]).astype(np.float32)
    A = "L0_attn_"
    par = np.stack([two(n[A + "Lambda_re"]), two(n[A + "Lambda_im"]), re_im(A + "B"), im_re(A + "B"),
                    re_im(A + "P"), im_re(A + "P"), np.broadcast_to(n[A + "step"], (128,)), sign], 1)
    cq = np.stack([con([n[A + "C_" + z].T, n[A + "Q_" + z][:, None]], 1) for z in ("re", "im")], 1)
    l = np.arange(TOK)
    tan = np.tan(np.pi * l / TOK)
    lag = TOK - 1 - l
    ang = 2 * np.pi * ((l[:, None] * lag[None, :]) % TOK) / TOK
    dft = np.stack([np.cos(ang) / TOK, -np.sin(ang) / TOK], 1).reshape(CH, CP, 2, TOK).transpose(1, 0, 2, 3)
    out = {
        "patches": p.transpose(0, 2, 1, 3),
        "txtT": n["txt"].transpose(0, 2, 1),
        "tokW": n["L0_tok_W"].T.reshape(KT, 128, C).transpose(1, 0, 2),
        "tokb": n["L0_tok_b"][:, None],
        "ident": np.eye(128, dtype=np.float32),
        "par": par,
        "cq": con([cq, cq]),
        "tanr": np.broadcast_to(tan.astype(np.float32), (128, TOK)),
        "tanc": tan.astype(np.float32).reshape(CH, CP).T,
        "dft": dft.astype(np.float32),
    }
    row = lambda v: np.broadcast_to(v, (CP, CH, C))
    out["fcT"] = n[A + "W_fc"].T
    out["skipD"] = np.broadcast_to(n[A + "D"], (C, 1))
    out["mix_rows"] = np.stack([row(n[A + k]) for k in ("b_fc", "ln_g", "ln_b")], 1)
    F = "L0_ffn_"
    pad = ((0, 0), (0, NT * HT - HID), (0, 0))
    w1, w3 = (np.pad(n[F + k], pad).transpose(2, 0, 1) for k in ("w1", "w3"))
    out["routerT"] = n[F + "router_w"].T
    out["w1T"], out["w3T"] = w1, w3
    out["w2"] = np.pad(n[F + "w2"].transpose(0, 2, 1), pad).reshape(E, NT, HT, C).transpose(2, 0, 1, 3)
    P = "L1_attn_"
    wi = n[P + "w_itr_att"]
    mix = np.zeros((C + 1, C + 1), np.float32)
    mix[:C, C] = wi[:C]
    mix[C, :C] = wi[C:2 * C]
    mix[np.arange(C), np.arange(C)] = wi[2 * C:]
    out["pair_mix"] = mix
    w = con([n[P + k] for k in ("w1", "w2", "w3")], 1)
    bias = con([n[P + k] for k in ("b1", "b2", "b3")])
    out["pair_top"] = con([w[:C], bias[None]])
    out["pair_bot"] = w[C:]
    M = "L1_ffn_"
    out["wq_pk"] = n[M + "Wq_pk"].reshape(C, 2, HEADS, DK).transpose(3, 1, 2, 0)
    out["pk_keys"] = n[M + "pk_keys"].transpose(3, 0, 2, 1)
    proj = np.zeros((128, HEADS, 128), np.float32)
    proj[:C, :, :C] = n[M + "Wq"].reshape(C, HEADS, C).transpose(2, 1, 0)
    proj[C:, :, C:] = n[M + "Wo"].reshape(HEADS, C, C).transpose(1, 0, 2)
    out["head_proj"] = proj
    tables = con([n[M + "keys_table"], n[M + "values_table"]], 1)
    out["tableT"] = tables.reshape(HEADS, NT4, 128, 2 * C).transpose(0, 3, 1, 2)
    row, sl, col = np.ogrid[0:128, 0:NT4, 0:128]
    out["key_pick"] = np.where(row < NK, row == col % NK, row - NK == 2 * sl + col // NK).astype(np.float32)
    t = np.arange(TOK)
    out["tri"] = np.where(t[None, None, :] > t.reshape(CH, CP).T[:, :, None], np.float32(HIDDEN), np.float32(0))
    return {k: np.ascontiguousarray(v) for k, v in out.items()}


def kernel(**inputs):
    import numpy as np
    import concourse.bacc as bacc
    from concourse import mybir as mb
    from concourse.bass_utils import run_bass_kernel_spmd as run

    nc = bacc.Bacc("TRN2", target_bir_lowering=False, num_devices=1)
    arrays = {"in_" + k: v for k, v in lay_out(np, inputs).items()}
    d = {k[3:]: nc.dram_tensor(k, v.shape, mb.dt.from_np(v.dtype), kind="ExternalInput").ap()
         for k, v in arrays.items()}
    d["out"] = nc.dram_tensor("out", (NB, TOK, C), mb.dt.float32, kind="ExternalOutput").ap()
    program(nc, d)
    r = run(nc, [arrays], core_ids=[0])
    return r.results[0]["out"]
```
